# Optimizing a Trainium2 kernel written in Bass

```python
import numpy as np
import jax
import jax.numpy as jnp

def _softmax(x, axis=-1):
    return jax.nn.softmax(x, axis=axis)

def _gelu(x):
    return jax.nn.gelu(x, approximate=True)

def _silu(x):
    return jax.nn.silu(x)

def _sigmoid(x):
    return jax.nn.sigmoid(x)

def _layernorm(x, axis=-1, eps=1e-05):
    m = jnp.mean(x, axis=axis, keepdims=True)
    v = jnp.var(x, axis=axis, keepdims=True)
    return (x - m) / jnp.sqrt(v + eps)

def _scatter_add(tgt, idx, src, axis=0):
    return tgt.at[idx].add(src)

def _segment_sum(src, seg, n):
    return jax.ops.segment_sum(src, seg, n)
kernel_name = 'mk_adaln_ffn_d2_seqx_r4_0a4ad8'

def setup_inputs(seed: int=0):
    np.random.seed(seed)
    _w = jnp.asarray

    def _rec_inputs():
        import jax
        import jax.numpy as jnp
        _rk = jax.random.key(seed)
        x = -7.109e-05 + 0.9999 * jax.random.normal(jax.random.fold_in(_rk, 1), (32, 64, 1024), jnp.float32)
        _lenS = 64 - jax.random.randint(jax.random.fold_in(_rk, 7), (32,), 0, max(1, 64 // 4) + 1, jnp.int32)
        _lenS2 = 64 - jax.random.randint(jax.random.fold_in(_rk, 8), (32,), 0, max(1, 64 // 4) + 1, jnp.int32)
        itok_B_0_15 = jax.random.randint(jax.random.fold_in(_rk, 11), (32,), 0, 16, jnp.int32)
        itok_B_2_6 = jax.random.randint(jax.random.fold_in(_rk, 12), (32,), 2, 7, jnp.int32)
        return (x, itok_B_0_15, itok_B_2_6)
    x, itok_B_0_15, itok_B_2_6 = _rec_inputs()

    def _L0_cond_setup():
        import jax, jax.numpy as jnp
        import numpy as np
        NUM_CONDITIONS = 16
        IN_CH = 64
        OUT_CH = 64
        B = 64
        T = 1024
        key = jax.random.key(seed)
        k_x, k_w, k_c = jax.random.split(key, 3)
        x = jax.random.normal(k_x, (B, IN_CH, T), dtype=jnp.float32)
        bound = float(np.sqrt(6.0 / IN_CH))
        weights = jax.random.uniform(k_w, (NUM_CONDITIONS, IN_CH, OUT_CH), dtype=jnp.float32, minval=-bound, maxval=bound)
        condition = jax.random.randint(k_c, (B,), 0, NUM_CONDITIONS, dtype=jnp.int64)
        return {'x': x, 'weights': weights, 'condition': condition}
    _L0_cond_all = _L0_cond_setup()
    _L0_cond_in = {k: v for k, v in _L0_cond_all.items() if k in ('weights',)}
    del _L0_cond_all

    def _L0_ffn_setup():
        import math
        import jax, jax.numpy as jnp
        import numpy as np
        SCALING = 16.0 / 32.0

        def real_fourier_orthogonal_multiply(c):
            n = c.shape[-1]
            sqrt_n = math.sqrt(n)
            pair_scale = math.sqrt(n / 2.0)
            max_f = (n - 1) // 2
            work = c.astype(jnp.float32)
            dc = (work[..., 0] * sqrt_n)[..., None].astype(jnp.complex64)
            cos = work[..., 1:1 + 2 * max_f:2] * pair_scale
            sin = work[..., 2:2 + 2 * max_f:2] * pair_scale
            mid = (cos - 1j * sin).astype(jnp.complex64)
            parts = [dc, mid]
            if n % 2 == 0:
                parts.append((work[..., -1] * sqrt_n)[..., None].astype(jnp.complex64))
            spectrum = jnp.concatenate(parts, axis=-1)
            return jnp.fft.irfft(spectrum, n=n, axis=-1).astype(c.dtype)
        key = jax.random.key(seed)
        ks = jax.random.split(key, 9)
        B, S, D_in, D_out, R0, R1, E = (4, 512, 1024, 1024, 32, 8, 3)
        x = jax.random.normal(ks[0], (B, S, D_in), dtype=jnp.float32)
        W_base = jax.random.normal(ks[1], (D_out, D_in), dtype=jnp.float32) * 0.02
        b_base = jax.random.normal(ks[2], (D_out,), dtype=jnp.float32) * 0.02
        enc0 = jax.random.normal(ks[3], (R0, D_in), dtype=jnp.float32) * 0.02
        enc1 = jax.random.normal(ks[4], (R1, D_in), dtype=jnp.float32) * 0.02
        coefs0 = jax.random.normal(ks[5], (E, D_out, R0), dtype=jnp.float32) * 0.02
        coefs1 = jax.random.normal(ks[6], (E, D_out, R1), dtype=jnp.float32) * 0.02
        mask0 = jax.random.randint(ks[7], (E, D_out, R0), 0, 2).astype(bool)
        mask1 = jax.random.randint(ks[8], (E, D_out, R1), 0, 2).astype(bool)
        return dict(x=x, W_base=W_base, b_base=b_base, enc0=enc0, enc1=enc1, coefs0=coefs0, coefs1=coefs1, mask0=mask0, mask1=mask1)
    _L0_ffn_all = _L0_ffn_setup()
    _L0_ffn_in = {k: v for k, v in _L0_ffn_all.items() if k in ('W_base', 'b_base', 'enc0', 'enc1', 'coefs0', 'coefs1', 'mask0', 'mask1')}
    del _L0_ffn_all

    def _L1_cond_setup():
        import jax, jax.numpy as jnp
        import numpy as np
        B, N, H, F = (4, 128, 1024, 2752)
        L, R, RANK = (1, 16, 16)
        SCALE = 0.5
        key = jax.random.key(seed)
        ks = jax.random.split(key, 12)
        nrm = lambda k, shape, fan: jax.random.normal(k, shape, jnp.float32) * fan ** (-0.5)
        inp = {'x': jax.random.normal(ks[0], (B, N, H), jnp.float32), 'W_gate': nrm(ks[1], (F, H), H), 'W_up': nrm(ks[2], (F, H), H), 'W_down': nrm(ks[3], (H, F), F), 'A_gate': nrm(ks[4], (L, R, RANK, H), H), 'B_gate': nrm(ks[5], (L, R, F, RANK), RANK), 'A_up': nrm(ks[6], (L, R, RANK, H), H), 'B_up': nrm(ks[7], (L, R, F, RANK), RANK), 'A_down': nrm(ks[8], (L, R, RANK, F), F), 'B_down': nrm(ks[9], (L, R, H, RANK), RANK), 'lora_indices': jax.random.randint(ks[10], (B,), 0, R), 'layer_idx': 0}
        return inp
    _L1_cond_all = _L1_cond_setup()
    _L1_cond_in = {k: v for k, v in _L1_cond_all.items() if k in ('W_gate', 'W_up', 'W_down', 'A_gate', 'B_gate', 'A_up', 'B_up', 'A_down', 'B_down')}
    del _L1_cond_all

    def _L1_ffn_setup():
        import jax, jax.numpy as jnp
        import numpy as np
        key = jax.random.key(seed)
        k1, k2, k3 = jax.random.split(key, 3)
        d_in, d_out = (1024, 1024)
        x = jax.random.normal(k1, (8, 256, d_in), dtype=jnp.float32)
        weight = jax.random.normal(k2, (d_out, d_in), dtype=jnp.float32) * (1.0 / np.sqrt(d_in))
        bias = jax.random.uniform(k3, (d_out,), dtype=jnp.float32, minval=-1.0 / np.sqrt(d_in), maxval=1.0 / np.sqrt(d_in))
        return {'x': x, 'weight': weight, 'bias': bias}
    _L1_ffn_all = _L1_ffn_setup()
    _L1_ffn_in = {k: v for k, v in _L1_ffn_all.items() if k in ('weight', 'bias')}
    del _L1_ffn_all
    return {'x': x, 'itok_B_0_15': itok_B_0_15, 'itok_B_2_6': itok_B_2_6, 'L0_cond_weights': _L0_cond_in['weights'], 'L0_ffn_W_base': _L0_ffn_in['W_base'], 'L0_ffn_b_base': _L0_ffn_in['b_base'], 'L0_ffn_enc0': _L0_ffn_in['enc0'], 'L0_ffn_enc1': _L0_ffn_in['enc1'], 'L0_ffn_coefs0': _L0_ffn_in['coefs0'], 'L0_ffn_coefs1': _L0_ffn_in['coefs1'], 'L0_ffn_mask0': _L0_ffn_in['mask0'], 'L0_ffn_mask1': _L0_ffn_in['mask1'], 'L1_cond_W_gate': _L1_cond_in['W_gate'], 'L1_cond_W_up': _L1_cond_in['W_up'], 'L1_cond_W_down': _L1_cond_in['W_down'], 'L1_cond_A_gate': _L1_cond_in['A_gate'], 'L1_cond_B_gate': _L1_cond_in['B_gate'], 'L1_cond_A_up': _L1_cond_in['A_up'], 'L1_cond_B_up': _L1_cond_in['B_up'], 'L1_cond_A_down': _L1_cond_in['A_down'], 'L1_cond_B_down': _L1_cond_in['B_down'], 'L1_ffn_weight': _L1_ffn_in['weight'], 'L1_ffn_bias': _L1_ffn_in['bias']}

def reference(x, itok_B_0_15, itok_B_2_6, L0_cond_weights, L0_ffn_W_base, L0_ffn_b_base, L0_ffn_enc0, L0_ffn_enc1, L0_ffn_coefs0, L0_ffn_coefs1, L0_ffn_mask0, L0_ffn_mask1, L1_cond_W_gate, L1_cond_W_up, L1_cond_W_down, L1_cond_A_gate, L1_cond_B_gate, L1_cond_A_up, L1_cond_B_up, L1_cond_A_down, L1_cond_B_down, L1_ffn_weight, L1_ffn_bias):
    import jax
    import jax.numpy as jnp

    def _L0_cond_ref(x, weights, condition):
        import jax, jax.numpy as jnp
        import numpy as np
        NUM_CONDITIONS = 16
        IN_CH = 64
        OUT_CH = 64
        B = 64
        T = 1024
        W = weights[condition]
        return jnp.einsum('bct,bcd->bdt', x, W)

    def _L0_ffn_ref(x, W_base, b_base, enc0, enc1, coefs0, coefs1, mask0, mask1):
        import math
        import jax, jax.numpy as jnp
        import numpy as np
        SCALING = 16.0 / 32.0

        def real_fourier_orthogonal_multiply(c):
            n = c.shape[-1]
            sqrt_n = math.sqrt(n)
            pair_scale = math.sqrt(n / 2.0)
            max_f = (n - 1) // 2
            work = c.astype(jnp.float32)
            dc = (work[..., 0] * sqrt_n)[..., None].astype(jnp.complex64)
            cos = work[..., 1:1 + 2 * max_f:2] * pair_scale
            sin = work[..., 2:2 + 2 * max_f:2] * pair_scale
            mid = (cos - 1j * sin).astype(jnp.complex64)
            parts = [dc, mid]
            if n % 2 == 0:
                parts.append((work[..., -1] * sqrt_n)[..., None].astype(jnp.complex64))
            spectrum = jnp.concatenate(parts, axis=-1)
            return jnp.fft.irfft(spectrum, n=n, axis=-1).astype(c.dtype)
        base = jnp.einsum('bsd,od->bso', x, W_base) + b_base
        e0 = jnp.einsum('bsd,rd->bsr', x, enc0)
        e1 = jnp.einsum('bsd,rd->bsr', x, enc1)
        w0 = coefs0 * mask0.astype(coefs0.dtype)
        w1 = coefs1 * mask1.astype(coefs1.dtype)
        decoded = jnp.einsum('bsr,eor->ebso', e0, w0) + jnp.einsum('bsr,eor->ebso', e1, w1)
        transformed = real_fourier_orthogonal_multiply(decoded)
        update = transformed.sum(axis=0)
        return base + update * SCALING

    def _L1_cond_ref(x, W_gate, W_up, W_down, A_gate, B_gate, A_up, B_up, A_down, B_down, lora_indices, layer_idx):
        import jax, jax.numpy as jnp
        import numpy as np
        B, N, H, F = (4, 128, 1024, 2752)
        L, R, RANK = (1, 16, 16)
        SCALE = 0.5

        def lora_add(base, inp, A, B):
            Ab = A[layer_idx][lora_indices]
            Bb = B[layer_idx][lora_indices]
            t = jnp.einsum('bri,bni->bnr', Ab, inp)
            return base + jnp.einsum('bor,bnr->bno', Bb, t) * SCALE
        gate = lora_add(jnp.einsum('bnh,fh->bnf', x, W_gate), x, A_gate, B_gate)
        up = lora_add(jnp.einsum('bnh,fh->bnf', x, W_up), x, A_up, B_up)
        act = jax.nn.silu(gate) * up
        down = lora_add(jnp.einsum('bnf,hf->bnh', act, W_down), act, A_down, B_down)
        return down

    def _L1_ffn_ref(x, weight, bias):
        import jax, jax.numpy as jnp
        import numpy as np
        w_bin = jnp.sign(weight)
        return jnp.einsum('bsi,oi->bso', x, w_bin) + bias
    x = x + _L0_ffn_ref(_L0_cond_ref(x, L0_cond_weights, itok_B_0_15), L0_ffn_W_base, L0_ffn_b_base, L0_ffn_enc0, L0_ffn_enc1, L0_ffn_coefs0, L0_ffn_coefs1, L0_ffn_mask0, L0_ffn_mask1)
    x = x + _L1_ffn_ref(_L1_cond_ref(x, L1_cond_W_gate, L1_cond_W_up, L1_cond_W_down, L1_cond_A_gate, L1_cond_B_gate, L1_cond_A_up, L1_cond_B_up, L1_cond_A_down, L1_cond_B_down, itok_B_2_6, 0), L1_ffn_weight, L1_ffn_bias)
    return x

_drawn_inputs = setup_inputs


def setup_inputs(seed=0):
    import zlib

    import numpy as np

    out = dict(_drawn_inputs(seed))
    spreads = {}
    factors = {'L0_ffn_b_base': 3.029, 'L1_ffn_bias': 200.0}
    for name, (base, spread) in spreads.items():
        noise = np.random.default_rng([zlib.crc32(name.encode()), seed]).standard_normal(out[name].shape)
        drawn = base * np.exp(spread * noise) if base else spread * noise
        out[name] = jnp.asarray(drawn.astype(out[name].dtype))
    for name, factor in factors.items():
        out[name] = (out[name] * factor).astype(out[name].dtype)
    return out
```

```python
from contextlib import ExitStack

import concourse.bass as bass
from concourse import mybir

F32 = mybir.dt.float32
F32R = mybir.dt.float32r
U8 = mybir.dt.uint8
ALU = mybir.AluOpType
ACT = mybir.ActivationFunctionType

P = 128
H = 1024
KC = H // P
F = 2752
PT = 3
NQ = F // (P * PT)
TILES = NQ * PT
FB = NQ * P * PT
FR = F - FB
G = 512
S = 64
NB = 32
NG = NB * S // G
GB = G // S
RANK = 16
NE, R0, R1 = 3, 32, 8
RL = R0 + R1
NAD = 16

NAT_SLOTS = 3
NAT_X, NAT_W, NAT_REM, NAT_SIGN, NAT_FIRST, NAT_GU = 0, 4, 12, (13, 14, 15, 16, 19, 20, 21, 22), (17, 18, 23), 21
NAT_UNITS = 63
SPLIT_SLOTS = 3
SPLIT_X, SPLIT_W, SPLIT_AG, SPLIT_AU, SPLIT_REM, SPLIT_GU, SPLIT_BD = 0, 4, 12, 13, 14, 15, 57
SPLIT_UNITS = 60
PART_UNITS = 6
assert NAT_UNITS % NAT_SLOTS == SPLIT_UNITS % SPLIT_SLOTS == PART_UNITS % NAT_SLOTS == 0

HEAD = (["AG"] * 2 + ["AU"] * 2 + ["REM"] * 2 + ["BREM"] + ["S0"] * 2 + ["S1"] * 2 + ["S2"] * 2 + ["S3"] * 2
        + ["DREM"] * 2 + ["ADREM"] + ["G0"] * 2 + ["U0"] * 2 + ["B"] * 3
        + ["S4"] * 2 + ["S5"] * 2 + ["S6"] * 2 + ["S7"] * 2 + ["G1"] * 2)
PART = (["D0"] * 2 + ["U1"] * 2 + ["G2"] * 2 + ["D1"] * 2 + ["U2"] * 2 + ["D2"] * 2 + ["AD"]
        + ["nextG0"] * 2 + ["nextB"] * 3 + ["nextU0"] * 2 + ["nextG1"] * 2)
LAST = PART[:13] + ["BD"] * 2
PART_PIECES = len(PART)
PIECES = len(HEAD) + (NQ - 1) * PART_PIECES + len(LAST)
SIGN_PIECES = 16
LOW_PIECES = PIECES - SIGN_PIECES
assert PIECES % 2 == 0 and PART_PIECES % 2 == 0


def first_of(name):
    return HEAD.index(name) if name in HEAD else len(HEAD) + (PART if name in PART else LAST).index(name)


def lows_before(c):
    return c if c <= 0 else sum(not x.startswith("S") for x in HEAD[:c]) + max(0, c - len(HEAD))


ACTS = TILES + 1
START = 1
CONSTS = 5
S1_BANKS = ((0, 2), (2, 4), (4, 6))
OUT_BANKS = (0, 1, 2, 6, 7, 3, 4, 5)
DOWNS = 9 * (1 + NQ) + 8
T_BANK = 6
D_BANK = 3


def build_effective_weight(nc, scratch, W_base, enc0, enc1, coefs, masks, fourier):
    with ExitStack() as ctx:
        def sb(name, shape, dtype):
            return ctx.enter_context(nc.sbuf_tensor(name, shape, dtype))

        def sem(name):
            return ctx.enter_context(nc.semaphore(name))

        coef = sb("coef", [P, NE, KC, RL], F32)
        mask = sb("coef_mask", [P, NE, KC, RL], U8)
        kept = sb("kept", [P, NE, KC, RL], F32)
        wsum = sb("wsum", [P, KC, RL], F32)
        table = sb("fourier_table", [P, KC, H], F32)
        enc = sb("enc", [RL, H], F32)
        enc_tiles = sb("enc_tiles", [RL, KC, P], F32)
        low_rank = sb("low_rank", [RL, H], F32)
        base = sb("base", [P, 2, 4, 256], F32)
        base_t = sb("base_t", [P, 2, H], F32)
        weight = sb("weight", [P, 2, H], F32)
        ps_g = ctx.enter_context(nc.psum_tensor("ps_g", [P, 2, 512], F32))
        ps_w = ctx.enter_context(nc.psum_tensor("ps_w", [P, 2, 2, 512], F32))
        coef_in, table_in, enc_in = sem("coef_in"), sem("table_in"), sem("enc_in")
        base_in = [sem("base_in0"), sem("base_in1")]
        step, wsum_done, g_psum, g_done = sem("step"), sem("wsum_done"), sem("g_psum"), sem("g_done")
        base_turned, w_psum, w_done = sem("base_turned"), sem("w_psum"), sem("w_done")
        stored = [sem("w_stored0"), sem("w_stored1")]

        block = ctx.enter_context(nc.Block())

        @block.sync
        def _(sp):
            c0, c1 = coefs
            m0, m1 = masks
            for e in range(NE):
                for dst, a, b in ((coef, c0, c1), (mask, m0, m1)):
                    sp.dma_start(dst[:, e, :, 0:R0], a[e].rearrange("(c p) r -> p c r", p=P)).then_inc(coef_in, 16)
                    sp.dma_start(dst[:, e, :, R0:RL], b[e].rearrange("(c p) r -> p c r", p=P)).then_inc(coef_in, 16)
            sp.dma_start(table[:], fourier.rearrange("(c p) n -> p c n", p=P)).then_inc(table_in, 16)
            sp.dma_start(enc[0:R0, :], enc0).then_inc(enc_in, 16)
            sp.dma_start(enc[R0:RL, :], enc1).then_inc(enc_in, 16)
            rows = W_base.rearrange("(oq u oo) (hq c) -> u hq oo oq c", oq=4, u=KC, hq=4)
            for u in range(KC):
                if u >= 2:
                    sp.wait_ge(base_turned, u - 1)
                for hq in range(4):
                    sp.dma_start(base[32 * hq:32 * hq + 32, u % 2], rows[u, hq]).then_inc(base_in[u % 2], 16)

        @block.vector
        def _(dve):
            dve.wait_ge(coef_in, 16 * 4 * NE)
            for e in range(NE):
                dve.tensor_tensor(kept[:, e], coef[:, e], mask[:, e], ALU.mult).then_inc(step, 1)
            dve.wait_ge(step, NE)
            dve.tensor_tensor(wsum[:], kept[:, 0], kept[:, 1], ALU.add).then_inc(step, 1)
            dve.wait_ge(step, NE + 1)
            dve.tensor_tensor(kept[:, 0], wsum[:], kept[:, 2], ALU.add).then_inc(step, 1)
            dve.wait_ge(step, NE + 2)
            dve.tensor_scalar(wsum[:], kept[:, 0], 0.5, None, ALU.mult).then_inc(wsum_done, 1)
            for u in range(KC):
                dve.wait_ge(base_in[u % 2], 64 * (u // 2 + 1))
                if u >= 2:
                    dve.wait_ge(w_done, u - 1)
                dve.transpose(base_t[:, u % 2].rearrange("p (k b h) -> p k b h", k=KC, b=4),
                              base[:, u % 2].rearrange("p b (k h) -> p k b h", k=KC)).then_inc(base_turned, 1)
                if u == 0:
                    dve.wait_ge(g_psum, 1)
                    dve.tensor_copy(low_rank[:], ps_g[0:RL].rearrange("p a n -> p (a n)")).then_inc(g_done, 1)
                    dve.wait_ge(enc_in, 32)
                    dve.tensor_copy(enc_tiles[:].rearrange("r k (q d) -> r k q d", q=4),
                                    enc[:].rearrange("r (q k d) -> r k q d", q=4, k=KC)).then_inc(g_done, 1)
                dve.wait_ge(base_turned, u + 1)
                dve.wait_ge(w_psum, u + 1)
                if u >= 2:
                    dve.wait_ge(stored[u % 2], 16 * (u // 2))
                dve.tensor_tensor(weight[:, u % 2], ps_w[:, u % 2].rearrange("p a n -> p (a n)"),
                                  base_t[:, u % 2], ALU.add).then_inc(w_done, 1)

        @block.tensor
        def _(pe):
            pe.wait_ge(table_in, 16)
            pe.wait_ge(wsum_done, 1)
            for half in range(2):
                for c in range(KC):
                    mm = pe.matmul(ps_g[0:RL, half], wsum[:, c], table[:, c, 512 * half:512 * half + 512],
                                   start=(c == 0), stop=(c == KC - 1))
            mm.then_inc(g_psum, 1)
            pe.wait_ge(g_done, 2)
            low_v = low_rank[:].rearrange("r (q u o) -> r u q o", q=4, u=KC)
            for u in range(KC):
                if u >= 2:
                    pe.wait_ge(w_done, u - 1)
                for k in range(KC):
                    mm = pe.matmul(ps_w[:, u % 2, k // 4, 128 * (k % 4):128 * (k % 4) + 128], enc_tiles[:, k],
                                   low_v[:, u], start=True, stop=True)
                mm.then_inc(w_psum, 1)

        @block.scalar
        def _(act):
            for u in range(KC):
                act.wait_ge(w_done, u + 1)
                act.dma_start(scratch[u], weight[:, u % 2]).then_inc(stored[u % 2], 16)
            for s in range(2):
                act.wait_ge(stored[s], 16 * KC // 2)


def build_layers(nc, x, cond_index, lora_index, cond_w, scratch, b_base, W_gate, W_up, W_down,
                 A_gate, B_gate, A_up, B_up, A_down, B_down, sign_w, bias, identity, own_batch, out):
    with ExitStack() as ctx:
        def sb(name, shape, dtype):
            return ctx.enter_context(nc.sbuf_tensor(name, shape, dtype))

        def sem(name):
            return ctx.enter_context(nc.semaphore(name))

        x1 = sb("x1", [P, 2, KC, G], F32R)
        turned = sb("turned", [P, 2 * KC * G], F32R)
        hidden = sb("hidden", [P, 9216], F32R)
        split = sb("split", [P, SPLIT_SLOTS, 2, H], F32R)
        lora_b = sb("lora_b", [P, 2, PT, 2, P], F32R)
        lora_b_rem = sb("lora_b_rem", [P, 2, 2, P], F32R)
        lora_ad = sb("lora_ad", [P, 2, PT, P], F32R)
        lora_t = sb("lora_t", [P, 2, 2, G], F32R)
        mix = sb("mix", [P, 2, 3, P], F32R)
        ident = sb("ident", [P, P], F32R)
        mixed = turned[:].rearrange("p (s k t) -> p s k t", s=2, k=KC)
        signs = turned[:].rearrange("p (m o) -> p m o", m=KC)
        down_w = hidden[:, 0:6144].rearrange("p (s j m h) -> p s j m h", s=2, j=PT, m=KC)
        acts = hidden[:, 6144:9216].rearrange("p (s j t) -> p s j t", s=2, j=PT)
        down = hidden[:, 0:8192].rearrange("p (s m t) -> p s m t", s=2, m=KC)

        nat = sb("nat", [P, NAT_SLOTS, H], F32)
        nat_down = sb("nat_down", [P, 32, 96], F32)
        nat_a = sb("nat_a", [P, 4, 256], F32)
        nat_b = sb("nat_b", [P, 2, 4, 2, PT * RANK], F32)
        nat_b_rem = sb("nat_b_rem", [P, 2, 2, 2, RANK], F32)
        nat_ad = sb("nat_ad", [P, 4, 96], F32)
        nat_c = sb("nat_c", [P, 2, P], F32)
        acc = sb("acc", [P, 9, G], F32)
        gated = sb("gated", [P, G], F32)
        act_f = sb("act_f", [P, G], F32)
        out_sb = sb("out_sb", [P, 2, 512], F32)
        bias_sb = sb("bias_sb", [P, H], F32)
        own_sb = sb("own_sb", [P, G], F32)
        b_col = sb("b_col", [P, KC], F32)
        ps = ctx.enter_context(nc.psum_tensor("ps", [P, 8, 512], F32))

        const_in, const_set = sem("const_in"), sem("const_set")
        nat_full = [sem(f"nat_full{i}") for i in range(NAT_SLOTS)]
        nat_c_full = [sem("nat_c_full0"), sem("nat_c_full1")]
        nat_down_full, nat_a_full, nat_b_full = sem("nat_down_full"), sem("nat_a_full"), sem("nat_b_full")
        nat_b_rem_full, nat_ad_full = sem("nat_b_rem_full"), sem("nat_ad_full")
        pool_passed = sem("pool_passed")
        plain_hi, plain_lo = sem("plain_hi"), sem("plain_lo")
        piece_turned, piece_hi, piece_lo = sem("piece_turned"), sem("piece_hi"), sem("piece_lo")
        mix_hi, mix_lo = sem("mix_hi"), sem("mix_lo")
        mixed_psum, mixed_hi, mixed_lo = sem("mixed_psum"), sem("mixed_hi"), sem("mixed_lo")
        xt_copied = sem("xt_copied")
        x1_psum, x1_sum, x1_hi, x1_lo = sem("x1_psum"), sem("x1_sum"), sem("x1_hi"), sem("x1_lo")
        rank_psum = sem("rank_psum")
        rank_sum, rank_hi, rank_lo = sem("rank_sum"), sem("rank_hi"), sem("rank_lo")
        rest_psum, rest_moved = sem("rest_psum"), sem("rest_moved")
        gate_psum, up_psum = sem("gate_psum"), sem("up_psum")
        gate_read, up_read = sem("gate_read"), sem("up_read")
        act_hi, act_lo = sem("act_hi"), sem("act_lo")
        down_psum, down_added = sem("down_psum"), sem("down_added")
        down_hi, down_lo = sem("down_hi"), sem("down_lo")
        out_psum, out_added = sem("out_psum"), sem("out_added")
        out_stored = [sem("out_stored0"), sem("out_stored1")]

        block = ctx.enter_context(nc.Block())


        def nat_filled(g, q, n):
            return (NAT_UNITS // NAT_SLOTS * g + PART_UNITS // NAT_SLOTS * q + (n // NAT_SLOTS + 1)) * 128

        def piece_number(g, q, c):
            return PIECES * g + PART_PIECES * q + c

        def low_number(g, q, c):
            return LOW_PIECES * g + PART_PIECES * q + lows_before(c)

        @block.sync
        def _(sp):
            sp.dma_start(bias_sb[:], bias.partition_broadcast(P)).then_inc(const_in, 16)
            sp.dma_start(own_sb[:], own_batch).then_inc(const_in, 16)
            sp.dma_start(act_f[:, 0:P], identity).then_inc(const_in, 16)
            b_rows = b_base.rearrange("(q k h) -> q h k", q=4, k=KC)
            for hq in range(4):
                with nc.allow_non_contiguous_dma(reason="1024 words, once"):
                    sp.dma_start(b_col[32 * hq:32 * hq + 32, :], b_rows[hq]).then_inc(const_in, 16)

            x_rows = x.rearrange("(n p) c -> n p c", p=P)
            part_rows = [a[0:FB, :].rearrange("(q fq ff j) (hq c) -> q ff fq j hq c", q=NQ, fq=4, j=PT, hq=4)
                         for a in (W_gate, W_up)]
            rest_rows = [a[FB:F, :].rearrange("(fq ff) (hq c) -> hq ff fq c", fq=2, hq=4) for a in (W_gate, W_up)]
            sign_rows = sign_w.rearrange("(u b o) (hq c) -> u hq o b c", u=KC, b=4, hq=4)
            down_rows = W_down[:, 0:FB].rearrange("(b h) (q fq c) -> q fq h b c", h=32, q=NQ, fq=4)
            down_rest = W_down[:, FB:F].rearrange("(b h) (fq c) -> fq h b c", h=32, fq=2)

            before = {NAT_W + u + 3: ("plain", 4 + u) for u in range(KC)}
            before |= {NAT_X + 3 + p: ("plain", p) for p in range(4)}
            before |= {NAT_REM + 3: ("piece", "REM")}
            before |= {NAT_SIGN[u] + 3: ("piece", f"S{u}") for u in range(8)}
            before |= {NAT_FIRST[k] + 3: ("piece", ("G0", "U0", "G1")[k]) for k in range(3)}

            def free_nat(g, q, n):
                if n >= NAT_GU + 3:
                    name = ("nextB", "nextU0", "nextG1", "U1", "G2", "U2")[n - NAT_GU - 3]
                    c = first_of(name) + (3 if name == "nextB" else 2)
                    if n < NAT_GU + 6:
                        c -= PART_PIECES
                    sp.wait_ge(piece_turned, piece_number(g, q, c))
                elif n >= 3:
                    kind, what = before[n]
                    if kind == "plain":
                        sp.wait_ge(plain_lo, 12 * g + what + 1)
                    else:
                        sp.wait_ge(piece_turned, piece_number(g, 0, first_of(what) + 2))

            def nat_quadrant(hq, n):
                return nat[32 * hq:32 * hq + 32, n % NAT_SLOTS, :].rearrange("p (b c) -> p b c", b=4)

            def load_gate_up(g, q, n, part, k):
                free_nat(g, q, n)
                for hq in range(4):
                    src = part_rows[k % 2][bass.ds(part, 1), :, :, k // 2, hq, :].rearrange("a f b c -> (a f) b c")
                    sp.dma_start(nat_quadrant(hq, n), src).then_inc(nat_full[n % NAT_SLOTS], 32)

            def load_down(part):
                for fq in range(4):
                    sp.dma_start(nat_down[32 * fq:32 * fq + 32],
                                 down_rows[bass.ds(part, 1), fq].rearrange("a h b c -> (a h) b c"))\
                      .then_inc(nat_down_full, 16)

            def load_sign(g, u):
                n = NAT_SIGN[u]
                free_nat(g, 0, n)
                for hq in range(4):
                    sp.dma_start(nat_quadrant(hq, n), sign_rows[u, hq]).then_inc(nat_full[n % NAT_SLOTS], 32)

            with sp.Fori(0, NG) as g:
                sp.wait_ge(down_psum, START + DOWNS * g)
                for p in range(4):
                    n = NAT_X + p
                    free_nat(g, 0, n)
                    sp.dma_start(nat[:, n % NAT_SLOTS, :], x_rows[bass.ds(4 * g + p, 1)].rearrange("a p c -> (a p) c"))\
                      .then_inc(nat_full[n % NAT_SLOTS], 128)
                for u in range(KC):
                    n = NAT_W + u
                    free_nat(g, 0, n)
                    sp.dma_start(nat[:, n % NAT_SLOTS, :], scratch[u]).then_inc(nat_full[n % NAT_SLOTS], 128)
                free_nat(g, 0, NAT_REM)
                for t in range(2):
                    for hq in range(4):
                        sp.dma_start(nat_quadrant(hq, NAT_REM)[:, 2 * t:2 * t + 2, :], rest_rows[t][hq])\
                          .then_inc(nat_full[NAT_REM % NAT_SLOTS], 16)
                for fq in range(2):
                    sp.dma_start(nat_down[32 * fq:32 * fq + 32, :, 0:32], down_rest[fq]).then_inc(nat_down_full, 32)
                for u in range(4):
                    load_sign(g, u)
                load_gate_up(g, 0, NAT_FIRST[0], 0, 0)
                load_gate_up(g, 0, NAT_FIRST[1], 0, 1)
                sp.wait_ge(piece_turned, piece_number(g, 0, first_of("DREM") + 2))
                load_down(0)
                for u in range(4, 8):
                    load_sign(g, u)
                load_gate_up(g, 0, NAT_FIRST[2], 0, 2)
                with sp.Fori(0, NQ - 1) as q:
                    for k in range(3, 6):
                        load_gate_up(g, q, NAT_GU + k, q, k)
                    for k in range(2):
                        load_gate_up(g, q, NAT_GU + PART_UNITS + k, q + 1, k)
                    sp.wait_ge(piece_turned, piece_number(g, q, first_of("D2") + 2))
                    load_down(q + 1)
                    load_gate_up(g, q, NAT_GU + PART_UNITS + 2, q + 1, 2)
                for k in range(3, 6):
                    load_gate_up(g, NQ - 1, NAT_GU + k, NQ - 1, k)

        @block.gpsimd
        def _(pool):
            b_rows = [a[0, :, 0:FB, :].rearrange("a (q fq ff j) r -> q a ff fq (j r)", q=NQ, fq=4, j=PT)
                      for a in (B_gate, B_up)]
            b_rest = [a[0, :, FB:F, :].rearrange("a (fq ff) r -> a ff fq r", fq=2) for a in (B_gate, B_up)]
            ad_rows = A_down[0, :, :, 0:FB].rearrange("a r (q fq c) -> q a fq r c", q=NQ, fq=4)
            ad_rest = A_down[0, :, :, FB:F].rearrange("a r (fq c) -> a fq r c", fq=2)

            def chosen(table, g, b):
                return pool.value_load(table[:, bass.ds(GB * g + b, 1)], min_val=0, max_val=NAD - 1)

            def wait(semaphore, value):
                pool.wait_ge(semaphore, value)
                pool.sem_inc(pool_passed, 1)

            def load_cond(g, p):
                wait(mix_lo, START + 4 * g + max(0, p - 1))
                for b2 in range(2):
                    i = chosen(cond_index, g, 2 * p + b2)
                    pool.dma_start(nat_c[S * b2:S * b2 + S, p % 2, S * b2:S * b2 + S],
                                   cond_w[bass.ds(i, 1)].rearrange("a c d -> (a c) d")).then_inc(nat_c_full[p % 2], 16)

            def load_a(g, a):
                for b in range(GB):
                    i = chosen(lora_index, g, b)
                    pool.dma_start(nat_a[b % 2::2, b // 2, :],
                                   a[0, bass.ds(i, 1)].rearrange("a r (hq c) -> hq (a r) c", hq=4)).then_inc(nat_a_full, 16)

            def load_b_down(g):
                slots = nat_a[:].rearrange("p a c -> p (a c)").rearrange("p (n s r) -> p n s r", s=2, r=RANK)
                for b in range(GB):
                    i = chosen(lora_index, g, b)
                    pool.dma_start(slots[32 * (b // 2):32 * (b // 2) + 32, :, b % 2, :],
                                   B_down[0, bass.ds(i, 1)].rearrange("a (n h) r -> (a h) n r", h=32))\
                        .then_inc(nat_a_full, 16)

            def load_rest(g):
                for b in range(GB):
                    i = chosen(lora_index, g, b)
                    for t in range(2):
                        pool.dma_start(nat_b_rem[32 * (b // 2):32 * (b // 2) + 32, t, :, b % 2, :],
                                       b_rest[t][bass.ds(i, 1)].rearrange("a f b c -> (a f) b c"))\
                            .then_inc(nat_b_rem_full, 16)
                    pool.dma_start(nat_ad[b % 2:64:2, b // 2, 0:32],
                                   ad_rest[bass.ds(i, 1)].rearrange("a f r c -> (a f) r c")).then_inc(nat_ad_full, 16)

            def load_b(g, part):
                for b in range(GB):
                    i = chosen(lora_index, g, b)
                    for t in range(2):
                        pool.dma_start(nat_b[32 * (b // 2):32 * (b // 2) + 32, t, :, b % 2, :],
                                       b_rows[t][bass.ds(part, 1), bass.ds(i, 1)].rearrange("q a f b c -> (q a f) b c"))\
                            .then_inc(nat_b_full, 16)

            def load_ad(g, part):
                for b in range(GB):
                    i = chosen(lora_index, g, b)
                    pool.dma_start(nat_ad[b % 2::2, b // 2, :],
                                   ad_rows[bass.ds(part, 1), bass.ds(i, 1)].rearrange("q a f r c -> (q a f) r c"))\
                        .then_inc(nat_ad_full, 16)

            def wait_turned(g, q, name, pieces):
                wait(piece_turned, piece_number(g, q, first_of(name) + pieces))

            pool.wait_ge(const_set, CONSTS)
            with pool.Fori(0, NG) as g:
                load_cond(g, 0)
                load_cond(g, 1)
                wait(piece_lo, START + LOW_PIECES * g)
                load_a(g, A_gate)
                load_cond(g, 2)
                load_cond(g, 3)
                load_rest(g)
                load_b(g, 0)
                wait_turned(g, 0, "AG", 2)
                load_a(g, A_up)
                wait_turned(g, 0, "AU", 2)
                load_b_down(g)
                wait_turned(g, 0, "ADREM", 1)
                load_ad(g, 0)
                with pool.Fori(0, NQ - 1) as q:
                    wait_turned(g, q - 1, "nextB", 3)
                    load_b(g, q + 1)
                    wait_turned(g, q, "AD", 1)
                    load_ad(g, q + 1)

        def bank_of(c):
            return ps[:, T_BANK + c % 2, :]

        def tiled(i, dst, src, *hi):
            if i >= 4:
                return (dst, src, *hi)
            dst, *hi = (v.rearrange("p (k q t) -> p q k t", q=4, k=KC) for v in (dst, *hi))
            return (dst, src.rearrange("p (q k t) -> p q k t", q=4, k=KC), *hi)

        def sign_target(u, half):
            return signs[:, 4 * half:4 * half + 4, P * u:P * u + P]

        @block.scalar
        def _(act):
            def copy(dst, src):
                return act.activation(dst, src, ACT.Copy)

            def slot_read(g, q, m):
                if m < 3:
                    act.wait_ge(down_psum, START + DOWNS * g)
                elif m < SPLIT_W + 3:
                    act.wait_ge(mixed_psum, START + 8 * g + 2 * (m - 3) + 2)
                elif m < SPLIT_AG + 3:
                    act.wait_ge(x1_psum, 8 * g + m - 3 - SPLIT_W + 1)
                elif m < SPLIT_REM + 3:
                    act.wait_ge(rank_psum, 2 * g + m - 3 - SPLIT_AG + 1)
                elif m == SPLIT_REM + 3:
                    act.wait_ge(rest_psum, g + 1)
                else:
                    k = m - 3 - SPLIT_GU
                    act.wait_ge(up_psum if k % 2 else gate_psum, (START if k % 2 else 0) + TILES * g + PT * q + k // 2 + 1)

            def plain_unit(g, i, n, m):
                act.wait_ge(nat_full[n % NAT_SLOTS], nat_filled(g, 0, n))
                slot_read(g, 0, m)
                copy(*tiled(i, split[:, m % SPLIT_SLOTS, 0, :], nat[:, n % NAT_SLOTS, :])).then_inc(plain_hi, 1)

            def piece(g, q, c, dst, src, func=ACT.Copy):
                act.wait_ge(piece_turned, piece_number(g, q, c) + 1)
                act.activation(dst, src, func).then_inc(piece_hi, 1)

            def unit(g, q, name, m):
                c = first_of(name)
                slot_read(g, q, m)
                for half in range(2):
                    piece(g, q, c + half, split[:, m % SPLIT_SLOTS, 0, 512 * half:512 * half + 512], bank_of(c + half))

            def sign_unit(g, u):
                c = first_of(f"S{u}")
                for half in range(2):
                    piece(g, 0, c + half, sign_target(u, half),
                          bank_of(c + half).rearrange("p (m o) -> p m o", m=4), ACT.Sign)

            def down_tile(g, q, j):
                c = first_of(f"D{j}")
                act.wait_ge(down_psum, START + DOWNS * g + 9 * (q + 1))
                for half in range(2):
                    piece(g, q, c + half, down_w[:, 0, j, 4 * half:4 * half + 4, :],
                          bank_of(c + half).rearrange("p (m h) -> p m h", m=4))

            def lora_b_tiles(g, q, name, part):
                c = first_of(name)
                act.wait_ge(up_psum, START + TILES * g + PT * part)
                for j in range(PT):
                    piece(g, q, c + j, lora_b[:, 0, j].rearrange("p t f -> p (t f)"), bank_of(c + j)[:, 0:256])

            def cond(g, p):
                act.wait_ge(nat_c_full[p % 2], 32 * (2 * g + p // 2 + 1))
                act.wait_ge(mixed_psum, START + 8 * g + max(0, 2 * p - 2))
                copy(mix[:, p % 2, 0, :], nat_c[:, p % 2, :]).then_inc(mix_hi, 1)

            def mixing(g, e):
                p, kh = e // 2, e % 2
                b0, b1 = S1_BANKS[e % 3]
                src = ps[:, b0:b1, :].rearrange("p a (k n t) -> p (a k) n t", k=2, n=2)
                act.wait_ge(mixed_psum, START + 8 * g + e + 1)
                copy(acc[:, 4 * kh:4 * kh + 4, P * p:P * p + P], src[:, :, 1, :]).then_inc(xt_copied, 1)
                copy(mixed[:, 0, 4 * kh:4 * kh + 4, P * p:P * p + P], src[:, :, 0, :]).then_inc(mixed_hi, 1)

            def x1_tile(g, u):
                act.wait_ge(x1_sum, 8 * g + u + 1)
                copy(x1[:, 0, u, :], acc[:, u, :]).then_inc(x1_hi, 1)

            def rank(g, n):
                act.wait_ge(rank_sum, 3 * g + n + 1)
                if n == 2:
                    act.wait_ge(up_psum, START + TILES * (g + 1))
                copy(lora_t[:, n % 2, 0, :], act_f[:]).then_inc(rank_hi, 1)

            def act_rest(g):
                act.wait_ge(up_read, START + ACTS * g)
                act.wait_ge(rest_psum, g + 1)
                act.activation(gated[0:64, :], ps[0:64, 1, :], ACT.Silu).then_inc(gate_read, 1)
                act.wait_ge(rank_lo, START + 3 * g + 2)
                copy(act_f[0:64, :], ps[64:128, 1, :]).then_inc(rest_moved, 1)
                act.wait_ge(up_read, START + ACTS * g + 1)
                copy(acts[0:64, 0, 0, :], act_f[0:64, :]).then_inc(act_hi, 1)

            def act_tile(g, q, j):
                act.wait_ge(up_read, START + ACTS * g + PT * q + j + 1)
                act.wait_ge(gate_psum, TILES * g + PT * q + j + 1)
                act.activation(gated[:], ps[:, 2 * j % 3, :], ACT.Silu).then_inc(gate_read, 1)
                act.wait_ge(up_read, START + ACTS * g + PT * q + j + 2)
                copy(acts[:, 0, j, :], act_f[:]).then_inc(act_hi, 1)

            def part(g, q, last):
                down_tile(g, q, 0)
                unit(g, q, "U1", SPLIT_GU + 3)
                act_tile(g, q, 0)
                unit(g, q, "G2", SPLIT_GU + 4)
                down_tile(g, q, 1)
                unit(g, q, "U2", SPLIT_GU + 5)
                act_tile(g, q, 1)
                down_tile(g, q, 2)
                c = first_of("AD")
                piece(g, q, c, lora_ad[:, 0].rearrange("p j a -> p (j a)"), bank_of(c)[:, 0:PT * P])
                if last:
                    act_tile(g, q, 2)
                    unit(g, q, "BD", SPLIT_BD - PART_UNITS * q)
                    return
                unit(g, q, "nextG0", SPLIT_GU + 6)
                act_tile(g, q, 2)
                lora_b_tiles(g, q, "nextB", q + 1)
                unit(g, q, "nextU0", SPLIT_GU + 7)
                unit(g, q, "nextG1", SPLIT_GU + 8)

            out_rows = out.rearrange("(n p) (a c) -> n p a c", p=P, a=2)
            for semaphore in out_stored:
                act.sem_inc(semaphore, 16 * START)
            with act.Fori(0, NG) as g:
                for p in range(2):
                    plain_unit(g, p, NAT_X + p, SPLIT_X + p)
                    cond(g, p)
                mixing(g, 0)
                mixing(g, 1)
                for p in range(2, 4):
                    plain_unit(g, p, NAT_X + p, SPLIT_X + p)
                    cond(g, p)
                    mixing(g, 2 * p - 2)
                    mixing(g, 2 * p - 1)
                plain_unit(g, 4, NAT_W, SPLIT_W)
                mixing(g, 6)
                mixing(g, 7)
                for u in range(1, 3):
                    plain_unit(g, 4 + u, NAT_W + u, SPLIT_W + u)
                for u in range(KC):
                    x1_tile(g, u)
                    if u < 5:
                        plain_unit(g, 7 + u, NAT_W + 3 + u, SPLIT_W + 3 + u)
                    else:
                        unit(g, 0, ("AG", "AU", "REM")[u - 5], SPLIT_W + 3 + u)
                c = first_of("BREM")
                act.wait_ge(out_psum, START + 8 * g)
                piece(g, 0, c, lora_b_rem[:, 0].rearrange("p t (n f) -> p (t n) f", n=2)[:, 0::3, :],
                      bank_of(c)[:, 0:P].rearrange("p (t f) -> p t f", t=2))
                act.wait_ge(x1_psum, 8 * g + KC)
                sign_unit(g, 0)
                sign_unit(g, 1)
                rank(g, 0)
                sign_unit(g, 2)
                rank(g, 1)
                sign_unit(g, 3)
                c = first_of("DREM")
                for half in range(2):
                    piece(g, 0, c + half, down_w[0:64, 0, 0, 4 * half:4 * half + 4, :],
                          bank_of(c + half)[0:64].rearrange("p (m h) -> p m h", m=4))
                c = first_of("ADREM")
                piece(g, 0, c, lora_ad[0:64, 0, 0, :], bank_of(c)[0:64, 0:P])
                unit(g, 0, "G0", SPLIT_GU)
                act_rest(g)
                unit(g, 0, "U0", SPLIT_GU + 1)
                lora_b_tiles(g, 0, "B", 0)
                for u in range(4, 8):
                    sign_unit(g, u)
                unit(g, 0, "G1", SPLIT_GU + 2)
                with act.Fori(0, NQ - 1) as q:
                    part(g, q, False)
                part(g, NQ - 1, True)
                rank(g, 2)
                act.wait_ge(down_psum, START + DOWNS * g + 9 * (NQ + 1))
                for m in range(KC):
                    act.wait_ge(down_added, DOWNS * g + 9 * (NQ + 1) + m + 1)
                    copy(down[:, 0, m, :], acc[:, m, :]).then_inc(down_hi, 1)
                for o in range(8):
                    act.wait_ge(out_added, START + 8 * g + o + 1)
                    act.dma_start(out_rows[bass.ds(4 * g + o // 2, 1), :, o % 2, :].rearrange("a p c -> (a p) c"),
                                  out_sb[:, o % 2, :]).then_inc(out_stored[o % 2], 16)
            for s in range(2):
                act.wait_ge(out_stored[s], 16 * (START + 4 * NG))

        @block.vector
        def _(dve):
            def lo(dst, full, hi):
                return dve.tensor_tensor(dst, full, hi.bitcast(F32), ALU.subtract)

            def plain_unit(g, i, n, m):
                s = m % SPLIT_SLOTS
                dve.wait_ge(plain_hi, 12 * g + i + 1)
                lo(*tiled(i, split[:, s, 1, :], nat[:, n % NAT_SLOTS, :], split[:, s, 0, :])).then_inc(plain_lo, 1)

            def turn(g, q, c, dst, src):
                if c < 2:
                    dve.wait_ge(piece_lo, START + LOW_PIECES * g)
                else:
                    dve.wait_ge(piece_hi, piece_number(g, q, c - 1))
                    dve.wait_ge(piece_lo, START + low_number(g, q, c - 1))
                dve.transpose(dst, src).then_inc(piece_turned, 1)

            def piece_low(g, q, c, dst, src, hi):
                dve.wait_ge(piece_hi, piece_number(g, q, c) + 1)
                lo(dst, src, hi).then_inc(piece_lo, 1)

            def turn_unit(g, q, c, rows):
                for half in range(2):
                    turn(g, q, c + half, bank_of(c + half).rearrange("p (k b h) -> p k b h", k=4, b=4),
                         rows.rearrange("p (b k h) -> p k b h", b=4, k=KC)[:, 4 * half:4 * half + 4])

            def unit_lows(g, q, c, m):
                s = m % SPLIT_SLOTS
                for half in range(2):
                    cols = slice(512 * half, 512 * half + 512)
                    piece_low(g, q, c + half, split[:, s, 1, cols], bank_of(c + half), split[:, s, 0, cols])

            def weight_unit(g, q, name, n, m):
                dve.wait_ge(nat_full[n % NAT_SLOTS], nat_filled(g, q, n))
                c = first_of(name)
                turn_unit(g, q, c, nat[:, n % NAT_SLOTS, :])
                unit_lows(g, q, c, m)

            def adapter_unit(g, name, fill, m):
                dve.wait_ge(nat_a_full, 128 * (3 * g + fill + 1))
                c = first_of(name)
                turn_unit(g, 0, c, nat_a[:].rearrange("p b c -> p (b c)"))
                unit_lows(g, 0, c, m)

            def b_down_unit(g, q, m):
                dve.wait_ge(nat_a_full, 128 * (3 * g + 3))
                c = first_of("BD")
                rows = nat_a[:].rearrange("p a c -> p (a c)").rearrange("p (q m s r) -> p m q r s", q=4, m=KC, s=2)
                for half in range(2):
                    if c + half >= 2:
                        dve.wait_ge(piece_hi, piece_number(g, q, c + half - 1))
                        dve.wait_ge(piece_lo, START + low_number(g, q, c + half - 1))
                    for m4 in range(4):
                        for hq in range(4):
                            t = dve.transpose(bank_of(c + half)[:, P * m4 + 32 * hq:P * m4 + 32 * hq + 32],
                                              rows[:, 4 * half + m4, hq])
                    t.then_inc(piece_turned, 1)
                unit_lows(g, q, c, m)

            def sign_unit(g, u):
                n = NAT_SIGN[u]
                dve.wait_ge(nat_full[n % NAT_SLOTS], nat_filled(g, 0, n))
                turn_unit(g, 0, first_of(f"S{u}"), nat[:, n % NAT_SLOTS, :])

            def down_tile(g, q, j):
                c = first_of(f"D{j}")
                dve.wait_ge(nat_down_full, 64 * (8 * g + q + 2))
                rows = nat_down[:].rearrange("p (q m) (f j) -> p m q f j", q=4, j=PT)
                for half in range(2):
                    turn(g, q, c + half, bank_of(c + half).rearrange("p (m q h) -> p m q h", m=4, q=4),
                         rows[:, 4 * half:4 * half + 4, :, :, j])
                for half in range(2):
                    ms = slice(4 * half, 4 * half + 4)
                    piece_low(g, q, c + half, down_w[:, 1, j, ms, :], bank_of(c + half).rearrange("p (m h) -> p m h", m=4),
                              down_w[:, 0, j, ms, :])

            def down_rest(g):
                c = first_of("DREM")
                dve.wait_ge(nat_down_full, 64 * (8 * g + 1))
                rows = nat_down[0:64, :, 0:32].rearrange("p (q m) f -> p m q f", q=4)
                for half in range(2):
                    turn(g, 0, c + half, bank_of(c + half)[0:64].rearrange("p (m q h) -> p m q h", m=4, q=4),
                         rows[:, 4 * half:4 * half + 4])
                for half in range(2):
                    ms = slice(4 * half, 4 * half + 4)
                    piece_low(g, 0, c + half, down_w[0:64, 1, 0, ms, :],
                              bank_of(c + half)[0:64].rearrange("p (m h) -> p m h", m=4), down_w[0:64, 0, 0, ms, :])

            def a_down_rest(g):
                c = first_of("ADREM")
                dve.wait_ge(nat_ad_full, 128 * (8 * g + 1))
                turn(g, 0, c, bank_of(c)[0:64, 0:P].rearrange("p (b a) -> p b a", b=4), nat_ad[0:64, :, 0:32])
                piece_low(g, 0, c, lora_ad[0:64, 1, 0, :], bank_of(c)[0:64, 0:P], lora_ad[0:64, 0, 0, :])

            def a_down_tiles(g, q):
                c = first_of("AD")
                dve.wait_ge(nat_ad_full, 128 * (8 * g + q + 2))
                turn(g, q, c, bank_of(c)[:, 0:PT * P].rearrange("p (j b a) -> p j b a", j=PT, b=4),
                     nat_ad[:].rearrange("p b (f j) -> p j b f", j=PT))
                piece_low(g, q, c, lora_ad[:, 1].rearrange("p j a -> p (j a)"), bank_of(c)[:, 0:PT * P],
                          lora_ad[:, 0].rearrange("p j a -> p (j a)"))

            def lora_b_tiles(g, q, name, part):
                c = first_of(name)
                dve.wait_ge(nat_b_full, 256 * (NQ * g + part + 1))
                rows = nat_b[:].rearrange("p t fq s (j r) -> p j (t fq) r s", j=PT)
                for j in range(PT):
                    turn(g, q, c + j, bank_of(c + j)[:, 0:256].rearrange("p (n r s) -> p n r s", n=8, r=RANK), rows[:, j])
                    piece_low(g, q, c + j, lora_b[:, 1, j].rearrange("p t f -> p (t f)"), bank_of(c + j)[:, 0:256],
                              lora_b[:, 0, j].rearrange("p t f -> p (t f)"))

            def lora_b_rest(g):
                c = first_of("BREM")
                dve.wait_ge(nat_b_rem_full, 256 * (g + 1))
                turn(g, 0, c, bank_of(c)[:, 0:P].rearrange("p (n r s) -> p n r s", n=4, r=RANK),
                     nat_b_rem[:].rearrange("p t fq s r -> p (t fq) r s"))
                halves = [lora_b_rem[:, s].rearrange("p t (n f) -> p (t n) f", n=2)[:, 0::3, :] for s in range(2)]
                piece_low(g, 0, c, halves[1], bank_of(c)[:, 0:P].rearrange("p (t f) -> p t f", t=2), halves[0])

            def cond(g, p):
                dve.wait_ge(mix_hi, 4 * g + p + 1)
                lo(mix[:, p % 2, 2, :], nat_c[:, p % 2, :], mix[:, p % 2, 0, :]).then_inc(mix_lo, 1)

            def mixing(g, e):
                p, kh = e // 2, e % 2
                b0, b1 = S1_BANKS[e % 3]
                src = ps[:, b0:b1, :].rearrange("p a (k n t) -> p (a k) n t", k=2, n=2)[:, :, 0, :]
                at = (slice(4 * kh, 4 * kh + 4), slice(P * p, P * p + P))
                dve.wait_ge(mixed_hi, 8 * g + e + 1)
                lo(mixed[:, 1, at[0], at[1]], src, mixed[:, 0, at[0], at[1]]).then_inc(mixed_lo, 1)

            def x1_total(g, u):
                dve.wait_ge(x1_psum, 8 * g + u + 1)
                dve.wait_ge(xt_copied, 8 * g + 8)
                dve.scalar_tensor_tensor(out=acc[:, u, :], in0=ps[:, u % 3, :], scalar=b_col[:, u:u + 1],
                                         in1=acc[:, u, :], op0=ALU.add, op1=ALU.add).then_inc(x1_sum, 1)

            def x1_low(g, u):
                dve.wait_ge(x1_hi, 8 * g + u + 1)
                lo(x1[:, 1, u, :], acc[:, u, :], x1[:, 0, u, :]).then_inc(x1_lo, 1)

            def rank(g, n):
                if n < 2:
                    dve.wait_ge(rank_psum, 2 * g + n + 1)
                    src = ps[:, (2, 0)[n], :]
                else:
                    dve.wait_ge(down_added, DOWNS * g + 9 * (NQ + 1))
                    src = acc[:, 8, :]
                dve.wait_ge(rank_lo, START + 3 * g + n)
                dve.wait_ge(act_lo, START + ACTS * g + (ACTS if n == 2 else 0))
                dve.tensor_tensor(act_f[:], src, own_sb[:], ALU.mult).then_inc(rank_sum, 1)
                dve.wait_ge(rank_hi, 3 * g + n + 1)
                lo(lora_t[:, n % 2, 1, :], act_f[:], lora_t[:, n % 2, 0, :]).then_inc(rank_lo, 1)

            def act_rest(g):
                dve.wait_ge(rest_moved, g + 1)
                dve.tensor_tensor(act_f[0:64, :], gated[0:64, :], act_f[0:64, :], ALU.mult).then_inc(up_read, 1)
                dve.wait_ge(act_hi, ACTS * g + 1)
                lo(acts[0:64, 1, 0, :], act_f[0:64, :], acts[0:64, 0, 0, :]).then_inc(act_lo, 1)

            def act_tile(g, q, j):
                n = ACTS * g + PT * q + j + 1
                dve.wait_ge(up_psum, START + TILES * g + PT * q + j + 1)
                dve.wait_ge(gate_read, n + 1)
                dve.wait_ge(act_lo, START + n)
                dve.tensor_tensor(act_f[:], ps[:, (2 * j + 1) % 3, :], gated[:], ALU.mult).then_inc(up_read, 1)
                dve.wait_ge(act_hi, n + 1)
                lo(acts[:, 1, j, :], act_f[:], acts[:, 0, j, :]).then_inc(act_lo, 1)

            def down_add(g, stage, m):
                n = DOWNS * g + 9 * stage + m + 1
                dve.wait_ge(down_psum, START + n)
                src = ps[:, D_BANK + m % 3, :]
                if isinstance(stage, int) and stage == 0:
                    dve.wait_ge(x1_lo, 8 * g + KC)
                    dve.wait_ge(rank_lo, START + 3 * g)
                    dve.tensor_copy(acc[:, m, :], src).then_inc(down_added, 1)
                else:
                    dve.wait_ge(down_added, n - 9)
                    dve.tensor_tensor(acc[:, m, :], src, acc[:, m, :], ALU.add).then_inc(down_added, 1)

            def down_low(g, m):
                dve.wait_ge(down_hi, 8 * g + m + 1)
                lo(down[:, 1, m, :], acc[:, m, :], down[:, 0, m, :]).then_inc(down_lo, 1)

            def part(g, q, last):
                down_tile(g, q, 0)
                weight_unit(g, q, "U1", NAT_GU + 3, SPLIT_GU + 3)
                act_tile(g, q, 0)
                weight_unit(g, q, "G2", NAT_GU + 4, SPLIT_GU + 4)
                down_tile(g, q, 1)
                weight_unit(g, q, "U2", NAT_GU + 5, SPLIT_GU + 5)
                act_tile(g, q, 1)
                down_tile(g, q, 2)
                a_down_tiles(g, q)
                if last:
                    act_tile(g, q, 2)
                    b_down_unit(g, q, SPLIT_BD)
                    for m in range(9):
                        down_add(g, q + 1, m)
                    return
                weight_unit(g, q, "nextG0", NAT_GU + 6, SPLIT_GU + 6)
                act_tile(g, q, 2)
                lora_b_tiles(g, q, "nextB", q + 1)
                weight_unit(g, q, "nextU0", NAT_GU + 7, SPLIT_GU + 7)
                for m in range(3):
                    down_add(g, q + 1, m)
                weight_unit(g, q, "nextG1", NAT_GU + 8, SPLIT_GU + 8)
                for m in range(3, 9):
                    down_add(g, q + 1, m)

            dve.memset(nat_c[:], 0.0).then_inc(const_set, 1)
            dve.memset(lora_b_rem[:].bitcast(F32), 0.0).then_inc(const_set, 1)
            dve.wait_ge(const_in, 16 * 7)
            dve.tensor_copy(ident[:], act_f[:, 0:P]).then_inc(const_set, 1)
            for s in range(2):
                dve.tensor_copy(mix[:, s, 1, :], act_f[:, 0:P]).then_inc(const_set, 1)
            dve.wait_ge(const_set, CONSTS)
            for semaphore in (piece_lo, mix_lo, up_read, out_added, rank_lo, act_lo):
                dve.sem_inc(semaphore, START)
            with dve.Fori(0, NG) as g:
                for p in range(2):
                    plain_unit(g, p, NAT_X + p, SPLIT_X + p)
                    cond(g, p)
                mixing(g, 0)
                mixing(g, 1)
                for p in range(2, 4):
                    plain_unit(g, p, NAT_X + p, SPLIT_X + p)
                    cond(g, p)
                    mixing(g, 2 * p - 2)
                    mixing(g, 2 * p - 1)
                plain_unit(g, 4, NAT_W, SPLIT_W)
                mixing(g, 6)
                mixing(g, 7)
                for u in range(1, 3):
                    plain_unit(g, 4 + u, NAT_W + u, SPLIT_W + u)
                for u in range(KC):
                    x1_total(g, u)
                    if u < 5:
                        plain_unit(g, 7 + u, NAT_W + 3 + u, SPLIT_W + 3 + u)
                    elif u == 5:
                        dve.wait_ge(out_added, START + 8 * g)
                        adapter_unit(g, "AG", 0, SPLIT_AG)
                    elif u == 6:
                        adapter_unit(g, "AU", 1, SPLIT_AU)
                    else:
                        weight_unit(g, 0, "REM", NAT_REM, SPLIT_REM)
                    x1_low(g, u)
                lora_b_rest(g)
                sign_unit(g, 0)
                sign_unit(g, 1)
                rank(g, 0)
                sign_unit(g, 2)
                rank(g, 1)
                sign_unit(g, 3)
                down_rest(g)
                a_down_rest(g)
                weight_unit(g, 0, "G0", NAT_FIRST[0], SPLIT_GU)
                act_rest(g)
                weight_unit(g, 0, "U0", NAT_FIRST[1], SPLIT_GU + 1)
                lora_b_tiles(g, 0, "B", 0)
                for u in range(4, 8):
                    sign_unit(g, u)
                    down_add(g, 0, 2 * u - 8)
                    down_add(g, 0, 2 * u - 7)
                weight_unit(g, 0, "G1", NAT_FIRST[2], SPLIT_GU + 2)
                down_add(g, 0, 8)
                with dve.Fori(0, NQ - 1) as q:
                    part(g, q, False)
                part(g, NQ - 1, True)
                rank(g, 2)
                for m in range(KC):
                    down_add(g, NQ + 1, m)
                    if m > 0:
                        down_low(g, m - 1)
                down_low(g, KC - 1)
                for o in range(8):
                    dve.wait_ge(out_psum, START + 8 * g + o + 1)
                    dve.wait_ge(out_stored[o % 2], 16 * (START + 4 * g + o // 2))
                    h = o % 2
                    dve.tensor_tensor(out_sb[:, h, :], ps[:, OUT_BANKS[o], :], bias_sb[:, 512 * h:512 * h + 512],
                                      ALU.add).then_inc(out_added, 1)

        @block.tensor
        def _(pe):
            def product(dst, a, b, first, last):
                pe.matmul(dst, a[0], b[0], start=first, stop=False)
                pe.matmul(dst, a[0], b[1], start=False, stop=False)
                return pe.matmul(dst, a[1], b[0], start=False, stop=last)

            def stationary(m, k):
                return [split[:, m % SPLIT_SLOTS, s, P * k:P * k + P] for s in range(2)]

            def mixing(g, e):
                p, kh = e // 2, e % 2
                if kh == 0:
                    pe.wait_ge(plain_lo, 12 * g + p + 1)
                    pe.wait_ge(mix_lo, START + 4 * g + p + 1)
                if e < 3:
                    pe.wait_ge(out_added, START + 8 * g)
                else:
                    pe.wait_ge(mixed_lo, 8 * g + e - 2)
                    pe.wait_ge(xt_copied, 8 * g + e - 2)
                for k in range(4):
                    bank = S1_BANKS[e % 3][0] + k // 2
                    dst = ps[:, bank, 256 * (k % 2):256 * (k % 2) + 256]
                    xs = stationary(SPLIT_X + p, 4 * kh + k)
                    both = mix[:, p % 2, 0:2, :].rearrange("p n t -> p (n t)")
                    pe.matmul(dst, xs[0], both, start=True, stop=False)
                    pe.matmul(dst[:, 0:P], xs[0], mix[:, p % 2, 2, :], start=False, stop=False)
                    mm = pe.matmul(dst, xs[1], both, start=False, stop=True)
                mm.then_inc(mixed_psum, 1)

            def first_layer(g, u):
                m = SPLIT_W + u
                pe.wait_ge(plain_lo, 12 * g + 4 + u + 1)
                if u == 0:
                    pe.wait_ge(mixed_lo, 8 * g + 8)
                    pe.wait_ge(xt_copied, 8 * g + 8)
                if u >= 3:
                    pe.wait_ge(x1_sum, 8 * g + u - 2)
                for k in range(KC):
                    mm = product(ps[:, u % 3, :], stationary(m, k), [mixed[:, s, k, :] for s in range(2)],
                                 k == 0, k == KC - 1)
                mm.then_inc(x1_psum, 1)

            def wait_unit(g, q, name):
                pe.wait_ge(piece_lo, START + low_number(g, q, first_of(name) + 2))

            def of_x1(dst, m, last):
                for k in range(KC):
                    mm = product(dst, stationary(m, k), [x1[:, s, k, :] for s in range(2)], k == 0, last and k == KC - 1)
                return mm

            def rank(g, n):
                wait_unit(g, 0, ("AG", "AU")[n])
                pe.wait_ge(x1_sum, 8 * g + (6, 7)[n])
                pe.wait_ge(x1_lo, 8 * g + KC)
                of_x1(ps[:, (2, 0)[n], :], SPLIT_AG + n, True).then_inc(rank_psum, 1)

            def gate_up_rest(g):
                wait_unit(g, 0, "REM")
                pe.wait_ge(x1_sum, 8 * g + 8)
                of_x1(ps[:, 1, :], SPLIT_REM, False)
                pe.wait_ge(piece_lo, START + low_number(g, 0, first_of("BREM") + 1))
                pe.wait_ge(rank_lo, START + 3 * g + 2)
                for t in range(2):
                    mm = product(ps[:, 1, :], [lora_b_rem[:, s, t, :] for s in range(2)],
                                 [lora_t[:, t, s, :] for s in range(2)], False, t == 1)
                mm.then_inc(rest_psum, 1)

            def down_rest(g):
                pe.wait_ge(piece_lo, START + low_number(g, 0, first_of("ADREM") + 1))
                pe.wait_ge(act_lo, START + ACTS * g + 1)
                for m in range(9):
                    if m >= 3:
                        pe.wait_ge(down_added, DOWNS * g + m - 2)
                    w = [(down_w[0:64, s, 0, m, :] if m < KC else lora_ad[0:64, s, 0, :]) for s in range(2)]
                    product(ps[:, D_BANK + m % 3, :], w, [acts[0:64, s, 0, :] for s in range(2)], True, True)\
                        .then_inc(down_psum, 1)

            def gate_up(g, q, k, name, in_part):
                t, j = k % 2, k // 2
                pe.wait_ge(piece_lo, START + low_number(g, in_part, first_of(name) + 2))
                if t == 0:
                    pe.wait_ge(up_read, START + ACTS * g + PT * q + j)
                else:
                    pe.wait_ge(gate_read, ACTS * g + PT * q + j + 1)
                dst = ps[:, k % 3, :]
                of_x1(dst, SPLIT_GU + k, False)
                if k == 0:
                    pe.wait_ge(piece_lo, START + low_number(g, q - 1, first_of("nextB") + 3))
                product(dst, [lora_b[:, s, j, t, :] for s in range(2)], [lora_t[:, t, s, :] for s in range(2)],
                        False, True).then_inc(up_psum if t else gate_psum, 1)

            def down_part(g, q):
                pe.wait_ge(piece_lo, START + low_number(g, q, first_of("AD") + 1))

                def tiles(m, js):
                    for j in js:
                        w = [(down_w[:, s, j, m, :] if m < KC else lora_ad[:, s, j, :]) for s in range(2)]
                        mm = product(ps[:, D_BANK + m % 3, :], w, [acts[:, s, j, :] for s in range(2)],
                                     j == 0, j == PT - 1)
                    return mm

                def bank_read(m):
                    pe.wait_ge(down_added, DOWNS * g + 9 * (q + 1) + m - 2)

                pe.wait_ge(act_lo, START + ACTS * g + PT * q + 3)
                for m in range(3):
                    bank_read(m)
                    tiles(m, (0, 1))
                pe.wait_ge(act_lo, START + ACTS * g + PT * q + 4)
                for m in range(3):
                    tiles(m, (2,)).then_inc(down_psum, 1)
                for m in range(3, 9):
                    bank_read(m)
                    tiles(m, range(PT)).then_inc(down_psum, 1)

            def part(g, q):
                for k, name in enumerate(("nextG0", "nextU0", "nextG1", "U1", "G2", "U2")):
                    gate_up(g, q, k, name, q if k > 2 else q - 1)
                down_part(g, q)

            def x1_rows(o):
                i, h = o // 2, o % 2
                dst = ps[:, OUT_BANKS[o], :].rearrange("p (q k h) -> p k q h", q=2, k=KC)
                for k in range(KC):
                    for s in range(2):
                        pe.matmul(dst[:, k], x1[:, s, k, P * i:P * i + P], ident[:, 64 * h:64 * h + 64],
                                  start=(k == 0 and s == 0), stop=False)

            def sign_product(o, m):
                i, h = o // 2, o % 2
                for s in range(2):
                    mm = pe.matmul(ps[:, OUT_BANKS[o], :], down[:, s, m, P * i:P * i + P],
                                   signs[:, m, 512 * h:512 * h + 512], start=False, stop=(m == KC - 1 and s == 1))
                return mm

            pe.wait_ge(const_set, CONSTS)
            for semaphore in (down_psum, mixed_psum, up_psum, out_psum):
                pe.sem_inc(semaphore, START)
            with pe.Fori(0, NG) as g:
                for e in range(8):
                    mixing(g, e)
                for u in range(KC):
                    first_layer(g, u)
                for n in range(2):
                    rank(g, n)
                gate_up_rest(g)
                down_rest(g)
                with pe.Fori(0, NQ - 1) as q:
                    part(g, q)
                part(g, NQ - 1)
                pe.wait_ge(up_read, START + ACTS * (g + 1))
                pe.wait_ge(piece_lo, START + LOW_PIECES * (g + 1))
                for o in range(4):
                    x1_rows(o)
                pe.wait_ge(rank_lo, START + 3 * g + 3)
                for m in range(KC):
                    pe.wait_ge(down_added, DOWNS * g + 9 * (NQ + 1) + m - 2)
                    product(ps[:, D_BANK + m % 3, :], stationary(SPLIT_BD, m), [lora_t[:, 0, s, :] for s in range(2)],
                            True, True).then_inc(down_psum, 1)
                pe.wait_ge(piece_hi, piece_number(g, 0, first_of("S7") + 2))
                for m in range(KC):
                    pe.wait_ge(down_lo, 8 * g + m + 1)
                    for o in range(4):
                        mm = sign_product(o, m)
                        if m == KC - 1:
                            mm.then_inc(out_psum, 1)
                pe.wait_ge(down_added, DOWNS * (g + 1))
                for o in range(4, 8):
                    x1_rows(o)
                    for m in range(KC):
                        mm = sign_product(o, m)
                    mm.then_inc(out_psum, 1)


_INS = ["x", "itok_B_0_15", "itok_B_2_6", "L0_cond_weights", "L0_ffn_W_base", "L0_ffn_b_base", "L0_ffn_enc0",
        "L0_ffn_enc1", "L0_ffn_coefs0", "L0_ffn_coefs1", "L0_ffn_mask0", "L0_ffn_mask1", "L1_cond_W_gate",
        "L1_cond_W_up", "L1_cond_W_down", "L1_cond_A_gate", "L1_cond_B_gate", "L1_cond_A_up", "L1_cond_B_up",
        "L1_cond_A_down", "L1_cond_B_down", "L1_ffn_weight", "L1_ffn_bias"]


def shape_constants():
    import numpy as np

    n = np.arange(H)
    table = np.empty((H, H))
    table[0] = 1 / np.sqrt(H)
    for f in range(1, H // 2):
        angle = 2 * np.pi * (f * n % H) / H
        table[2 * f - 1] = np.sqrt(2 / H) * np.cos(angle)
        table[2 * f] = np.sqrt(2 / H) * np.sin(angle)
    table[H - 1] = (1 - 2 * (n % 2)) / np.sqrt(H)
    row = np.arange(P)
    batch = 2 * (row // 32) + row % 2
    own = 0.5 * (batch[:, None] == np.arange(G)[None, :] // S)
    return {"fourier": table.astype(np.float32), "identity": np.eye(P, dtype=np.float32),
            "own_batch": own.astype(np.float32)}


def kernel(**inputs):
    import numpy as np
    import concourse.bacc as bacc
    from concourse.bass_utils import run_bass_kernel_spmd

    nc = bacc.Bacc("TRN2", target_bir_lowering=False, num_devices=1, dynamic_dma_scratch_size=4096)
    arrays, ap = {}, {}
    for name, a in {**{n: inputs[n] for n in _INS}, **shape_constants()}.items():
        a = np.ascontiguousarray(a)
        if name == "x":
            a = a.reshape(NB * S, H)
        if name.startswith("itok"):
            a = a.reshape(1, NB)
        arrays[name] = a
        ap[name] = nc.dram_tensor(name, a.shape, mybir.dt.from_np(a.dtype), kind="ExternalInput").ap()
    out = nc.dram_tensor("out", (NB * S, H), F32, kind="ExternalOutput").ap()
    scratch = nc.dram_tensor("effective_weight", (KC, P, H), F32, kind="Internal").ap()
    build_effective_weight(nc, scratch, ap["L0_ffn_W_base"], ap["L0_ffn_enc0"], ap["L0_ffn_enc1"],
                           (ap["L0_ffn_coefs0"], ap["L0_ffn_coefs1"]), (ap["L0_ffn_mask0"], ap["L0_ffn_mask1"]),
                           ap["fourier"])
    c = {n.removeprefix("L1_cond_"): v for n, v in ap.items() if n.startswith("L1_cond_")}
    build_layers(nc, ap["x"], ap["itok_B_0_15"], ap["itok_B_2_6"], ap["L0_cond_weights"], scratch,
                 ap["L0_ffn_b_base"], c["W_gate"], c["W_up"], c["W_down"], c["A_gate"], c["B_gate"], c["A_up"],
                 c["B_up"], c["A_down"], c["B_down"], ap["L1_ffn_weight"], ap["L1_ffn_bias"], ap["identity"],
                 ap["own_batch"], out)
    r = run_bass_kernel_spmd(nc, [arrays], core_ids=[0])
    return np.asarray(r.results[0]["out"]).reshape(NB, S, H)
```

```python
from contextlib import ExitStack

import concourse.bass as bass
from concourse import mybir

F32 = mybir.dt.float32
F32R = mybir.dt.float32r
U8 = mybir.dt.uint8
ALU = mybir.AluOpType
ACT = mybir.ActivationFunctionType

P = 128
H = 1024
KC = H // P
F = 2752
PT = 3
NQ = F // (P * PT)
TILES = NQ * PT
FB = NQ * P * PT
FR = F - FB
G = 512
S = 64
NB = 32
NG = NB * S // G
GB = G // S
RANK = 16
NE, R0, R1 = 3, 32, 8
RL = R0 + R1
NAD = 16

NAT_SLOTS = 3
NAT_X, NAT_W, NAT_REM, NAT_SIGN, NAT_GU = 0, 4, 12, 13, 15
NAT_UNITS = 57
SPLIT_SLOTS = 3
SPLIT_X, SPLIT_W, SPLIT_AG, SPLIT_AU, SPLIT_REM, SPLIT_GU, SPLIT_BD = 0, 4, 12, 13, 14, 15, 57
SPLIT_UNITS = 60
PART_UNITS = 6
assert NAT_UNITS % NAT_SLOTS == SPLIT_UNITS % SPLIT_SLOTS == PART_UNITS % NAT_SLOTS == 0

HEAD = (["AG"] * 2 + ["AU"] * 2 + ["REM"] * 2 + ["BREM"] + ["S6"] * 2 + ["S7"] * 2 + ["G0"] * 2
        + ["DREM"] * 2 + ["ADREM"] + ["B"] * 3 + ["U0"] * 2 + ["G1"] * 2)
PART = (["D0"] * 2 + ["U1"] * 2 + ["G2"] * 2 + ["D1"] * 2 + ["U2"] * 2 + ["D2"] * 2 + ["AD"] + ["Sq"] * 2
        + ["nextG0"] * 2 + ["nextB"] * 3 + ["nextU0"] * 2 + ["nextG1"] * 2)
LAST = PART[:13] + ["BD"] * 2
PART_PIECES = len(PART)
PIECES = len(HEAD) + (NQ - 1) * PART_PIECES + len(LAST)
SIGN_PIECES = 16
LOW_PIECES = PIECES - SIGN_PIECES
PART_LOWS = PART_PIECES - 2
assert PIECES % 2 == 0 and PART_PIECES % 2 == 0


def first_of(name):
    return HEAD.index(name) if name in HEAD else len(HEAD) + (PART if name in PART else LAST).index(name)


def lows_before(c):
    return sum(not x.startswith("S") for x in (HEAD + PART)[:max(0, c)])


ACTS = TILES + 1
START = 1
CONSTS = 5
S1_BANKS = ((0, 2), (2, 4), (4, 6))
OUT_BANKS = (0, 1, 2, 6, 7, 3, 4, 5)
X1_BANKS = (6, 7, 2, 0, 1, 2, 0, 1)
DOWN_ORDER = (8, 0, 1, 2, 3, 4, 5, 6, 7)
DOWNS = 9 * (1 + NQ)
BASE_SLOTS = 4
T_BANK = 6
D_BANK = 3


def build_layers(nc, x, cond_index, lora_index, cond_w, W_base, b_base, enc0, enc1, coefs, masks, fourier, scratch,
                 W_gate, W_up, W_down, A_gate, B_gate, A_up, B_up, A_down, B_down, sign_w, bias, identity,
                 own_batch, out):
    with ExitStack() as ctx:
        def sb(name, shape, dtype):
            return ctx.enter_context(nc.sbuf_tensor(name, shape, dtype))

        def sem(name):
            return ctx.enter_context(nc.semaphore(name))

        with ExitStack() as early:
            def early_sb(name, shape, dtype=F32):
                return early.enter_context(nc.sbuf_tensor(name, shape, dtype))[:]

            table = early_sb("fourier_table", [P, KC, H])
            base = early_sb("base", [P, 2, 4, 256])
            base_t = early_sb("base_t", [P, BASE_SLOTS, H])
            low_rank = early_sb("low_rank", [RL, H])
            enc_tiles = early_sb("enc_tiles", [RL, KC, P])
            wsum = early_sb("wsum", [P, KC, RL])
            coef, kept = ([early_sb(f"{name}{i}", [P, NE, KC * r]) for i, r in enumerate((R0, R1))]
                          for name in ("coef", "kept"))
            enc = early_sb("enc", [RL, H])

        x1 = sb("x1", [P, 2, KC, G], F32R)
        hidden = sb("hidden", [P, 9216], F32R)
        lora_b = sb("lora_b", [P, 2, PT, 2, P], F32R)
        lora_t = sb("lora_t", [P, 2, 2, G], F32R)
        turned = sb("turned", [P, 2 * KC * G], F32R)
        split = sb("split", [P, SPLIT_SLOTS, 2, H], F32R)
        lora_b_rem = sb("lora_b_rem", [P, 2, 2, P], F32R)
        lora_ad = sb("lora_ad", [P, 2, PT, P], F32R)
        mix = sb("mix", [P, 2, 3, P], F32R)
        ident = sb("ident", [P, P], F32R)
        mixed = turned[:].rearrange("p (s k t) -> p s k t", s=2, k=KC)
        signs = turned[:].rearrange("p (m o) -> p m o", m=KC)
        down_w = hidden[:, 0:6144].rearrange("p (s j m h) -> p s j m h", s=2, j=PT, m=KC)
        acts = hidden[:, 6144:9216].rearrange("p (s j t) -> p s j t", s=2, j=PT)
        down = hidden[:, 0:8192].rearrange("p (s m t) -> p s m t", s=2, m=KC)

        nat = sb("nat", [P, NAT_SLOTS, H], F32)
        nat_down = sb("nat_down", [P, 32, 96], F32)
        nat_a = sb("nat_a", [P, 2, 4, 256], F32)
        nat_b = sb("nat_b", [P, 2, 4, 2, PT * RANK], F32)
        nat_b_rem = sb("nat_b_rem", [P, 2, 2, 2, RANK], F32)
        nat_ad = sb("nat_ad", [P, 4, 96], F32)
        nat_c = sb("nat_c", [P, 2, P], F32)
        acc = sb("acc", [P, 9, G], F32)
        gated = sb("gated", [P, G], F32)
        act_f = sb("act_f", [P, G], F32)
        out_sb = sb("out_sb", [P, 2, 512], F32)
        bias_sb = sb("bias_sb", [P, H], F32)
        own_sb = sb("own_sb", [P, G], F32)
        b_col = sb("b_col", [P, KC], F32)
        coef_mask = [sb(f"coef_mask{i}", [P, NE, KC * r], U8) for i, r in enumerate((R0, R1))]
        ps = ctx.enter_context(nc.psum_tensor("ps", [P, 8, 512], F32))

        ident_in, const_in, const_set = sem("ident_in"), sem("const_in"), sem("const_set")
        coef_in, table_in, enc_in = sem("coef_in"), sem("table_in"), sem("enc_in")
        base_in = [sem("base_in0"), sem("base_in1")]
        kept_step, wsum_done, g_psum, g_read = sem("kept_step"), sem("wsum_done"), sem("g_psum"), sem("g_read")
        base_turned, w_psum, w_added = sem("base_turned"), sem("w_psum"), sem("w_added")
        w_stored = [sem(f"w_stored{i}") for i in range(BASE_SLOTS)]
        nat_full = [sem(f"nat_full{i}") for i in range(NAT_SLOTS)]
        nat_c_full = [sem("nat_c_full0"), sem("nat_c_full1")]
        nat_down_full, nat_b_full = sem("nat_down_full"), sem("nat_b_full")
        nat_a_full = [sem("nat_a_full0"), sem("nat_a_full1")]
        nat_b_rem_full, nat_ad_full, nat_sign_full = sem("nat_b_rem_full"), sem("nat_ad_full"), sem("nat_sign_full")
        pool_passed = sem("pool_passed")
        plain_hi, plain_lo = sem("plain_hi"), sem("plain_lo")
        piece_turned, piece_hi, piece_lo = sem("piece_turned"), sem("piece_hi"), sem("piece_lo")
        mix_hi, mix_lo = sem("mix_hi"), sem("mix_lo")
        mixed_psum, mixed_hi, mixed_lo = sem("mixed_psum"), sem("mixed_hi"), sem("mixed_lo")
        xt_copied = sem("xt_copied")
        x1_psum, x1_sum, x1_hi, x1_lo = sem("x1_psum"), sem("x1_sum"), sem("x1_hi"), sem("x1_lo")
        rank_psum = sem("rank_psum")
        rank_sum, rank_hi, rank_lo = sem("rank_sum"), sem("rank_hi"), sem("rank_lo")
        rest_psum, rest_moved = sem("rest_psum"), sem("rest_moved")
        gate_psum, up_psum = sem("gate_psum"), sem("up_psum")
        gate_read, up_read = sem("gate_read"), sem("up_read")
        act_hi, act_lo = sem("act_hi"), sem("act_lo")
        down_psum, down_added = sem("down_psum"), sem("down_added")
        down_hi, down_lo = sem("down_hi"), sem("down_lo")
        out_psum, out_added = sem("out_psum"), sem("out_added")
        out_stored = [sem("out_stored0"), sem("out_stored1")]

        block = ctx.enter_context(nc.Block())

        def nat_filled(g, q, n):
            return (NAT_UNITS // NAT_SLOTS * g + PART_UNITS // NAT_SLOTS * q + (n // NAT_SLOTS + 1)) * 128

        def piece_number(g, q, c):
            return PIECES * g + PART_PIECES * q + c

        def low_number(g, q, c):
            return LOW_PIECES * g + PART_LOWS * q + lows_before(c)

        @block.sync
        def _(sp):
            def constants():
                sp.dma_start(own_sb[:], own_batch).then_inc(const_in, 16)
                b_rows = b_base.rearrange("(q k h) -> q h k", q=4, k=KC)
                for hq in range(4):
                    with nc.allow_non_contiguous_dma(reason="1024 words, once"):
                        sp.dma_start(b_col[32 * hq:32 * hq + 32, :], b_rows[hq]).then_inc(const_in, 16)
                sp.dma_start(bias_sb[:], bias.partition_broadcast(P)).then_inc(const_in, 16)

            base_rows = W_base.rearrange("(oq u oo) (hq c) -> u hq oo oq c", oq=4, u=KC, hq=4)

            def load_base(u):
                if u >= 2:
                    sp.wait_ge(base_turned, u - 1)
                for hq in range(4):
                    sp.dma_start(base[32 * hq:32 * hq + 32, u % 2], base_rows[u, hq]).then_inc(base_in[u % 2], 16)

            x_rows = x.rearrange("(n p) c -> n p c", p=P)
            part_rows = [a[0:FB, :].rearrange("(q fq ff j) (hq c) -> q ff fq j hq c", q=NQ, fq=4, j=PT, hq=4)
                         for a in (W_gate, W_up)]
            rest_rows = [a[FB:F, :].rearrange("(fq ff) (hq c) -> hq ff fq c", fq=2, hq=4) for a in (W_gate, W_up)]
            sign_rows = sign_w.rearrange("(u b o) (hq c) -> u hq o b c", u=KC, b=4, hq=4)
            down_rows = W_down[:, 0:FB].rearrange("(b h) (q fq c) -> q fq h b c", h=32, q=NQ, fq=4)
            down_rest = W_down[:, FB:F].rearrange("(b h) (fq c) -> fq h b c", h=32, fq=2)

            before = {NAT_W + u + 3: ("plain", 4 + u) for u in range(KC)}
            before |= {NAT_X + 3 + p: ("plain", p) for p in range(4)}
            before |= {NAT_REM + 3: ("piece", "REM")}
            before |= {NAT_SIGN + 3 + i: ("piece", f"S{6 + i}") for i in range(2)}

            def free_nat(g, q, n):
                if n >= NAT_GU + 3:
                    name = ("nextG0", "nextU0", "nextG1", "U1", "G2", "U2")[n - NAT_GU - 3]
                    c = first_of(name) + 2
                    if n < NAT_GU + 6:
                        c -= PART_PIECES
                    sp.wait_ge(piece_turned, piece_number(g, q, c))
                elif n >= 3:
                    kind, what = before[n]
                    if kind == "plain":
                        sp.wait_ge(plain_lo, 12 * g + what + 1)
                    else:
                        sp.wait_ge(piece_turned, piece_number(g, 0, first_of(what) + 2))

            def nat_quadrant(hq, n):
                return nat[32 * hq:32 * hq + 32, n % NAT_SLOTS, :].rearrange("p (b c) -> p b c", b=4)

            def load_gate_up(g, q, n, part, k):
                free_nat(g, q, n)
                for hq in range(4):
                    src = part_rows[k % 2][bass.ds(part, 1), :, :, k // 2, hq, :].rearrange("a f b c -> (a f) b c")
                    sp.dma_start(nat_quadrant(hq, n), src).then_inc(nat_full[n % NAT_SLOTS], 32)

            def load_down(part):
                for fq in range(4):
                    sp.dma_start(nat_down[32 * fq:32 * fq + 32],
                                 down_rows[bass.ds(part, 1), fq].rearrange("a h b c -> (a h) b c"))\
                      .then_inc(nat_down_full, 16)

            def load_sign(g, i):
                n = NAT_SIGN + i
                free_nat(g, 0, n)
                for hq in range(4):
                    sp.dma_start(nat_quadrant(hq, n), sign_rows[6 + i, hq]).then_inc(nat_full[n % NAT_SLOTS], 32)

            def load_sign_part(g, q):
                sp.wait_ge(piece_turned, piece_number(g, q - 1, first_of("Sq") + 2))
                for hq in range(4):
                    sp.dma_start(nat_a[32 * hq:32 * hq + 32, 1], sign_rows[bass.ds(q, 1), hq].rearrange("a o b c -> (a o) b c"))\
                      .then_inc(nat_sign_full, 16)

            out_rows = out.rearrange("(n p) (a c) -> n p a c", p=P, a=2)

            def load_x(g, p, ahead=None):
                n = NAT_X + p
                if p == 3:
                    free_nat(g, 0, n)
                elif ahead is not None:
                    sp.wait_ge(piece_turned, piece_number(ahead, NQ - 1, first_of(("U1", "G2", "U2")[p]) + 2))
                sp.dma_start(nat[:, n % NAT_SLOTS, :], x_rows[bass.ds(4 * g + p, 1)].rearrange("a p c -> (a p) c"))\
                  .then_inc(nat_full[n % NAT_SLOTS], 128)

            def load_weight(g, u):
                n = NAT_W + u
                free_nat(g, 0, n)
                sp.dma_start(nat[:, n % NAT_SLOTS, :], scratch[u]).then_inc(nat_full[n % NAT_SLOTS], 128)

            def store(g):
                for o in range(8):
                    sp.wait_ge(out_added, START + 8 * g + o + 1)
                    sp.dma_start(out_rows[bass.ds(4 * g + o // 2, 1), :, o % 2, :].rearrange("a p c -> (a p) c"),
                                 out_sb[:, o % 2, :]).then_inc(out_stored[o % 2], 16)

            def group(g):
                free_nat(g, 0, NAT_REM)
                for t in range(2):
                    for hq in range(4):
                        sp.dma_start(nat_quadrant(hq, NAT_REM)[:, 2 * t:2 * t + 2, :], rest_rows[t][hq])\
                          .then_inc(nat_full[NAT_REM % NAT_SLOTS], 16)
                for fq in range(2):
                    sp.dma_start(nat_down[32 * fq:32 * fq + 32, :, 0:32], down_rest[fq]).then_inc(nat_down_full, 32)
                for i in range(2):
                    load_sign(g, i)
                for k in range(3):
                    load_gate_up(g, 0, NAT_GU + k, 0, k)
                sp.wait_ge(piece_turned, piece_number(g, 0, first_of("DREM") + 2))
                load_down(0)
                with sp.Fori(0, NQ - 1) as q:
                    load_sign_part(g, q)
                    for k in range(3, 6):
                        load_gate_up(g, q, NAT_GU + k, q, k)
                    for k in range(2):
                        load_gate_up(g, q, NAT_GU + PART_UNITS + k, q + 1, k)
                    sp.wait_ge(piece_turned, piece_number(g, q, first_of("D2") + 2))
                    load_down(q + 1)
                    load_gate_up(g, q, NAT_GU + PART_UNITS + 2, q + 1, 2)
                for k in range(3, 6):
                    load_gate_up(g, NQ - 1, NAT_GU + k, NQ - 1, k)

            sp.dma_start(act_f[:, 0:P], identity).then_inc(ident_in, 16)
            for p in range(3):
                load_x(0, p)
            load_x(0, 3)
            table_rows = fourier.rearrange("(p c) n -> p c n", c=KC)
            for c in range(0, KC, 2):
                sp.dma_start(table[:, c:c + 2], table_rows[:, c:c + 2]).then_inc(table_in, 16)
            load_base(0)
            load_base(1)
            constants()
            for u in range(2, KC):
                load_base(u)
            for semaphore in out_stored:
                sp.sem_inc(semaphore, 16 * START)
            for u in range(KC):
                sp.wait_ge(w_stored[u % BASE_SLOTS], 16 * (u // BASE_SLOTS + 1))
                load_weight(0, u)
            with sp.Fori(0, NG - 1) as g:
                group(g)
                for p in range(4):
                    load_x(g + 1, p, g)
                load_weight(g + 1, 0)
                load_weight(g + 1, 1)
                store(g)
                for u in range(2, KC):
                    load_weight(g + 1, u)
            group(NG - 1)
            store(NG - 1)
            for s in range(2):
                sp.wait_ge(out_stored[s], 16 * (START + 4 * NG))

        @block.gpsimd
        def _(pool):
            b_rows = [a[0, :, 0:FB, :].rearrange("a (q fq ff j) r -> q a ff fq (j r)", q=NQ, fq=4, j=PT)
                      for a in (B_gate, B_up)]
            b_rest = [a[0, :, FB:F, :].rearrange("a (fq ff) r -> a ff fq r", fq=2) for a in (B_gate, B_up)]
            ad_rows = A_down[0, :, :, 0:FB].rearrange("a r (q fq c) -> q a fq r c", q=NQ, fq=4)
            ad_rest = A_down[0, :, :, FB:F].rearrange("a r (fq c) -> a fq r c", fq=2)

            def chosen(table, g, b):
                return pool.value_load(table[:, bass.ds(GB * g + b, 1)], min_val=0, max_val=NAD - 1)

            def wait(semaphore, value):
                pool.wait_ge(semaphore, value)
                pool.sem_inc(pool_passed, 1)

            def load_cond(g, p):
                wait(mix_lo, START + 4 * g + max(0, p - 1))
                for b2 in range(2):
                    i = chosen(cond_index, g, 2 * p + b2)
                    pool.dma_start(nat_c[S * b2:S * b2 + S, p % 2, S * b2:S * b2 + S],
                                   cond_w[bass.ds(i, 1)].rearrange("a c d -> (a c) d")).then_inc(nat_c_full[p % 2], 16)

            def load_a(g, a, slot):
                for b in range(GB):
                    i = chosen(lora_index, g, b)
                    pool.dma_start(nat_a[b % 2::2, slot, b // 2, :],
                                   a[0, bass.ds(i, 1)].rearrange("a r (hq c) -> hq (a r) c", hq=4))\
                        .then_inc(nat_a_full[slot], 16)

            def load_b_down(g):
                slots = nat_a[:, 0].rearrange("p a c -> p (a c)").rearrange("p (n s r) -> p n s r", s=2, r=RANK)
                for b in range(GB):
                    i = chosen(lora_index, g, b)
                    pool.dma_start(slots[32 * (b // 2):32 * (b // 2) + 32, :, b % 2, :],
                                   B_down[0, bass.ds(i, 1)].rearrange("a (n h) r -> (a h) n r", h=32))\
                        .then_inc(nat_a_full[0], 16)

            def load_rest(g):
                for b in range(GB):
                    i = chosen(lora_index, g, b)
                    for t in range(2):
                        pool.dma_start(nat_b_rem[32 * (b // 2):32 * (b // 2) + 32, t, :, b % 2, :],
                                       b_rest[t][bass.ds(i, 1)].rearrange("a f b c -> (a f) b c"))\
                            .then_inc(nat_b_rem_full, 16)
                    pool.dma_start(nat_ad[b % 2:64:2, b // 2, 0:32],
                                   ad_rest[bass.ds(i, 1)].rearrange("a f r c -> (a f) r c")).then_inc(nat_ad_full, 16)

            def load_b(g, part):
                for b in range(GB):
                    i = chosen(lora_index, g, b)
                    for t in range(2):
                        pool.dma_start(nat_b[32 * (b // 2):32 * (b // 2) + 32, t, :, b % 2, :],
                                       b_rows[t][bass.ds(part, 1), bass.ds(i, 1)].rearrange("q a f b c -> (q a f) b c"))\
                            .then_inc(nat_b_full, 16)

            def load_ad(g, part):
                for b in range(GB):
                    i = chosen(lora_index, g, b)
                    pool.dma_start(nat_ad[b % 2::2, b // 2, :],
                                   ad_rows[bass.ds(part, 1), bass.ds(i, 1)].rearrange("q a f r c -> (q a f) r c"))\
                        .then_inc(nat_ad_full, 16)

            def wait_turned(g, q, name, pieces):
                wait(piece_turned, piece_number(g, q, first_of(name) + pieces))

            def group(g):
                wait(piece_lo, START + LOW_PIECES * g)
                load_a(g, A_gate, 0)
                load_a(g, A_up, 1)
                load_rest(g)
                load_b(g, 0)
                wait_turned(g, 0, "AG", 2)
                load_b_down(g)
                wait_turned(g, 0, "ADREM", 1)
                load_ad(g, 0)
                with pool.Fori(0, NQ - 1) as q:
                    wait_turned(g, q - 1, "nextB", 3)
                    load_b(g, q + 1)
                    wait_turned(g, q, "AD", 1)
                    load_ad(g, q + 1)

            pool.wait_ge(const_set, 1)
            for p in range(4):
                load_cond(0, p)
            with pool.Fori(0, NG - 1) as g:
                group(g)
                for p in range(4):
                    load_cond(g + 1, p)
            group(NG - 1)

        def bank_of(c):
            return ps[:, T_BANK + c % 2, :]

        def weight_bank(u, half):
            return (6 + 2 * u + half) % 8

        def tiled(i, dst, src, *hi):
            if i >= 4:
                return (dst, src, *hi)
            dst, *hi = (v.rearrange("p (k q t) -> p q k t", q=4, k=KC) for v in (dst, *hi))
            return (dst, src.rearrange("p (q k t) -> p q k t", q=4, k=KC), *hi)

        def sign_target(u, half):
            return signs[:, 4 * half:4 * half + 4, bass.ds(P * u, P)]

        @block.scalar
        def _(act):
            def copy(dst, src):
                return act.activation(dst, src, ACT.Copy)

            def slot_read(g, q, m):
                if m < 3:
                    act.wait_ge(down_psum, START + DOWNS * g)
                elif m < SPLIT_W + 3:
                    act.wait_ge(mixed_psum, START + 8 * g + 2 * (m - 3) + 2)
                elif m < SPLIT_AG + 3:
                    act.wait_ge(x1_psum, 8 * g + m - 3 - SPLIT_W + 1)
                elif m < SPLIT_REM + 3:
                    act.wait_ge(rank_psum, 2 * g + m - 3 - SPLIT_AG + 1)
                elif m == SPLIT_REM + 3:
                    act.wait_ge(rest_psum, g + 1)
                else:
                    k = m - 3 - SPLIT_GU
                    act.wait_ge(up_psum if k % 2 else gate_psum, (START if k % 2 else 0) + TILES * g + PT * q + k // 2 + 1)

            def plain_unit(g, i, n, m):
                act.wait_ge(nat_full[n % NAT_SLOTS], nat_filled(g, 0, n))
                slot_read(g, 0, m)
                copy(*tiled(i, split[:, m % SPLIT_SLOTS, 0, :], nat[:, n % NAT_SLOTS, :])).then_inc(plain_hi, 1)

            def piece(g, q, c, dst, src, func=ACT.Copy):
                act.wait_ge(piece_turned, piece_number(g, q, c) + 1)
                act.activation(dst, src, func).then_inc(piece_hi, 1)

            def unit(g, q, name, m):
                c = first_of(name)
                slot_read(g, q, m)
                for half in range(2):
                    piece(g, q, c + half, split[:, m % SPLIT_SLOTS, 0, 512 * half:512 * half + 512], bank_of(c + half))

            def sign_unit(g, q, name, u):
                c = first_of(name)
                for half in range(2):
                    piece(g, q, c + half, sign_target(u, half),
                          bank_of(c + half).rearrange("p (m o) -> p m o", m=4), ACT.Sign)

            def down_tile(g, q, j):
                c = first_of(f"D{j}")
                act.wait_ge(down_psum, START + DOWNS * g + 9 * (q + 1))
                for half in range(2):
                    piece(g, q, c + half, down_w[:, 0, j, 4 * half:4 * half + 4, :],
                          bank_of(c + half).rearrange("p (m h) -> p m h", m=4))

            def lora_b_tiles(g, q, name, part):
                c = first_of(name)
                act.wait_ge(up_psum, START + TILES * g + PT * part)
                for j in range(PT):
                    piece(g, q, c + j, lora_b[:, 0, j].rearrange("p t f -> p (t f)"), bank_of(c + j)[:, 0:256])

            def cond(g, p):
                act.wait_ge(nat_c_full[p % 2], 32 * (2 * g + p // 2 + 1))
                act.wait_ge(mixed_psum, START + 8 * g + max(0, 2 * p - 2))
                copy(mix[:, p % 2, 0, :], nat_c[:, p % 2, :]).then_inc(mix_hi, 1)

            def mixing(g, e):
                p, kh = e // 2, e % 2
                b0, b1 = S1_BANKS[e % 3]
                src = ps[:, b0:b1, :].rearrange("p a (k n t) -> p (a k) n t", k=2, n=2)
                act.wait_ge(mixed_psum, START + 8 * g + e + 1)
                copy(acc[:, 4 * kh:4 * kh + 4, P * p:P * p + P], src[:, :, 1, :]).then_inc(xt_copied, 1)
                copy(mixed[:, 0, 4 * kh:4 * kh + 4, P * p:P * p + P], src[:, :, 0, :]).then_inc(mixed_hi, 1)

            def x1_tile(g, u):
                act.wait_ge(x1_sum, 8 * g + u + 1)
                copy(x1[:, 0, u, :], acc[:, u, :]).then_inc(x1_hi, 1)

            def rank(g, n):
                act.wait_ge(rank_sum, 3 * g + n + 1)
                if n == 2:
                    act.wait_ge(up_psum, START + TILES * (g + 1))
                copy(lora_t[:, n % 2, 0, :], act_f[:]).then_inc(rank_hi, 1)

            def act_rest(g):
                act.wait_ge(up_read, START + ACTS * g)
                act.wait_ge(rest_psum, g + 1)
                act.activation(gated[0:64, :], ps[0:64, 1, :], ACT.Silu).then_inc(gate_read, 1)
                act.wait_ge(rank_lo, START + 3 * g + 2)
                copy(act_f[0:64, :], ps[64:128, 1, :]).then_inc(rest_moved, 1)
                act.wait_ge(up_read, START + ACTS * g + 1)
                copy(acts[0:64, 0, 0, :], act_f[0:64, :]).then_inc(act_hi, 1)

            def act_tile(g, q, j):
                act.wait_ge(up_read, START + ACTS * g + PT * q + j + 1)
                act.wait_ge(gate_psum, TILES * g + PT * q + j + 1)
                act.activation(gated[:], ps[:, 2 * j % 3, :], ACT.Silu).then_inc(gate_read, 1)
                act.wait_ge(up_read, START + ACTS * g + PT * q + j + 2)
                copy(acts[:, 0, j, :], act_f[:]).then_inc(act_hi, 1)

            def part(g, q, last):
                down_tile(g, q, 0)
                unit(g, q, "U1", SPLIT_GU + 3)
                act_tile(g, q, 0)
                unit(g, q, "G2", SPLIT_GU + 4)
                down_tile(g, q, 1)
                unit(g, q, "U2", SPLIT_GU + 5)
                act_tile(g, q, 1)
                down_tile(g, q, 2)
                c = first_of("AD")
                piece(g, q, c, lora_ad[:, 0].rearrange("p j a -> p (j a)"), bank_of(c)[:, 0:PT * P])
                if last:
                    unit(g, q, "BD", SPLIT_BD - PART_UNITS * q)
                    act_tile(g, q, 2)
                    return
                sign_unit(g, q, "Sq", q)
                unit(g, q, "nextG0", SPLIT_GU + 6)
                act_tile(g, q, 2)
                lora_b_tiles(g, q, "nextB", q + 1)
                unit(g, q, "nextU0", SPLIT_GU + 7)
                unit(g, q, "nextG1", SPLIT_GU + 8)

            def mixing_ahead(g):
                for p in range(3):
                    plain_unit(g, p, NAT_X + p, SPLIT_X + p)
                    if p < 2:
                        cond(g, p)

            def weight_unit(g, u):
                plain_unit(g, 4 + u, NAT_W + u, SPLIT_W + u)

            def mixing_all(g, weights):
                for e in range(8):
                    mixing(g, e)
                    if e == 1:
                        plain_unit(g, 3, NAT_X + 3, SPLIT_X + 3)
                        cond(g, 2)
                    if e == 3:
                        cond(g, 3)
                    if weights and e in (3, 5, 7):
                        weight_unit(g, e // 2 - 1)

            def group(g, last):
                for u in range(KC):
                    x1_tile(g, u)
                    if u < 5:
                        weight_unit(g, 3 + u)
                    else:
                        unit(g, 0, ("AG", "AU", "REM")[u - 5], SPLIT_W + 3 + u)
                c = first_of("BREM")
                act.wait_ge(out_psum, START + 8 * g)
                piece(g, 0, c, lora_b_rem[:, 0].rearrange("p t (n f) -> p (t n) f", n=2)[:, 0::3, :],
                      bank_of(c)[:, 0:P].rearrange("p (t f) -> p t f", t=2))
                act.wait_ge(x1_psum, 8 * g + KC)
                sign_unit(g, 0, "S6", 6)
                rank(g, 0)
                sign_unit(g, 0, "S7", 7)
                rank(g, 1)
                unit(g, 0, "G0", SPLIT_GU)
                c = first_of("DREM")
                for half in range(2):
                    piece(g, 0, c + half, down_w[0:64, 0, 0, 4 * half:4 * half + 4, :],
                          bank_of(c + half)[0:64].rearrange("p (m h) -> p m h", m=4))
                c = first_of("ADREM")
                piece(g, 0, c, lora_ad[0:64, 0, 0, :], bank_of(c)[0:64, 0:P])
                act_rest(g)
                lora_b_tiles(g, 0, "B", 0)
                unit(g, 0, "U0", SPLIT_GU + 1)
                unit(g, 0, "G1", SPLIT_GU + 2)
                with act.Fori(0, NQ - 1) as q:
                    part(g, q, False)
                part(g, NQ - 1, True)
                rank(g, 2)
                act.wait_ge(down_psum, START + DOWNS * (g + 1))
                for m in range(KC):
                    act.wait_ge(down_added, DOWNS * g + 9 * NQ + DOWN_ORDER.index(m) + 1)
                    copy(down[:, 0, m, :], acc[:, m, :]).then_inc(down_hi, 1)
                if not last:
                    mixing_ahead(g + 1)
                    mixing_all(g + 1, True)

            for i in range(2):
                act.dma_start(coef[i], coefs[i].rearrange("e (p c) r -> p e (c r)", c=KC)).then_inc(coef_in, 16)
                act.dma_start(coef_mask[i][:], masks[i].rearrange("e (p c) r -> p e (c r)", c=KC)).then_inc(coef_in, 16)
            act.dma_start(enc[0:R0, :], enc0).then_inc(enc_in, 16)
            act.dma_start(enc[R0:RL, :], enc1).then_inc(enc_in, 16)
            mixing_ahead(0)
            mixing_all(0, False)
            for u in range(KC):
                act.wait_ge(w_added, 2 * u + 2)
                act.dma_start(scratch[u], base_t[:, u % BASE_SLOTS]).then_inc(w_stored[u % BASE_SLOTS], 16)
                if u >= 5:
                    weight_unit(0, u - 5)
            with act.Fori(0, NG - 1) as g:
                group(g, False)
            group(NG - 1, True)

        @block.vector
        def _(dve):
            def lo(dst, full, hi):
                return dve.tensor_tensor(dst, full, hi.bitcast(F32), ALU.subtract)

            def plain_unit(g, i, n, m):
                s = m % SPLIT_SLOTS
                dve.wait_ge(plain_hi, 12 * g + i + 1)
                lo(*tiled(i, split[:, s, 1, :], nat[:, n % NAT_SLOTS, :], split[:, s, 0, :])).then_inc(plain_lo, 1)

            def turn(g, q, c, dst, src):
                if c < 2:
                    dve.wait_ge(piece_lo, START + LOW_PIECES * g)
                else:
                    dve.wait_ge(piece_hi, piece_number(g, q, c - 1))
                    dve.wait_ge(piece_lo, START + low_number(g, q, c - 1))
                dve.transpose(dst, src).then_inc(piece_turned, 1)

            def piece_low(g, q, c, dst, src, hi):
                dve.wait_ge(piece_hi, piece_number(g, q, c) + 1)
                lo(dst, src, hi).then_inc(piece_lo, 1)

            def turn_unit(g, q, c, rows):
                for half in range(2):
                    turn(g, q, c + half, bank_of(c + half).rearrange("p (k b h) -> p k b h", k=4, b=4),
                         rows.rearrange("p (b k h) -> p k b h", b=4, k=KC)[:, 4 * half:4 * half + 4])

            def unit_lows(g, q, c, m):
                s = m % SPLIT_SLOTS
                for half in range(2):
                    cols = slice(512 * half, 512 * half + 512)
                    piece_low(g, q, c + half, split[:, s, 1, cols], bank_of(c + half), split[:, s, 0, cols])

            def weight_unit(g, q, name, n, m):
                dve.wait_ge(nat_full[n % NAT_SLOTS], nat_filled(g, q, n))
                c = first_of(name)
                turn_unit(g, q, c, nat[:, n % NAT_SLOTS, :])
                unit_lows(g, q, c, m)

            def adapter_unit(g, name, fill, m):
                dve.wait_ge(nat_a_full[fill], 128 * ((2, 1)[fill] * g + 1))
                c = first_of(name)
                turn_unit(g, 0, c, nat_a[:, fill].rearrange("p b c -> p (b c)"))
                unit_lows(g, 0, c, m)

            def b_down_unit(g, q, m):
                dve.wait_ge(nat_a_full[0], 128 * (2 * g + 2))
                c = first_of("BD")
                rows = nat_a[:, 0].rearrange("p a c -> p (a c)").rearrange("p (q m s r) -> p m q r s", q=4, m=KC, s=2)
                for half in range(2):
                    if c + half >= 2:
                        dve.wait_ge(piece_hi, piece_number(g, q, c + half - 1))
                        dve.wait_ge(piece_lo, START + low_number(g, q, c + half - 1))
                    for m4 in range(4):
                        for hq in range(4):
                            t = dve.transpose(bank_of(c + half)[:, P * m4 + 32 * hq:P * m4 + 32 * hq + 32],
                                              rows[:, 4 * half + m4, hq])
                    t.then_inc(piece_turned, 1)
                unit_lows(g, q, c, m)

            def sign_unit(g, i):
                n = NAT_SIGN + i
                dve.wait_ge(nat_full[n % NAT_SLOTS], nat_filled(g, 0, n))
                turn_unit(g, 0, first_of(f"S{6 + i}"), nat[:, n % NAT_SLOTS, :])

            def sign_part(g, q):
                dve.wait_ge(nat_sign_full, 64 * ((NQ - 1) * g + q + 1))
                turn_unit(g, q, first_of("Sq"), nat_a[:, 1].rearrange("p b c -> p (b c)"))

            def down_tile(g, q, j):
                c = first_of(f"D{j}")
                dve.wait_ge(nat_down_full, 64 * (8 * g + q + 2))
                rows = nat_down[:].rearrange("p (q m) (f j) -> p m q f j", q=4, j=PT)
                for half in range(2):
                    turn(g, q, c + half, bank_of(c + half).rearrange("p (m q h) -> p m q h", m=4, q=4),
                         rows[:, 4 * half:4 * half + 4, :, :, j])
                for half in range(2):
                    ms = slice(4 * half, 4 * half + 4)
                    piece_low(g, q, c + half, down_w[:, 1, j, ms, :], bank_of(c + half).rearrange("p (m h) -> p m h", m=4),
                              down_w[:, 0, j, ms, :])

            def down_rest(g):
                c = first_of("DREM")
                dve.wait_ge(nat_down_full, 64 * (8 * g + 1))
                rows = nat_down[0:64, :, 0:32].rearrange("p (q m) f -> p m q f", q=4)
                for half in range(2):
                    turn(g, 0, c + half, bank_of(c + half)[0:64].rearrange("p (m q h) -> p m q h", m=4, q=4),
                         rows[:, 4 * half:4 * half + 4])
                for half in range(2):
                    ms = slice(4 * half, 4 * half + 4)
                    piece_low(g, 0, c + half, down_w[0:64, 1, 0, ms, :],
                              bank_of(c + half)[0:64].rearrange("p (m h) -> p m h", m=4), down_w[0:64, 0, 0, ms, :])

            def a_down_rest(g):
                c = first_of("ADREM")
                dve.wait_ge(nat_ad_full, 128 * (8 * g + 1))
                turn(g, 0, c, bank_of(c)[0:64, 0:P].rearrange("p (b a) -> p b a", b=4), nat_ad[0:64, :, 0:32])
                piece_low(g, 0, c, lora_ad[0:64, 1, 0, :], bank_of(c)[0:64, 0:P], lora_ad[0:64, 0, 0, :])

            def a_down_tiles(g, q):
                c = first_of("AD")
                dve.wait_ge(nat_ad_full, 128 * (8 * g + q + 2))
                turn(g, q, c, bank_of(c)[:, 0:PT * P].rearrange("p (j b a) -> p j b a", j=PT, b=4),
                     nat_ad[:].rearrange("p b (f j) -> p j b f", j=PT))
                piece_low(g, q, c, lora_ad[:, 1].rearrange("p j a -> p (j a)"), bank_of(c)[:, 0:PT * P],
                          lora_ad[:, 0].rearrange("p j a -> p (j a)"))

            def lora_b_tiles(g, q, name, part):
                c = first_of(name)
                dve.wait_ge(nat_b_full, 256 * (NQ * g + part + 1))
                rows = nat_b[:].rearrange("p t fq s (j r) -> p j (t fq) r s", j=PT)
                for j in range(PT):
                    turn(g, q, c + j, bank_of(c + j)[:, 0:256].rearrange("p (n r s) -> p n r s", n=8, r=RANK), rows[:, j])
                    piece_low(g, q, c + j, lora_b[:, 1, j].rearrange("p t f -> p (t f)"), bank_of(c + j)[:, 0:256],
                              lora_b[:, 0, j].rearrange("p t f -> p (t f)"))

            def lora_b_rest(g):
                c = first_of("BREM")
                dve.wait_ge(nat_b_rem_full, 256 * (g + 1))
                turn(g, 0, c, bank_of(c)[:, 0:P].rearrange("p (n r s) -> p n r s", n=4, r=RANK),
                     nat_b_rem[:].rearrange("p t fq s r -> p (t fq) r s"))
                halves = [lora_b_rem[:, s].rearrange("p t (n f) -> p (t n) f", n=2)[:, 0::3, :] for s in range(2)]
                piece_low(g, 0, c, halves[1], bank_of(c)[:, 0:P].rearrange("p (t f) -> p t f", t=2), halves[0])

            def cond(g, p):
                dve.wait_ge(mix_hi, 4 * g + p + 1)
                lo(mix[:, p % 2, 2, :], nat_c[:, p % 2, :], mix[:, p % 2, 0, :]).then_inc(mix_lo, 1)

            def mixing(g, e):
                p, kh = e // 2, e % 2
                b0, b1 = S1_BANKS[e % 3]
                src = ps[:, b0:b1, :].rearrange("p a (k n t) -> p (a k) n t", k=2, n=2)[:, :, 0, :]
                at = (slice(4 * kh, 4 * kh + 4), slice(P * p, P * p + P))
                dve.wait_ge(mixed_hi, 8 * g + e + 1)
                lo(mixed[:, 1, at[0], at[1]], src, mixed[:, 0, at[0], at[1]]).then_inc(mixed_lo, 1)

            def x1_total(g, u):
                dve.wait_ge(x1_psum, 8 * g + u + 1)
                dve.wait_ge(xt_copied, 8 * g + 8)
                dve.scalar_tensor_tensor(out=acc[:, u, :], in0=ps[:, X1_BANKS[u], :], scalar=b_col[:, u:u + 1],
                                         in1=acc[:, u, :], op0=ALU.add, op1=ALU.add).then_inc(x1_sum, 1)

            def x1_low(g, u):
                dve.wait_ge(x1_hi, 8 * g + u + 1)
                lo(x1[:, 1, u, :], acc[:, u, :], x1[:, 0, u, :]).then_inc(x1_lo, 1)

            def rank(g, n):
                if n < 2:
                    dve.wait_ge(rank_psum, 2 * g + n + 1)
                    src = ps[:, (2, 0)[n], :]
                else:
                    dve.wait_ge(down_added, DOWNS * g + 9 * NQ + 1)
                    src = acc[:, 8, :]
                dve.wait_ge(rank_lo, START + 3 * g + n)
                dve.wait_ge(act_lo, START + ACTS * g + (ACTS if n == 2 else 0))
                dve.tensor_tensor(act_f[:], src, own_sb[:], ALU.mult).then_inc(rank_sum, 1)
                dve.wait_ge(rank_hi, 3 * g + n + 1)
                lo(lora_t[:, n % 2, 1, :], act_f[:], lora_t[:, n % 2, 0, :]).then_inc(rank_lo, 1)

            def act_rest(g):
                dve.wait_ge(rest_moved, g + 1)
                dve.tensor_tensor(act_f[0:64, :], gated[0:64, :], act_f[0:64, :], ALU.mult).then_inc(up_read, 1)
                dve.wait_ge(act_hi, ACTS * g + 1)
                lo(acts[0:64, 1, 0, :], act_f[0:64, :], acts[0:64, 0, 0, :]).then_inc(act_lo, 1)

            def act_tile(g, q, j):
                n = ACTS * g + PT * q + j + 1
                dve.wait_ge(up_psum, START + TILES * g + PT * q + j + 1)
                dve.wait_ge(gate_read, n + 1)
                dve.wait_ge(act_lo, START + n)
                dve.tensor_tensor(act_f[:], ps[:, (2 * j + 1) % 3, :], gated[:], ALU.mult).then_inc(up_read, 1)
                dve.wait_ge(act_hi, n + 1)
                lo(acts[:, 1, j, :], act_f[:], acts[:, 0, j, :]).then_inc(act_lo, 1)

            def down_add(g, stage, i):
                n = DOWNS * g + 9 * stage + i + 1
                m = DOWN_ORDER[i]
                dve.wait_ge(down_psum, START + n)
                src = ps[:, D_BANK + i % 3, :]
                if isinstance(stage, int) and stage == 0:
                    dve.wait_ge(x1_lo, 8 * g + KC)
                    dve.wait_ge(rank_lo, START + 3 * g)
                    dve.tensor_copy(acc[:, m, :], src).then_inc(down_added, 1)
                else:
                    dve.wait_ge(down_added, n - 9)
                    dve.tensor_tensor(acc[:, m, :], src, acc[:, m, :], ALU.add).then_inc(down_added, 1)

            def down_low(g, m):
                dve.wait_ge(down_hi, 8 * g + m + 1)
                lo(down[:, 1, m, :], acc[:, m, :], down[:, 0, m, :]).then_inc(down_lo, 1)

            def part(g, q, last):
                down_tile(g, q, 0)
                weight_unit(g, q, "U1", NAT_GU + 3, SPLIT_GU + 3)
                act_tile(g, q, 0)
                weight_unit(g, q, "G2", NAT_GU + 4, SPLIT_GU + 4)
                down_tile(g, q, 1)
                weight_unit(g, q, "U2", NAT_GU + 5, SPLIT_GU + 5)
                act_tile(g, q, 1)
                down_tile(g, q, 2)
                a_down_tiles(g, q)
                if last:
                    b_down_unit(g, q, SPLIT_BD)
                    act_tile(g, q, 2)
                    down_add(g, q + 1, 0)
                    rank(g, 2)
                    for i in range(1, 9):
                        down_add(g, q + 1, i)
                    return
                sign_part(g, q)
                weight_unit(g, q, "nextG0", NAT_GU + 6, SPLIT_GU + 6)
                act_tile(g, q, 2)
                lora_b_tiles(g, q, "nextB", q + 1)
                weight_unit(g, q, "nextU0", NAT_GU + 7, SPLIT_GU + 7)
                for i in range(3):
                    down_add(g, q + 1, i)
                weight_unit(g, q, "nextG1", NAT_GU + 8, SPLIT_GU + 8)
                for i in range(3, 9):
                    down_add(g, q + 1, i)

            def mixing_ahead(g):
                for p in range(3):
                    plain_unit(g, p, NAT_X + p, SPLIT_X + p)
                    if p < 2:
                        cond(g, p)

            def first_weight_unit(g, u):
                plain_unit(g, 4 + u, NAT_W + u, SPLIT_W + u)

            def mixing_all(g, weights):
                for e in range(8):
                    mixing(g, e)
                    if e == 1:
                        plain_unit(g, 3, NAT_X + 3, SPLIT_X + 3)
                        cond(g, 2)
                    if e == 3:
                        cond(g, 3)
                    if weights and e in (3, 5, 7):
                        first_weight_unit(g, e // 2 - 1)

            def adapter_sum():
                dve.wait_ge(coef_in, 64)
                for i in range(2):
                    dve.tensor_tensor(kept[i], coef[i], coef_mask[i][:], ALU.mult).then_inc(kept_step, 1)
                for i in range(2):
                    dve.wait_ge(kept_step, i + 1)
                    dve.tensor_tensor(coef[i][:, 0], kept[i][:, 0], kept[i][:, 1], ALU.add).then_inc(kept_step, 1)
                for i in range(2):
                    dve.wait_ge(kept_step, i + 3)
                    dve.tensor_tensor(coef[i][:, 1], coef[i][:, 0], kept[i][:, 2], ALU.add).then_inc(kept_step, 1)
                for i, (r0, r1) in enumerate(((0, R0), (R0, RL))):
                    dve.wait_ge(kept_step, i + 5)
                    dve.tensor_scalar(wsum[:, :, r0:r1], coef[i][:, 1].rearrange("p (c r) -> p c r", c=KC), 0.5, None,
                                      ALU.mult).then_inc(wsum_done, 1)

            def turn_base(u):
                dve.wait_ge(base_in[u % 2], 64 * (u // 2 + 1))
                if u >= BASE_SLOTS:
                    dve.wait_ge(w_stored[u % BASE_SLOTS], 16 * (u // BASE_SLOTS))
                dve.transpose(base_t[:, u % BASE_SLOTS].rearrange("p (k b h) -> p k b h", k=KC, b=4),
                              base[:, u % 2].rearrange("p b (k h) -> p k b h", k=KC)).then_inc(base_turned, 1)

            def effective_weight():
                for u in range(BASE_SLOTS):
                    turn_base(u)
                dve.wait_ge(enc_in, 32)
                dve.tensor_copy(enc_tiles.rearrange("r k (q d) -> r k q d", q=4),
                                enc.rearrange("r (q k d) -> r k q d", q=4, k=KC)).then_inc(g_read, 1)
                dve.wait_ge(g_psum, 1)
                dve.tensor_copy(low_rank, ps[0:RL, 6:8, :].rearrange("p a n -> p (a n)")).then_inc(g_read, 1)
                for u in range(KC):
                    dve.wait_ge(base_turned, u + 1)
                    for half in range(2):
                        part_t = base_t[:, u % BASE_SLOTS, 512 * half:512 * half + 512]
                        dve.wait_ge(w_psum, 2 * u + half + 1)
                        dve.tensor_tensor(part_t, ps[:, weight_bank(u, half), :], part_t, ALU.add).then_inc(w_added, 1)
                    if 1 <= u < KC - 3:
                        turn_base(u + 3)
                    if u >= 5:
                        first_weight_unit(0, u - 5)

            def group(g, last):
                for u in range(KC):
                    x1_total(g, u)
                    if u < 5:
                        first_weight_unit(g, 3 + u)
                    elif u == 5:
                        dve.wait_ge(x1_sum, 8 * g + 2)
                        adapter_unit(g, "AG", 0, SPLIT_AG)
                    elif u == 6:
                        adapter_unit(g, "AU", 1, SPLIT_AU)
                    else:
                        weight_unit(g, 0, "REM", NAT_REM, SPLIT_REM)
                    x1_low(g, u)
                lora_b_rest(g)
                sign_unit(g, 0)
                rank(g, 0)
                sign_unit(g, 1)
                rank(g, 1)
                weight_unit(g, 0, "G0", NAT_GU, SPLIT_GU)
                down_rest(g)
                a_down_rest(g)
                act_rest(g)
                lora_b_tiles(g, 0, "B", 0)
                for i in range(3):
                    down_add(g, 0, i)
                weight_unit(g, 0, "U0", NAT_GU + 1, SPLIT_GU + 1)
                for i in range(3, 9):
                    down_add(g, 0, i)
                weight_unit(g, 0, "G1", NAT_GU + 2, SPLIT_GU + 2)
                with dve.Fori(0, NQ - 1) as q:
                    part(g, q, False)
                part(g, NQ - 1, True)
                for m in range(KC):
                    down_low(g, m)
                if not last:
                    mixing_ahead(g + 1)
                for o in range(8):
                    dve.wait_ge(out_psum, START + 8 * g + o + 1)
                    dve.wait_ge(out_stored[o % 2], 16 * (START + 4 * g + o // 2))
                    h = o % 2
                    dve.tensor_tensor(out_sb[:, h, :], ps[:, OUT_BANKS[o], :], bias_sb[:, 512 * h:512 * h + 512],
                                      ALU.add).then_inc(out_added, 1)
                if not last:
                    mixing_all(g + 1, True)

            dve.memset(nat_c[:], 0.0).then_inc(const_set, 1)
            dve.memset(lora_b_rem[:].bitcast(F32), 0.0).then_inc(const_set, 1)
            dve.wait_ge(ident_in, 16)
            dve.tensor_copy(ident[:], act_f[:, 0:P]).then_inc(const_set, 1)
            for s in range(2):
                dve.tensor_copy(mix[:, s, 1, :], act_f[:, 0:P]).then_inc(const_set, 1)
            dve.wait_ge(const_set, CONSTS)
            for semaphore in (piece_lo, mix_lo, up_read, out_added, rank_lo, act_lo):
                dve.sem_inc(semaphore, START)
            mixing_ahead(0)
            adapter_sum()
            mixing_all(0, False)
            effective_weight()
            dve.wait_ge(const_in, 16 * 6)
            with dve.Fori(0, NG - 1) as g:
                group(g, False)
            group(NG - 1, True)

        @block.tensor
        def _(pe):
            def product(dst, a, b, first, last):
                pe.matmul(dst, a[0], b[0], start=first, stop=False)
                pe.matmul(dst, a[0], b[1], start=False, stop=False)
                return pe.matmul(dst, a[1], b[0], start=False, stop=last)

            def stationary(m, k):
                return [split[:, m % SPLIT_SLOTS, s, P * k:P * k + P] for s in range(2)]

            def mixing(g, e, before):
                p, kh = e // 2, e % 2
                if kh == 0:
                    pe.wait_ge(plain_lo, 12 * g + p + 1)
                    pe.wait_ge(mix_lo, START + 4 * g + p + 1)
                if e < 3:
                    if before is not None:
                        pe.wait_ge(out_added, START + 8 * before + (2, 6, 8)[e])
                else:
                    pe.wait_ge(mixed_lo, 8 * g + e - 2)
                    pe.wait_ge(xt_copied, 8 * g + e - 2)
                for k in range(4):
                    bank = S1_BANKS[e % 3][0] + k // 2
                    dst = ps[:, bank, 256 * (k % 2):256 * (k % 2) + 256]
                    xs = stationary(SPLIT_X + p, 4 * kh + k)
                    both = mix[:, p % 2, 0:2, :].rearrange("p n t -> p (n t)")
                    pe.matmul(dst, xs[0], both, start=True, stop=False)
                    pe.matmul(dst[:, 0:P], xs[0], mix[:, p % 2, 2, :], start=False, stop=False)
                    mm = pe.matmul(dst, xs[1], both, start=False, stop=True)
                mm.then_inc(mixed_psum, 1)

            def first_layer(g, u, half=None):
                m = SPLIT_W + u
                pe.wait_ge(plain_lo, 12 * g + 4 + u + 1)
                if half == 0:
                    pe.wait_ge(mixed_lo, 8 * g + 4)
                if u >= 5:
                    pe.wait_ge(x1_sum, 8 * g + u - 2)
                t = slice(0, G) if half is None else slice(256 * half, 256 * half + 256)
                for k in range(KC):
                    if half == 1 and k % 4 == 0:
                        pe.wait_ge(mixed_lo, 8 * g + 7 + k // 4)
                        pe.wait_ge(xt_copied, 8 * g + 7 + k // 4)
                    mm = product(ps[:, X1_BANKS[u], t], stationary(m, k), [mixed[:, s, k, t] for s in range(2)],
                                 k == 0, k == KC - 1)
                if half != 0:
                    mm.then_inc(x1_psum, 1)

            def wait_unit(g, q, name):
                pe.wait_ge(piece_lo, START + low_number(g, q, first_of(name) + 2))

            def of_x1(dst, m, last, wait=lambda k: None):
                for k in range(KC):
                    wait(k)
                    mm = product(dst, stationary(m, k), [x1[:, s, k, :] for s in range(2)], k == 0, last and k == KC - 1)
                return mm

            def rank(g, n):
                wait_unit(g, 0, ("AG", "AU")[n])
                pe.wait_ge(x1_sum, 8 * g + (6, 7)[n])
                of_x1(ps[:, (2, 0)[n], :], SPLIT_AG + n, True, lambda k: pe.wait_ge(x1_lo, 8 * g + k + 1))\
                    .then_inc(rank_psum, 1)

            def gate_up_rest(g):
                wait_unit(g, 0, "REM")
                pe.wait_ge(x1_sum, 8 * g + 8)
                of_x1(ps[:, 1, :], SPLIT_REM, False)
                pe.wait_ge(piece_lo, START + low_number(g, 0, first_of("BREM") + 1))
                pe.wait_ge(rank_lo, START + 3 * g + 2)
                for t in range(2):
                    mm = product(ps[:, 1, :], [lora_b_rem[:, s, t, :] for s in range(2)],
                                 [lora_t[:, t, s, :] for s in range(2)], False, t == 1)
                mm.then_inc(rest_psum, 1)

            def down_rest(g):
                pe.wait_ge(piece_lo, START + low_number(g, 0, first_of("ADREM") + 1))
                pe.wait_ge(act_lo, START + ACTS * g + 1)
                for i in range(9):
                    m = DOWN_ORDER[i]
                    if i >= 3:
                        pe.wait_ge(down_added, DOWNS * g + i - 2)
                    w = [(down_w[0:64, s, 0, m, :] if m < KC else lora_ad[0:64, s, 0, :]) for s in range(2)]
                    product(ps[:, D_BANK + i % 3, :], w, [acts[0:64, s, 0, :] for s in range(2)], True, True)\
                        .then_inc(down_psum, 1)

            def gate_up_weight(g, q, k, name, in_part):
                t, j = k % 2, k // 2
                pe.wait_ge(piece_lo, START + low_number(g, in_part, first_of(name) + 2))
                if t == 0:
                    pe.wait_ge(up_read, START + ACTS * g + PT * q + j)
                else:
                    pe.wait_ge(gate_read, ACTS * g + PT * q + j + 1)
                of_x1(ps[:, k % 3, :], SPLIT_GU + k, False)

            def gate_up_adapter(g, q, k):
                t, j = k % 2, k // 2
                if k == 0:
                    pe.wait_ge(piece_lo, START + low_number(g, q - 1, first_of("nextB") + 3))
                product(ps[:, k % 3, :], [lora_b[:, s, j, t, :] for s in range(2)], [lora_t[:, t, s, :] for s in range(2)],
                        False, True).then_inc(up_psum if t else gate_psum, 1)

            def part_gate_up(g, q):
                gate_up_adapter(g, q, 0)
                for k, name in enumerate(("nextU0", "nextG1", "U1", "G2", "U2"), 1):
                    gate_up_weight(g, q, k, name, q if k > 2 else q - 1)
                    gate_up_adapter(g, q, k)

            def down_part(g, q, last):
                pe.wait_ge(piece_lo, START + low_number(g, q, first_of("AD") + 1))

                def tiles(i, js, stop=True):
                    m = DOWN_ORDER[i]
                    for j in js:
                        w = [(down_w[:, s, j, m, :] if m < KC else lora_ad[:, s, j, :]) for s in range(2)]
                        mm = product(ps[:, D_BANK + i % 3, :], w, [acts[:, s, j, :] for s in range(2)],
                                     j == 0, stop and j == PT - 1)
                    return mm

                def adapter(i):
                    product(ps[:, D_BANK + i % 3, :], stationary(SPLIT_BD, DOWN_ORDER[i]),
                            [lora_t[:, 0, s, :] for s in range(2)], False, True).then_inc(down_psum, 1)

                def bank_read(i):
                    pe.wait_ge(down_added, DOWNS * g + 9 * (q + 1) + i - 2)

                pe.wait_ge(act_lo, START + ACTS * g + PT * q + 3)
                for i in range(3):
                    bank_read(i)
                    tiles(i, (0, 1))
                pe.wait_ge(act_lo, START + ACTS * g + PT * q + 4)
                if not last:
                    for i in range(3):
                        tiles(i, (2,)).then_inc(down_psum, 1)
                    for i in range(3, 9):
                        bank_read(i)
                        tiles(i, range(PT)).then_inc(down_psum, 1)
                    return
                tiles(0, (2,)).then_inc(down_psum, 1)
                for i in (1, 2):
                    tiles(i, (2,), False)
                bank_read(3)
                tiles(3, range(PT), False)
                pe.wait_ge(piece_lo, START + LOW_PIECES * (g + 1))
                pe.wait_ge(rank_lo, START + 3 * g + 3)
                for i in (1, 2, 3):
                    adapter(i)
                for i in range(4, 9):
                    bank_read(i)
                    tiles(i, range(PT), False)
                    adapter(i)

            def x1_rows(o):
                i, h = o // 2, o % 2
                dst = ps[:, OUT_BANKS[o], :].rearrange("p (q k h) -> p k q h", q=2, k=KC)
                for k in range(KC):
                    for s in range(2):
                        pe.matmul(dst[:, k], x1[:, s, k, P * i:P * i + P], ident[:, 64 * h:64 * h + 64],
                                  start=(k == 0 and s == 0), stop=False)

            def sign_product(o, m):
                i, h = o // 2, o % 2
                for s in range(2):
                    mm = pe.matmul(ps[:, OUT_BANKS[o], :], down[:, s, m, P * i:P * i + P],
                                   signs[:, m, 512 * h:512 * h + 512], start=False, stop=(m == KC - 1 and s == 1))
                return mm

            def mixing_all(g, before=None):
                for e in range(8):
                    mixing(g, e, before)
                    if e == 5 and before is not None:
                        first_layer(g, 0, 0)

            def effective_weight():
                pe.wait_ge(table_in, 16 * KC // 2)
                pe.wait_ge(wsum_done, 2)
                for half in range(2):
                    for c in range(KC):
                        mm = pe.matmul(ps[0:RL, 6 + half, :], wsum[:, c], table[:, c, 512 * half:512 * half + 512],
                                       start=(c == 0), stop=(c == KC - 1))
                mm.then_inc(g_psum, 1)
                pe.wait_ge(g_read, 2)
                low_v = low_rank.rearrange("r (q u o) -> r u q o", q=4, u=KC)
                for u in range(KC):
                    for half in range(2):
                        if u >= 4:
                            pe.wait_ge(w_added, 2 * (u - 4) + half + 1)
                        for k in range(4):
                            mm = pe.matmul(ps[:, weight_bank(u, half), P * k:P * k + P], enc_tiles[:, 4 * half + k], low_v[:, u],
                                           start=True, stop=True)
                        mm.then_inc(w_psum, 1)
                pe.wait_ge(w_added, 9)

            def group(g, last):
                first_layer(g, 0, 1)
                for u in range(1, KC):
                    first_layer(g, u)
                for n in range(2):
                    rank(g, n)
                gate_up_rest(g)
                gate_up_weight(g, 0, 0, "G0", 0)
                down_rest(g)
                with pe.Fori(0, NQ - 1) as q:
                    part_gate_up(g, q)
                    gate_up_weight(g, q + 1, 0, "nextG0", q)
                    down_part(g, q, False)
                part_gate_up(g, NQ - 1)
                down_part(g, NQ - 1, True)
                pe.wait_ge(up_read, START + ACTS * (g + 1))
                for o in range(5):
                    x1_rows(o)
                pe.wait_ge(down_added, DOWNS * (g + 1))
                for o in range(5, 8):
                    x1_rows(o)
                pe.wait_ge(piece_hi, PIECES * (g + 1))
                for m in range(KC):
                    pe.wait_ge(down_lo, 8 * g + m + 1)
                    for o in range(4):
                        mm = sign_product(o, m)
                        if m == KC - 1:
                            mm.then_inc(out_psum, 1)
                for o in range(4, 8):
                    for m in range(KC):
                        mm = sign_product(o, m)
                    mm.then_inc(out_psum, 1)
                if not last:
                    mixing_all(g + 1, g)

            pe.wait_ge(const_set, CONSTS)
            for semaphore in (down_psum, mixed_psum, up_psum, out_psum):
                pe.sem_inc(semaphore, START)
            mixing_all(0)
            effective_weight()
            first_layer(0, 0, 0)
            pe.wait_ge(w_added, 2 * KC)
            with pe.Fori(0, NG - 1) as g:
                group(g, False)
            group(NG - 1, True)


_INS = ["x", "itok_B_0_15", "itok_B_2_6", "L0_cond_weights", "L0_ffn_W_base", "L0_ffn_b_base", "L0_ffn_enc0",
        "L0_ffn_enc1", "L0_ffn_coefs0", "L0_ffn_coefs1", "L0_ffn_mask0", "L0_ffn_mask1", "L1_cond_W_gate",
        "L1_cond_W_up", "L1_cond_W_down", "L1_cond_A_gate", "L1_cond_B_gate", "L1_cond_A_up", "L1_cond_B_up",
        "L1_cond_A_down", "L1_cond_B_down", "L1_ffn_weight", "L1_ffn_bias"]


def shape_constants():
    import numpy as np

    n = np.arange(H)
    table = np.empty((H, H))
    table[0] = 1 / np.sqrt(H)
    for f in range(1, H // 2):
        angle = 2 * np.pi * (f * n % H) / H
        table[2 * f - 1] = np.sqrt(2 / H) * np.cos(angle)
        table[2 * f] = np.sqrt(2 / H) * np.sin(angle)
    table[H - 1] = (1 - 2 * (n % 2)) / np.sqrt(H)
    row = np.arange(P)
    batch = 2 * (row // 32) + row % 2
    own = 0.5 * (batch[:, None] == np.arange(G)[None, :] // S)
    return {"fourier": table.astype(np.float32), "identity": np.eye(P, dtype=np.float32),
            "own_batch": own.astype(np.float32)}


def kernel(**inputs):
    import numpy as np
    import concourse.bacc as bacc
    from concourse.bass_utils import run_bass_kernel_spmd

    nc = bacc.Bacc("TRN2", target_bir_lowering=False, num_devices=1, dynamic_dma_scratch_size=4096)
    arrays, ap = {}, {}
    for name, a in {**{n: inputs[n] for n in _INS}, **shape_constants()}.items():
        a = np.ascontiguousarray(a)
        if name == "x":
            a = a.reshape(NB * S, H)
        if name.startswith("itok"):
            a = a.reshape(1, NB)
        arrays[name] = a
        ap[name] = nc.dram_tensor(name, a.shape, mybir.dt.from_np(a.dtype), kind="ExternalInput").ap()
    out = nc.dram_tensor("out", (NB * S, H), F32, kind="ExternalOutput").ap()
    scratch = nc.dram_tensor("effective_weight", (KC, P, H), F32, kind="Internal").ap()
    c = {n.removeprefix("L1_cond_"): v for n, v in ap.items() if n.startswith("L1_cond_")}
    build_layers(nc, ap["x"], ap["itok_B_0_15"], ap["itok_B_2_6"], ap["L0_cond_weights"], ap["L0_ffn_W_base"],
                 ap["L0_ffn_b_base"], ap["L0_ffn_enc0"], ap["L0_ffn_enc1"], (ap["L0_ffn_coefs0"], ap["L0_ffn_coefs1"]),
                 (ap["L0_ffn_mask0"], ap["L0_ffn_mask1"]), ap["fourier"], scratch, c["W_gate"], c["W_up"], c["W_down"],
                 c["A_gate"], c["B_gate"], c["A_up"], c["B_up"], c["A_down"], c["B_down"], ap["L1_ffn_weight"],
                 ap["L1_ffn_bias"], ap["identity"], ap["own_batch"], out)
    r = run_bass_kernel_spmd(nc, [arrays], core_ids=[0])
    return np.asarray(r.results[0]["out"]).reshape(NB, S, H)
```

```python
from contextlib import ExitStack

import concourse.bass as bass
from concourse import mybir

F32 = mybir.dt.float32
F32R = mybir.dt.float32r
U8 = mybir.dt.uint8
ALU = mybir.AluOpType
ACT = mybir.ActivationFunctionType

P = 128
H = 1024
KC = H // P
F = 2752
PT = 3
NQ = F // (P * PT)
TILES = NQ * PT
FB = NQ * P * PT
FR = F - FB
G = 512
S = 64
NB = 32
NG = NB * S // G
GB = G // S
RANK = 16
NE, R0, R1 = 3, 32, 8
RL = R0 + R1
NAD = 16

NAT_SLOTS = 3
NAT_X, NAT_W, NAT_REM, NAT_FIRST, NAT_SIGN, NAT_GU = 0, 4, 12, (13, 14, 17), 15, 15
NAT_UNITS = 57
SPLIT_SLOTS = 3
SPLIT_X, SPLIT_W, SPLIT_AG, SPLIT_AU, SPLIT_REM, SPLIT_GU, SPLIT_BD = 0, 4, 12, 13, 14, 15, 57
SPLIT_UNITS = 60
PART_UNITS = 6
assert NAT_UNITS % NAT_SLOTS == SPLIT_UNITS % SPLIT_SLOTS == PART_UNITS % NAT_SLOTS == 0

HEAD = (["B"] * 3 + ["AG"] * 2 + ["AU"] * 2 + ["REM"] * 2 + ["BREM"] + ["DREM"] * 2 + ["ADREM"]
        + ["G0"] * 2 + ["U0"] * 2 + ["S6"] * 2 + ["S7"] * 2 + ["G1"] * 2)
PART = (["U1"] * 2 + ["D0"] * 2 + ["G2"] * 2 + ["D1"] * 2 + ["U2"] * 2 + ["D2"] * 2 + ["AD"] + ["nextG0"] * 2
        + ["Sq"] * 2 + ["nextB"] * 3 + ["nextU0"] * 2 + ["nextG1"] * 2)
LAST = PART[:13] + ["BD"] * 2
PART_PIECES = len(PART)
PIECES = len(HEAD) + (NQ - 1) * PART_PIECES + len(LAST)
LOW_PIECES = PIECES - 2 * KC
PART_LOWS = PART_PIECES - 2
assert PIECES % 2 == 0 and PART_PIECES % 2 == 0


def first_of(name):
    return HEAD.index(name) if name in HEAD else len(HEAD) + (PART if name in PART else LAST).index(name)


def lows_before(c):
    return sum(not x.startswith("S") for x in (HEAD + PART)[:max(0, c)])


ACTS = TILES + 1
START = 1
CONSTS = 4
S1_BANKS = ((0, 2), (2, 4), (4, 6))
OUT_BANKS = (0, 1, 2, 6, 7, 3, 4, 5)
X1_BANKS = (6, 7, 2, 0, 1, 2, 0, 1)
DOWN_ORDER = (8, 0, 1, 2, 3, 4, 5, 6, 7)
BASE_SLOTS = 4
DOWNS = 9 * (1 + NQ)
T_BANK = 6
D_BANK = 3


def build_layers(nc, x, cond_index, lora_index, cond_w, W_base, b_base, enc0, enc1, coefs, masks, fourier, scratch,
                 W_gate, W_up, W_down, A_gate, B_gate, A_up, B_up, A_down, B_down, sign_w, bias, identity,
                 own_batch, out):
    with ExitStack() as ctx:
        def sb(name, shape, dtype):
            return ctx.enter_context(nc.sbuf_tensor(name, shape, dtype))

        def sem(name):
            return ctx.enter_context(nc.semaphore(name))

        with ExitStack() as early:
            def early_sb(name, shape, dtype=F32):
                return early.enter_context(nc.sbuf_tensor(name, shape, dtype))[:]

            table = early_sb("fourier_table", [P, KC, H])
            base = early_sb("base", [P, BASE_SLOTS, 4, 256])
            base_t = early_sb("base_t", [P, KC, H])
            low_rank = early_sb("low_rank", [RL, H])
            enc_tiles = early_sb("enc_tiles", [RL, KC, P])
            wsum = early_sb("wsum", [P, KC, RL])
            coef, kept = ([early_sb(f"{name}{i}", [P, NE, KC * r]) for i, r in enumerate((R0, R1))]
                          for name in ("coef", "kept"))
            coef_mask = [early_sb(f"coef_mask{i}", [P, NE, KC * r], U8) for i, r in enumerate((R0, R1))]
            enc = early_sb("enc", [RL, H])

        x1 = sb("x1", [P, 2, KC, G], F32R)
        hidden = sb("hidden", [P, 9216], F32R)
        lora_b = sb("lora_b", [P, 3, PT, 2, P], F32R)
        lora_t = sb("lora_t", [P, 2, 2, G], F32R)
        lora_ad = sb("lora_ad", [P, 2, PT, P], F32R)
        nat_down = sb("nat_down", [P, 32, 96], F32)
        out_sb = sb("out_sb", [P, G // 32, P], F32)
        turned = sb("turned", [P, 2 * KC * G], F32R)
        split = sb("split", [P, SPLIT_SLOTS, 2, H], F32R)
        lora_b_rem = sb("lora_b_rem", [P, 3, 2, P], F32R)
        mix = sb("mix", [P, 2, 3, P], F32R)
        mixed = turned[:].rearrange("p (s k t) -> p s k t", s=2, k=KC)
        signs = turned[:].rearrange("p (m o) -> p m o", m=KC)
        down_w = hidden[:, 0:6144].rearrange("p (s j m h) -> p s j m h", s=2, j=PT, m=KC)
        acts = hidden[:, 6144:9216].rearrange("p (s j t) -> p s j t", s=2, j=PT)
        down_later = hidden[:, 0:7168].rearrange("p (s m t) -> p s m t", s=2, m=KC - 1)
        down_first = lora_b[:].rearrange("p s j t f -> p (s j t f)")[:, 0:1024].rearrange("p (s t) -> p s t", s=2)

        nat = sb("nat", [P, NAT_SLOTS, H], F32)
        nat_a = sb("nat_a", [P, 2, 4, 256], F32)
        nat_b = sb("nat_b", [P, 2, 4, 2, PT * RANK], F32)
        nat_b_rem = sb("nat_b_rem", [P, 2, 2, 2, RANK], F32)
        nat_ad = sb("nat_ad", [P, 4, 96], F32)
        nat_c = sb("nat_c", [P, 4, P], F32)
        acc = sb("acc", [P, 9, G], F32)
        gated = sb("gated", [P, G], F32)
        act_f = sb("act_f", [P, G], F32)
        own_sb = sb("own_sb", [P, GB], F32)
        b_col = sb("b_col", [P, KC], F32)
        bias_col = sb("bias_col", [P, KC], F32)
        out_halves = [out_sb[:], nat_down[:].rearrange("p a b -> p (a b)")[:, 0:G // 32 * P]
                      .rearrange("p (n c) -> p n c", c=P)]
        ps = ctx.enter_context(nc.psum_tensor("ps", [P, 8, 512], F32))

        ident_in, const_in, const_set = sem("ident_in"), sem("const_in"), sem("const_set")
        coef_in, table_in, enc_in = sem("coef_in"), sem("table_in"), sem("enc_in")
        base_in = [sem(f"base_in{i}") for i in range(BASE_SLOTS)]
        kept_step, wsum_done, g_psum, g_read = sem("kept_step"), sem("wsum_done"), sem("g_psum"), sem("g_read")
        base_turned, w_psum, w_added = sem("base_turned"), sem("w_psum"), sem("w_added")
        w_stored = [sem(f"w_stored{u}") for u in range(KC)]
        nat_full = [sem(f"nat_full{i}") for i in range(NAT_SLOTS)]
        nat_c_full = [sem(f"nat_c_full{p}") for p in range(4)]
        nat_down_full, nat_b_full = sem("nat_down_full"), sem("nat_b_full")
        nat_a_full = [sem("nat_a_full0"), sem("nat_a_full1")]
        nat_b_rem_full, nat_ad_full, nat_sign_full = sem("nat_b_rem_full"), sem("nat_ad_full"), sem("nat_sign_full")
        pool_passed = sem("pool_passed")
        plain_hi, plain_lo = sem("plain_hi"), sem("plain_lo")
        piece_turned, piece_hi, piece_lo = sem("piece_turned"), sem("piece_hi"), sem("piece_lo")
        mix_hi, mix_lo = sem("mix_hi"), sem("mix_lo")
        mixed_psum, mixed_hi, mixed_lo = sem("mixed_psum"), sem("mixed_hi"), sem("mixed_lo")
        xt_copied = sem("xt_copied")
        x1_psum, x1_sum, x1_hi, x1_lo = sem("x1_psum"), sem("x1_sum"), sem("x1_hi"), sem("x1_lo")
        rank_psum = sem("rank_psum")
        rank_sum, rank_hi, rank_lo = sem("rank_sum"), sem("rank_hi"), sem("rank_lo")
        rest_psum, rest_moved = sem("rest_psum"), sem("rest_moved")
        gate_psum, up_psum = sem("gate_psum"), sem("up_psum")
        gate_read, up_read = sem("gate_read"), sem("up_read")
        act_hi, act_lo = sem("act_hi"), sem("act_lo")
        down_psum, down_added = sem("down_psum"), sem("down_added")
        down_hi, down_lo = sem("down_hi"), sem("down_lo")
        out_psum, out_read = sem("out_psum"), sem("out_read")
        out_sum, out_turned = sem("out_sum"), sem("out_turned")
        out_stored = [sem("out_stored0"), sem("out_stored1")]

        block = ctx.enter_context(nc.Block())

        def nat_filled(g, q, n):
            return (NAT_UNITS // NAT_SLOTS * g + PART_UNITS // NAT_SLOTS * q + (n // NAT_SLOTS + 1)) * 128

        def piece_number(g, q, c):
            return PIECES * g + PART_PIECES * q + c

        def low_number(g, q, c):
            return LOW_PIECES * g + PART_LOWS * q + lows_before(c)

        @block.sync
        def _(sp):
            def constants():
                sp.dma_start(own_sb[:], own_batch).then_inc(const_in, 16)
                for dst, src in ((b_col, b_base), (bias_col, bias)):
                    for hq in range(4):
                        with nc.allow_non_contiguous_dma(reason="1024 words, once"):
                            sp.dma_start(dst[32 * hq:32 * hq + 32, :], src.rearrange("(q k h) -> q h k", q=4, k=KC)[hq])\
                              .then_inc(const_in, 16)

            base_rows = W_base.rearrange("(oq u oo) (hq c) -> u hq oo oq c", oq=4, u=KC, hq=4)

            def load_base(u):
                if u >= BASE_SLOTS:
                    sp.wait_ge(base_turned, u - BASE_SLOTS + 1)
                for hq in range(4):
                    sp.dma_start(base[32 * hq:32 * hq + 32, u % BASE_SLOTS], base_rows[u, hq])\
                      .then_inc(base_in[u % BASE_SLOTS], 16)

            x_rows = x.rearrange("(n p) c -> n p c", p=P)
            part_rows = [a[0:FB, :].rearrange("(q fq ff j) (hq c) -> q ff fq j hq c", q=NQ, fq=4, j=PT, hq=4)
                         for a in (W_gate, W_up)]
            rest_rows = [a[FB:F, :].rearrange("(fq ff) (hq c) -> hq ff fq c", fq=2, hq=4) for a in (W_gate, W_up)]
            sign_rows = sign_w.rearrange("(b u o) (hq c) -> u hq o b c", u=KC, b=4, hq=4)
            down_rows = W_down[:, 0:FB].rearrange("(b h) (q fq c) -> q fq h b c", h=32, q=NQ, fq=4)
            down_rest = W_down[:, FB:F].rearrange("(b h) (fq c) -> fq h b c", h=32, fq=2)

            before = {NAT_W + u + 3: ("plain", 4 + u) for u in range(KC)}
            before |= {NAT_X + 3 + p: ("plain", p) for p in range(4)}
            before |= {NAT_REM + 3: ("piece", "REM")}
            before |= {NAT_FIRST[0] + 3: ("piece", "G0"), NAT_FIRST[1] + 3: ("piece", "U0")}

            def free_nat(g, q, n):
                if n >= NAT_GU + 3:
                    name = ("nextB", "nextU0", "nextG1", "U1", "G2", "U2")[n - NAT_GU - 3]
                    c = first_of(name) + (3 if name == "nextB" else 2)
                    if n < NAT_GU + 6:
                        c -= PART_PIECES
                    sp.wait_ge(piece_turned, piece_number(g, q, c))
                elif n >= 3:
                    kind, what = before[n]
                    if kind == "plain":
                        sp.wait_ge(plain_lo, 12 * g + what + 1)
                    else:
                        sp.wait_ge(piece_turned, piece_number(g, 0, first_of(what) + 2))

            def nat_quadrant(hq, n):
                return nat[32 * hq:32 * hq + 32, n % NAT_SLOTS, :].rearrange("p (b c) -> p b c", b=4)

            def load_gate_up(g, q, n, part, k):
                free_nat(g, q, n)
                for hq in range(4):
                    src = part_rows[k % 2][bass.ds(part, 1), :, :, k // 2, hq, :].rearrange("a f b c -> (a f) b c")
                    sp.dma_start(nat_quadrant(hq, n), src).then_inc(nat_full[n % NAT_SLOTS], 32)

            def load_down(part):
                for fq in range(4):
                    sp.dma_start(nat_down[32 * fq:32 * fq + 32],
                                 down_rows[bass.ds(part, 1), fq].rearrange("a h b c -> (a h) b c"))\
                      .then_inc(nat_down_full, 16)

            def load_sign(g, i):
                n = NAT_SIGN + i
                free_nat(g, 0, n)
                for hq in range(4):
                    sp.dma_start(nat_quadrant(hq, n), sign_rows[6 + i, hq]).then_inc(nat_full[n % NAT_SLOTS], 32)

            def load_sign_part(g, q):
                sp.wait_ge(piece_turned, piece_number(g, q - 1, first_of("Sq") + 2))
                for hq in range(4):
                    sp.dma_start(nat_a[32 * hq:32 * hq + 32, 1],
                                 sign_rows[bass.ds(q, 1), hq].rearrange("a o b c -> (a o) b c"))\
                      .then_inc(nat_sign_full, 16)

            out_rows = out.rearrange("(g n t) (hq a c) -> g hq a t n c", g=NG, t=32, hq=4, a=2)

            def load_x(g, p, ahead=None):
                n = NAT_X + p
                if p == 3:
                    free_nat(g, 0, n)
                elif ahead is not None:
                    sp.wait_ge(piece_turned, piece_number(ahead, NQ - 1, first_of(("U1", "G2", "U2")[p]) + 2))
                sp.dma_start(nat[:, n % NAT_SLOTS, :], x_rows[bass.ds(4 * g + p, 1)].rearrange("a p c -> (a p) c"))\
                  .then_inc(nat_full[n % NAT_SLOTS], 128)

            def load_weight(g, u):
                n = NAT_W + u
                free_nat(g, 0, n)
                sp.dma_start(nat[:, n % NAT_SLOTS, :], scratch[u]).then_inc(nat_full[n % NAT_SLOTS], 128)

            def store(g):
                for half in range(2):
                    sp.wait_ge(out_turned, START + 8 * g + 4 * half + 4)
                    for hq in range(4):
                        sp.dma_start(out_rows[bass.ds(g, 1), hq, half].rearrange("a t n c -> (a t) n c"),
                                     out_halves[half][32 * hq:32 * hq + 32]).then_inc(out_stored[half], 16)

            def group(g):
                free_nat(g, 0, NAT_REM)
                for t in range(2):
                    for hq in range(4):
                        sp.dma_start(nat_quadrant(hq, NAT_REM)[:, 2 * t:2 * t + 2, :], rest_rows[t][hq])\
                          .then_inc(nat_full[NAT_REM % NAT_SLOTS], 16)
                sp.wait_ge(out_stored[1], 64 * (START + g))
                for fq in range(2):
                    sp.dma_start(nat_down[32 * fq:32 * fq + 32, :, 0:32], down_rest[fq]).then_inc(nat_down_full, 32)
                for k in range(2):
                    load_gate_up(g, 0, NAT_FIRST[k], 0, k)
                for i in range(2):
                    load_sign(g, i)
                load_gate_up(g, 0, NAT_FIRST[2], 0, 2)
                sp.wait_ge(piece_turned, piece_number(g, 0, first_of("DREM") + 2))
                load_down(0)
                with sp.Fori(0, NQ - 1) as q:
                    load_sign_part(g, q)
                    for k in range(3, 6):
                        load_gate_up(g, q, NAT_GU + k, q, k)
                    for k in range(2):
                        load_gate_up(g, q, NAT_GU + PART_UNITS + k, q + 1, k)
                    sp.wait_ge(piece_turned, piece_number(g, q, first_of("D2") + 2))
                    load_down(q + 1)
                    load_gate_up(g, q, NAT_GU + PART_UNITS + 2, q + 1, 2)
                for k in range(3, 6):
                    load_gate_up(g, NQ - 1, NAT_GU + k, NQ - 1, k)

            sp.dma_start(act_f[:, 0:P], identity).then_inc(ident_in, 16)
            for p in range(3):
                load_x(0, p)
            for i in range(2):
                sp.dma_start(coef[i], coefs[i].rearrange("e (p c) r -> p e (c r)", c=KC)).then_inc(coef_in, 16)
                sp.dma_start(coef_mask[i], masks[i].rearrange("e (p c) r -> p e (c r)", c=KC)).then_inc(coef_in, 16)
            load_x(0, 3)
            table_rows = fourier.rearrange("(p c) n -> p c n", c=KC)
            for c in range(KC):
                if c in (2, 5):
                    sp.wait_ge(plain_lo, 2 + c // 5)
                sp.dma_start(table[:, c], table_rows[:, c]).then_inc(table_in, 16)
            sp.dma_start(enc[0:R0, :], enc0).then_inc(enc_in, 16)
            sp.dma_start(enc[R0:RL, :], enc1).then_inc(enc_in, 16)
            for u in range(2):
                load_base(u)
            constants()
            for u in range(2, KC):
                load_base(u)
            for semaphore in out_stored:
                sp.sem_inc(semaphore, 64 * START)
            for u in range(KC):
                sp.wait_ge(w_stored[u], 16)
                load_weight(0, u)
            with sp.Fori(0, NG - 1) as g:
                group(g)
                for p in range(4):
                    load_x(g + 1, p, g)
                load_weight(g + 1, 0)
                load_weight(g + 1, 1)
                store(g)
                for u in range(2, KC):
                    load_weight(g + 1, u)
            group(NG - 1)
            store(NG - 1)
            for s in range(2):
                sp.wait_ge(out_stored[s], 64 * (START + NG))

        @block.gpsimd
        def _(pool):
            b_rows = [a[0, :, 0:FB, :].rearrange("a (q fq ff j) r -> q a ff fq (j r)", q=NQ, fq=4, j=PT)
                      for a in (B_gate, B_up)]
            b_rest = [a[0, :, FB:F, :].rearrange("a (fq ff) r -> a ff fq r", fq=2) for a in (B_gate, B_up)]
            ad_rows = A_down[0, :, :, 0:FB].rearrange("a r (q fq c) -> q a fq r c", q=NQ, fq=4)
            ad_rest = A_down[0, :, :, FB:F].rearrange("a r (fq c) -> a fq r c", fq=2)

            def chosen(table, g, b):
                return pool.value_load(table[:, bass.ds(GB * g + b, 1)], min_val=0, max_val=NAD - 1)

            def wait(semaphore, value):
                pool.wait_ge(semaphore, value)
                pool.sem_inc(pool_passed, 1)

            def load_cond(g, p):
                if p == 0:
                    wait(mix_lo, START + 4 * g)
                for b2 in range(2):
                    i = chosen(cond_index, g, 2 * p + b2)
                    pool.dma_start(nat_c[S * b2:S * b2 + S, p, S * b2:S * b2 + S],
                                   cond_w[bass.ds(i, 1)].rearrange("a c d -> (a c) d")).then_inc(nat_c_full[p], 16)

            def load_a(g, a, slot):
                for b in range(GB):
                    i = chosen(lora_index, g, b)
                    pool.dma_start(nat_a[b % 2::2, slot, b // 2, :],
                                   a[0, bass.ds(i, 1)].rearrange("a r (hq c) -> hq (a r) c", hq=4))\
                        .then_inc(nat_a_full[slot], 16)

            def load_b_down(g):
                slots = nat_a[:, 0].rearrange("p a c -> p (a c)").rearrange("p (n s r) -> p n s r", s=2, r=RANK)
                for b in range(GB):
                    i = chosen(lora_index, g, b)
                    pool.dma_start(slots[32 * (b // 2):32 * (b // 2) + 32, :, b % 2, :],
                                   B_down[0, bass.ds(i, 1)].rearrange("a (n h) r -> (a h) n r", h=32))\
                        .then_inc(nat_a_full[0], 16)

            def load_rest(g):
                for b in range(GB):
                    i = chosen(lora_index, g, b)
                    for t in range(2):
                        pool.dma_start(nat_b_rem[32 * (b // 2):32 * (b // 2) + 32, t, :, b % 2, :],
                                       b_rest[t][bass.ds(i, 1)].rearrange("a f b c -> (a f) b c"))\
                            .then_inc(nat_b_rem_full, 16)
                    pool.dma_start(nat_ad[b % 2:64:2, b // 2, 0:32],
                                   ad_rest[bass.ds(i, 1)].rearrange("a f r c -> (a f) r c")).then_inc(nat_ad_full, 16)

            def load_b(g, part):
                for b in range(GB):
                    i = chosen(lora_index, g, b)
                    for t in range(2):
                        pool.dma_start(nat_b[32 * (b // 2):32 * (b // 2) + 32, t, :, b % 2, :],
                                       b_rows[t][bass.ds(part, 1), bass.ds(i, 1)].rearrange("q a f b c -> (q a f) b c"))\
                            .then_inc(nat_b_full, 16)

            def load_ad(g, part):
                for b in range(GB):
                    i = chosen(lora_index, g, b)
                    pool.dma_start(nat_ad[b % 2::2, b // 2, :],
                                   ad_rows[bass.ds(part, 1), bass.ds(i, 1)].rearrange("q a f r c -> (q a f) r c"))\
                        .then_inc(nat_ad_full, 16)

            def wait_turned(g, q, name, pieces):
                wait(piece_turned, piece_number(g, q, first_of(name) + pieces))

            def group(g):
                wait(piece_lo, START + LOW_PIECES * g)
                load_a(g, A_gate, 0)
                load_a(g, A_up, 1)
                load_b(g, 0)
                load_rest(g)
                wait_turned(g, 0, "AG", 2)
                load_b_down(g)
                wait_turned(g, 0, "ADREM", 1)
                load_ad(g, 0)
                with pool.Fori(0, NQ - 1) as q:
                    wait_turned(g, q - 1, "nextB", 3)
                    load_b(g, q + 1)
                    wait_turned(g, q, "AD", 1)
                    load_ad(g, q + 1)

            pool.wait_ge(const_set, 1)
            for p in range(4):
                load_cond(0, p)
            with pool.Fori(0, NG - 1) as g:
                group(g)
                for p in range(4):
                    load_cond(g + 1, p)
            group(NG - 1)

        HALVES = ((slice(0, P // 2), slice(0, G // 2)), (slice(P // 2, P), slice(G // 2, G)))

        def rest_columns(kind):
            return lora_b_rem[:, kind].rearrange("p t (n f) -> p (t n) f", n=2)[:, 0::3, :]

        def bank_of(c):
            return ps[:, T_BANK + c % 2, :]

        def down(s, m):
            return down_later[:, s, m - 1, :] if m else down_first[:, s, :]

        def weight_bank(u, half):
            return 3 + (2 * u + half) % 3

        def tiled(i, dst, src, *hi):
            if i >= 4:
                return (dst, src, *hi)
            dst, *hi = (v.rearrange("p (k q t) -> p q k t", q=4, k=KC) for v in (dst, *hi))
            return (dst, src.rearrange("p (q k t) -> p q k t", q=4, k=KC), *hi)

        def sign_target(u, half):
            return signs[:, 4 * half:4 * half + 4, bass.ds(P * u, P)]

        @block.scalar
        def _(act):
            def copy(dst, src):
                return act.activation(dst, src, ACT.Copy)

            def slot_read(g, q, m):
                if m < 3:
                    act.wait_ge(down_psum, START + DOWNS * g)
                elif m < SPLIT_W + 3:
                    act.wait_ge(mixed_psum, START + 8 * g + 2 * (m - 3) + 2)
                elif m < SPLIT_AG + 3:
                    act.wait_ge(x1_psum, 8 * g + m - 3 - SPLIT_W + 1)
                elif m < SPLIT_REM + 3:
                    act.wait_ge(rank_psum, 2 * g + m - 3 - SPLIT_AG + 1)
                elif m == SPLIT_REM + 3:
                    act.wait_ge(rest_psum, g + 1)
                else:
                    k = m - 3 - SPLIT_GU
                    act.wait_ge(up_psum if k % 2 else gate_psum, (START if k % 2 else 0) + TILES * g + PT * q + k // 2 + 1)

            def plain_unit(g, i, n, m):
                act.wait_ge(nat_full[n % NAT_SLOTS], nat_filled(g, 0, n))
                slot_read(g, 0, m)
                copy(*tiled(i, split[:, m % SPLIT_SLOTS, 0, :], nat[:, n % NAT_SLOTS, :])).then_inc(plain_hi, 1)

            def piece(g, q, c, dst, src, func=ACT.Copy):
                act.wait_ge(piece_turned, piece_number(g, q, c) + 1)
                act.activation(dst, src, func).then_inc(piece_hi, 1)

            def doubled(g, q, c, dsts, src):
                act.wait_ge(piece_turned, piece_number(g, q, c) + 1)
                for dst, (rows, _) in zip(dsts, HALVES):
                    for to, _ in HALVES:
                        last = copy(dst[to], src[rows])
                last.then_inc(piece_hi, 1)

            def unit(g, q, name, m):
                c = first_of(name)
                slot_read(g, q, m)
                for half in range(2):
                    piece(g, q, c + half, split[:, m % SPLIT_SLOTS, 0, 512 * half:512 * half + 512], bank_of(c + half))

            def sign_unit(g, q, name, u):
                c = first_of(name)
                for half in range(2):
                    piece(g, q, c + half, sign_target(u, half),
                          bank_of(c + half).rearrange("p (m o) -> p m o", m=4), ACT.Sign)

            def down_tile(g, q, j):
                c = first_of(f"D{j}")
                act.wait_ge(down_psum, START + DOWNS * g + 9 * (q + 1))
                for half in range(2):
                    piece(g, q, c + half, down_w[:, 0, j, 4 * half:4 * half + 4, :],
                          bank_of(c + half).rearrange("p (m h) -> p m h", m=4))

            def lora_b_tiles(g, q, name, part):
                c = first_of(name)
                act.wait_ge(up_psum, START + TILES * g + PT * part)
                for j in range(PT):
                    doubled(g, q, c + j, [lora_b[:, kind, j].rearrange("p t f -> p (t f)") for kind in range(2)],
                            bank_of(c + j)[:, 0:256])

            def cond(g, p):
                act.wait_ge(nat_c_full[p], 32 * (g + 1))
                act.wait_ge(mixed_psum, START + 8 * g + max(0, 2 * p - 2))
                copy(mix[:, p % 2, 0, :], nat_c[:, p, :]).then_inc(mix_hi, 1)

            def mixing(g, e):
                p, kh = e // 2, e % 2
                b0, b1 = S1_BANKS[e % 3]
                src = ps[:, b0:b1, :].rearrange("p a (k n t) -> p (a k) n t", k=2, n=2)
                act.wait_ge(mixed_psum, START + 8 * g + e + 1)
                copy(acc[:, 4 * kh:4 * kh + 4, P * p:P * p + P], src[:, :, 1, :]).then_inc(xt_copied, 1)
                copy(mixed[:, 0, 4 * kh:4 * kh + 4, P * p:P * p + P], src[:, :, 0, :]).then_inc(mixed_hi, 1)

            def x1_tile(g, u):
                act.wait_ge(x1_sum, 8 * g + u + 1)
                copy(x1[:, 0, u, :], acc[:, u, :]).then_inc(x1_hi, 1)

            def rank(g, n):
                act.wait_ge(rank_sum, 3 * g + n + 1)
                if n == 2:
                    act.wait_ge(up_psum, START + TILES * (g + 1))
                if n < 2:
                    for rows, tokens in HALVES:
                        copy(lora_t[rows, n, 1, tokens], act_f[rows, tokens])
                copy(lora_t[:, n % 2, 0, :], act_f[:]).then_inc(rank_hi, 1)

            def act_rest(g):
                act.wait_ge(up_read, START + ACTS * g)
                act.wait_ge(rest_psum, g + 1)
                act.activation(gated[0:64, :], ps[0:64, 1, :], ACT.Silu).then_inc(gate_read, 1)
                act.wait_ge(rank_lo, START + 3 * g + 2)
                copy(act_f[0:64, :], ps[64:128, 1, :]).then_inc(rest_moved, 1)
                act.wait_ge(up_read, START + ACTS * g + 1)
                copy(acts[0:64, 0, 0, :], act_f[0:64, :]).then_inc(act_hi, 1)

            def act_tile(g, q, j):
                act.wait_ge(up_read, START + ACTS * g + PT * q + j + 1)
                act.wait_ge(gate_psum, TILES * g + PT * q + j + 1)
                act.activation(gated[:], ps[:, 2 * j % 3, :], ACT.Silu).then_inc(gate_read, 1)
                act.wait_ge(up_read, START + ACTS * g + PT * q + j + 2)
                copy(acts[:, 0, j, :], act_f[:]).then_inc(act_hi, 1)

            def part(g, q, last):
                unit(g, q, "U1", SPLIT_GU + 3)
                down_tile(g, q, 0)
                act_tile(g, q, 0)
                unit(g, q, "G2", SPLIT_GU + 4)
                down_tile(g, q, 1)
                unit(g, q, "U2", SPLIT_GU + 5)
                act_tile(g, q, 1)
                down_tile(g, q, 2)
                c = first_of("AD")
                piece(g, q, c, lora_ad[:, 0].rearrange("p j a -> p (j a)"), bank_of(c)[:, 0:PT * P])
                if last:
                    unit(g, q, "BD", SPLIT_BD - PART_UNITS * q)
                    act_tile(g, q, 2)
                    return
                unit(g, q, "nextG0", SPLIT_GU + 6)
                act_tile(g, q, 2)
                sign_unit(g, q, "Sq", q)
                lora_b_tiles(g, q, "nextB", q + 1)
                unit(g, q, "nextU0", SPLIT_GU + 7)
                unit(g, q, "nextG1", SPLIT_GU + 8)

            def mixing_ahead(g):
                for p in range(3):
                    plain_unit(g, p, NAT_X + p, SPLIT_X + p)
                    if p < 2:
                        cond(g, p)

            def weight_unit(g, u):
                plain_unit(g, 4 + u, NAT_W + u, SPLIT_W + u)

            def mixing_all(g, weights):
                for e in range(8):
                    mixing(g, e)
                    if e == 1:
                        cond(g, 2)
                        plain_unit(g, 3, NAT_X + 3, SPLIT_X + 3)
                    if e == 3:
                        cond(g, 3)
                    if weights and e in (3, 5, 7):
                        weight_unit(g, e // 2 - 1)

            def store_weight(u):
                act.wait_ge(w_added, 2 * u + 2)
                act.dma_start(scratch[u], base_t[:, u]).then_inc(w_stored[u], 16)

            def first_layer_all(g, making):
                for u in range(KC):
                    x1_tile(g, u)
                    if making and u < 4:
                        store_weight(u + 4)
                    if u < 5:
                        weight_unit(g, 3 + u)
                        if u == 4:
                            lora_b_tiles(g, 0, "B", 0)
                    else:
                        unit(g, 0, ("AG", "AU", "REM")[u - 5], SPLIT_W + 3 + u)
                c = first_of("BREM")
                act.wait_ge(out_psum, START + 8 * g)
                doubled(g, 0, c, [rest_columns(kind) for kind in range(2)],
                        bank_of(c)[:, 0:P].rearrange("p (t f) -> p t f", t=2))

            def group(g, last):
                act.wait_ge(x1_psum, 8 * g + KC)
                rank(g, 0)
                c = first_of("DREM")
                for half in range(2):
                    piece(g, 0, c + half, down_w[0:64, 0, 0, 4 * half:4 * half + 4, :],
                          bank_of(c + half)[0:64].rearrange("p (m h) -> p m h", m=4))
                c = first_of("ADREM")
                piece(g, 0, c, lora_ad[0:64, 0, 0, :], bank_of(c)[0:64, 0:P])
                rank(g, 1)
                unit(g, 0, "G0", SPLIT_GU)
                unit(g, 0, "U0", SPLIT_GU + 1)
                act_rest(g)
                sign_unit(g, 0, "S6", 6)
                sign_unit(g, 0, "S7", 7)
                unit(g, 0, "G1", SPLIT_GU + 2)
                with act.Fori(0, NQ - 1) as q:
                    part(g, q, False)
                part(g, NQ - 1, True)
                rank(g, 2)
                for m in range(KC):
                    if m == 1:
                        act.wait_ge(down_psum, START + DOWNS * (g + 1))
                    act.wait_ge(down_added, DOWNS * g + 9 * NQ + DOWN_ORDER.index(m) + 1)
                    copy(down(0, m), acc[:, m, :]).then_inc(down_hi, 1)
                if not last:
                    mixing_ahead(g + 1)
                    mixing_all(g + 1, True)
                    first_layer_all(g + 1, False)

            act.wait_ge(const_set, 2)
            act.activation(gated[:, 0:1], lora_b_rem[:, 0, 0, 0:1].bitcast(F32), ACT.Silu)
            mixing_ahead(0)
            mixing_all(0, False)
            for u in range(4):
                if u == 3:
                    weight_unit(0, 0)
                store_weight(u)
            for u in (1, 2):
                weight_unit(0, u)
            first_layer_all(0, True)
            with act.Fori(0, NG - 1) as g:
                group(g, False)
            group(NG - 1, True)

        @block.vector
        def _(dve):
            def lo(dst, full, hi):
                return dve.tensor_tensor(dst, full, hi.bitcast(F32), ALU.subtract)

            def plain_unit(g, i, n, m):
                s = m % SPLIT_SLOTS
                dve.wait_ge(plain_hi, 12 * g + i + 1)
                lo(*tiled(i, split[:, s, 1, :], nat[:, n % NAT_SLOTS, :], split[:, s, 0, :])).then_inc(plain_lo, 1)

            def turn(g, q, c, dst, src):
                if c < 2:
                    dve.wait_ge(piece_lo, START + LOW_PIECES * g)
                else:
                    dve.wait_ge(piece_hi, piece_number(g, q, c - 1))
                    dve.wait_ge(piece_lo, START + low_number(g, q, c - 1))
                dve.transpose(dst, src).then_inc(piece_turned, 1)

            def piece_low(g, q, c, dst, src, hi):
                dve.wait_ge(piece_hi, piece_number(g, q, c) + 1)
                lo(dst, src, hi).then_inc(piece_lo, 1)

            def doubled_low(g, q, c, kinds, src):
                dve.wait_ge(piece_hi, piece_number(g, q, c) + 1)
                for kind, (rows, _) in enumerate(HALVES):
                    last = lo(kinds[2][rows], src[rows], kinds[kind][rows])
                last.then_inc(piece_lo, 1)

            def turn_unit(g, q, c, rows):
                for half in range(2):
                    turn(g, q, c + half, bank_of(c + half).rearrange("p (k b h) -> p k b h", k=4, b=4),
                         rows.rearrange("p (b k h) -> p k b h", b=4, k=KC)[:, 4 * half:4 * half + 4])

            def unit_lows(g, q, c, m):
                s = m % SPLIT_SLOTS
                for half in range(2):
                    cols = slice(512 * half, 512 * half + 512)
                    piece_low(g, q, c + half, split[:, s, 1, cols], bank_of(c + half), split[:, s, 0, cols])

            def weight_unit(g, q, name, n, m):
                dve.wait_ge(nat_full[n % NAT_SLOTS], nat_filled(g, q, n))
                c = first_of(name)
                turn_unit(g, q, c, nat[:, n % NAT_SLOTS, :])
                unit_lows(g, q, c, m)

            def adapter_unit(g, name, fill, m):
                dve.wait_ge(nat_a_full[fill], 128 * ((2, 1)[fill] * g + 1))
                c = first_of(name)
                turn_unit(g, 0, c, nat_a[:, fill].rearrange("p b c -> p (b c)"))
                unit_lows(g, 0, c, m)

            def b_down_unit(g, q, m):
                dve.wait_ge(nat_a_full[0], 128 * (2 * g + 2))
                c = first_of("BD")
                rows = nat_a[:, 0].rearrange("p a c -> p (a c)").rearrange("p (q m s r) -> p m q r s", q=4, m=KC, s=2)
                for half in range(2):
                    if c + half >= 2:
                        dve.wait_ge(piece_hi, piece_number(g, q, c + half - 1))
                        dve.wait_ge(piece_lo, START + low_number(g, q, c + half - 1))
                    for m4 in range(4):
                        for hq in range(4):
                            t = dve.transpose(bank_of(c + half)[:, P * m4 + 32 * hq:P * m4 + 32 * hq + 32],
                                              rows[:, 4 * half + m4, hq])
                    t.then_inc(piece_turned, 1)
                unit_lows(g, q, c, m)

            def sign_unit(g, i):
                n = NAT_SIGN + i
                dve.wait_ge(nat_full[n % NAT_SLOTS], nat_filled(g, 0, n))
                turn_unit(g, 0, first_of(f"S{6 + i}"), nat[:, n % NAT_SLOTS, :])

            def sign_part(g, q):
                dve.wait_ge(nat_sign_full, 64 * ((NQ - 1) * g + q + 1))
                turn_unit(g, q, first_of("Sq"), nat_a[:, 1].rearrange("p b c -> p (b c)"))

            def down_tile(g, q, j):
                c = first_of(f"D{j}")
                dve.wait_ge(nat_down_full, 64 * (8 * g + q + 2))
                rows = nat_down[:].rearrange("p (q m) (f j) -> p m q f j", q=4, j=PT)
                for half in range(2):
                    turn(g, q, c + half, bank_of(c + half).rearrange("p (m q h) -> p m q h", m=4, q=4),
                         rows[:, 4 * half:4 * half + 4, :, :, j])
                for half in range(2):
                    ms = slice(4 * half, 4 * half + 4)
                    piece_low(g, q, c + half, down_w[:, 1, j, ms, :], bank_of(c + half).rearrange("p (m h) -> p m h", m=4),
                              down_w[:, 0, j, ms, :])

            def down_rest(g):
                c = first_of("DREM")
                dve.wait_ge(nat_down_full, 64 * (8 * g + 1))
                rows = nat_down[0:64, :, 0:32].rearrange("p (q m) f -> p m q f", q=4)
                for half in range(2):
                    turn(g, 0, c + half, bank_of(c + half)[0:64].rearrange("p (m q h) -> p m q h", m=4, q=4),
                         rows[:, 4 * half:4 * half + 4])
                for half in range(2):
                    ms = slice(4 * half, 4 * half + 4)
                    piece_low(g, 0, c + half, down_w[0:64, 1, 0, ms, :],
                              bank_of(c + half)[0:64].rearrange("p (m h) -> p m h", m=4), down_w[0:64, 0, 0, ms, :])

            def a_down_rest(g):
                c = first_of("ADREM")
                dve.wait_ge(nat_ad_full, 128 * (8 * g + 1))
                turn(g, 0, c, bank_of(c)[0:64, 0:P].rearrange("p (b a) -> p b a", b=4), nat_ad[0:64, :, 0:32])
                piece_low(g, 0, c, lora_ad[0:64, 1, 0, :], bank_of(c)[0:64, 0:P], lora_ad[0:64, 0, 0, :])

            def a_down_tiles(g, q):
                c = first_of("AD")
                dve.wait_ge(nat_ad_full, 128 * (8 * g + q + 2))
                turn(g, q, c, bank_of(c)[:, 0:PT * P].rearrange("p (j b a) -> p j b a", j=PT, b=4),
                     nat_ad[:].rearrange("p b (f j) -> p j b f", j=PT))
                piece_low(g, q, c, lora_ad[:, 1].rearrange("p j a -> p (j a)"), bank_of(c)[:, 0:PT * P],
                          lora_ad[:, 0].rearrange("p j a -> p (j a)"))

            def lora_b_tiles(g, q, name, part):
                c = first_of(name)
                dve.wait_ge(nat_b_full, 256 * (NQ * g + part + 1))
                rows = nat_b[:].rearrange("p t fq s (j r) -> p j (t fq) r s", j=PT)

                def low(j):
                    doubled_low(g, q, c + j, [lora_b[:, kind, j].rearrange("p t f -> p (t f)") for kind in range(3)],
                                bank_of(c + j)[:, 0:256])

                for j in range(PT):
                    turn(g, q, c + j, bank_of(c + j)[:, 0:256].rearrange("p (n r s) -> p n r s", n=8, r=RANK), rows[:, j])
                    if j > 0:
                        low(j - 1)
                low(PT - 1)

            def lora_b_rest(g):
                c = first_of("BREM")
                dve.wait_ge(nat_b_rem_full, 256 * (g + 1))
                turn(g, 0, c, bank_of(c)[:, 0:P].rearrange("p (n r s) -> p n r s", n=4, r=RANK),
                     nat_b_rem[:].rearrange("p t fq s r -> p (t fq) r s"))
                doubled_low(g, 0, c, [rest_columns(kind) for kind in range(3)],
                            bank_of(c)[:, 0:P].rearrange("p (t f) -> p t f", t=2))

            def cond(g, p):
                dve.wait_ge(mix_hi, 4 * g + p + 1)
                lo(mix[:, p % 2, 2, :], nat_c[:, p, :], mix[:, p % 2, 0, :]).then_inc(mix_lo, 1)

            def mixing(g, e):
                p, kh = e // 2, e % 2
                b0, b1 = S1_BANKS[e % 3]
                src = ps[:, b0:b1, :].rearrange("p a (k n t) -> p (a k) n t", k=2, n=2)[:, :, 0, :]
                at = (slice(4 * kh, 4 * kh + 4), slice(P * p, P * p + P))
                dve.wait_ge(mixed_hi, 8 * g + e + 1)
                lo(mixed[:, 1, at[0], at[1]], src, mixed[:, 0, at[0], at[1]]).then_inc(mixed_lo, 1)

            def x1_total(g, u):
                dve.wait_ge(x1_psum, 8 * g + u + 1)
                dve.wait_ge(xt_copied, 8 * g + 8)
                dve.scalar_tensor_tensor(out=acc[:, u, :], in0=ps[:, X1_BANKS[u], :], scalar=b_col[:, u:u + 1],
                                         in1=acc[:, u, :], op0=ALU.add, op1=ALU.add).then_inc(x1_sum, 1)

            def x1_low(g, u):
                dve.wait_ge(x1_hi, 8 * g + u + 1)
                lo(x1[:, 1, u, :], acc[:, u, :], x1[:, 0, u, :]).then_inc(x1_lo, 1)

            def rank(g, n):
                if n < 2:
                    dve.wait_ge(rank_psum, 2 * g + n + 1)
                    src = ps[:, (2, 0)[n], :]
                else:
                    dve.wait_ge(down_added, DOWNS * g + 9 * NQ + 1)
                    src = acc[:, 8, :]
                dve.wait_ge(rank_lo, START + 3 * g + n)
                dve.wait_ge(act_lo, START + ACTS * g + (ACTS if n == 2 else 0))
                dve.tensor_tensor(act_f[:].rearrange("p (b s) -> p b s", b=GB), src.rearrange("p (b s) -> p b s", b=GB),
                                  own_sb[:].unsqueeze(2).to_broadcast([P, GB, S]), ALU.mult).then_inc(rank_sum, 1)
                dve.wait_ge(rank_hi, 3 * g + n + 1)
                if n < 2:
                    for (rows, tokens), (to, _) in zip(HALVES, HALVES[::-1]):
                        last = lo(lora_t[to, n, 1, tokens], act_f[rows, tokens], lora_t[rows, n, 0, tokens])
                else:
                    last = lo(lora_t[:, 0, 1, :], act_f[:], lora_t[:, 0, 0, :])
                last.then_inc(rank_lo, 1)

            def act_rest(g):
                dve.wait_ge(rest_moved, g + 1)
                dve.tensor_tensor(act_f[0:64, :], gated[0:64, :], act_f[0:64, :], ALU.mult).then_inc(up_read, 1)
                dve.wait_ge(act_hi, ACTS * g + 1)
                lo(acts[0:64, 1, 0, :], act_f[0:64, :], acts[0:64, 0, 0, :]).then_inc(act_lo, 1)

            def act_tile(g, q, j):
                n = ACTS * g + PT * q + j + 1
                dve.wait_ge(up_psum, START + TILES * g + PT * q + j + 1)
                dve.wait_ge(gate_read, n + 1)
                dve.wait_ge(act_lo, START + n)
                dve.tensor_tensor(act_f[:], ps[:, (2 * j + 1) % 3, :], gated[:], ALU.mult).then_inc(up_read, 1)
                dve.wait_ge(act_hi, n + 1)
                lo(acts[:, 1, j, :], act_f[:], acts[:, 0, j, :]).then_inc(act_lo, 1)

            def down_add(g, stage, i):
                n = DOWNS * g + 9 * stage + i + 1
                m = DOWN_ORDER[i]
                dve.wait_ge(down_psum, START + n)
                src = ps[:, D_BANK + i % 3, :]
                if isinstance(stage, int) and stage == 0:
                    dve.wait_ge(x1_lo, 8 * g + KC)
                    dve.wait_ge(rank_lo, START + 3 * g)
                    dve.tensor_copy(acc[:, m, :], src).then_inc(down_added, 1)
                else:
                    dve.wait_ge(down_added, n - 9)
                    dve.tensor_tensor(acc[:, m, :], src, acc[:, m, :], ALU.add).then_inc(down_added, 1)

            def down_low(g, m):
                dve.wait_ge(down_hi, 8 * g + m + 1)
                lo(down(1, m), acc[:, m, :], down(0, m)).then_inc(down_lo, 1)

            def part(g, q, last):
                weight_unit(g, q, "U1", NAT_GU + 3, SPLIT_GU + 3)
                down_tile(g, q, 0)
                act_tile(g, q, 0)
                weight_unit(g, q, "G2", NAT_GU + 4, SPLIT_GU + 4)
                down_tile(g, q, 1)
                weight_unit(g, q, "U2", NAT_GU + 5, SPLIT_GU + 5)
                act_tile(g, q, 1)
                down_tile(g, q, 2)
                a_down_tiles(g, q)
                if last:
                    b_down_unit(g, q, SPLIT_BD)
                    act_tile(g, q, 2)
                    down_add(g, q + 1, 0)
                    rank(g, 2)
                    for i in range(1, 9):
                        down_add(g, q + 1, i)
                        if i == 5:
                            down_low(g, 0)
                    return
                weight_unit(g, q, "nextG0", NAT_GU + 6, SPLIT_GU + 6)
                act_tile(g, q, 2)
                sign_part(g, q)
                lora_b_tiles(g, q, "nextB", q + 1)
                for i in range(3):
                    down_add(g, q + 1, i)
                weight_unit(g, q, "nextU0", NAT_GU + 7, SPLIT_GU + 7)
                for i in range(3, 5):
                    down_add(g, q + 1, i)
                weight_unit(g, q, "nextG1", NAT_GU + 8, SPLIT_GU + 8)
                for i in range(5, 9):
                    down_add(g, q + 1, i)

            def out_tile(g, o, dst):
                dve.wait_ge(out_psum, START + 8 * g + o + 1)
                dve.wait_ge(out_sum, START + 8 * g + o)
                dve.scalar_tensor_tensor(out=gated[:], in0=ps[:, OUT_BANKS[o], :], scalar=bias_col[:, o:o + 1],
                                         in1=x1[:, 0, o, :].bitcast(F32), op0=ALU.add, op1=ALU.add).then_inc(out_read, 1)
                dve.wait_ge(out_read, START + 8 * g + o + 1)
                dve.wait_ge(out_turned, START + 8 * g + o)
                dve.tensor_tensor(act_f[:], gated[:], x1[:, 1, o, :].bitcast(F32), ALU.add).then_inc(out_sum, 1)
                dve.wait_ge(out_sum, START + 8 * g + o + 1)
                dve.transpose(dst, act_f[:].rearrange("p (n t) -> p n t", t=32)).then_inc(out_turned, 1)

            def mixing_ahead(g, meanwhile=lambda: None):
                for p in range(3):
                    plain_unit(g, p, NAT_X + p, SPLIT_X + p)
                    if p == 1:
                        meanwhile()
                    if p < 2:
                        cond(g, p)

            def first_weight_unit(g, u):
                plain_unit(g, 4 + u, NAT_W + u, SPLIT_W + u)

            def mixing_all(g, weights):
                for e in range(8):
                    mixing(g, e)
                    if e == 1:
                        cond(g, 2)
                        plain_unit(g, 3, NAT_X + 3, SPLIT_X + 3)
                    if e == 3:
                        cond(g, 3)
                    if weights and e in (3, 5, 7):
                        first_weight_unit(g, e // 2 - 1)

            def adapter_sum():
                dve.wait_ge(coef_in, 64)
                for i in range(2):
                    dve.tensor_tensor(kept[i], coef[i], coef_mask[i], ALU.mult).then_inc(kept_step, 1)
                for i in range(2):
                    dve.wait_ge(kept_step, i + 1)
                    dve.tensor_tensor(coef[i][:, 0], kept[i][:, 0], kept[i][:, 1], ALU.add).then_inc(kept_step, 1)
                for i in range(2):
                    dve.wait_ge(kept_step, i + 3)
                    dve.tensor_tensor(coef[i][:, 1], coef[i][:, 0], kept[i][:, 2], ALU.add).then_inc(kept_step, 1)
                for i, (r0, r1) in enumerate(((0, R0), (R0, RL))):
                    dve.wait_ge(kept_step, i + 5)
                    dve.tensor_scalar(wsum[:, :, r0:r1], coef[i][:, 1].rearrange("p (c r) -> p c r", c=KC), 0.5, None,
                                      ALU.mult).then_inc(wsum_done, 1)

            def turn_base(u):
                dve.wait_ge(base_in[u % BASE_SLOTS], 64 * (u // BASE_SLOTS + 1))
                dve.transpose(base_t[:, u].rearrange("p (k b h) -> p k b h", k=KC, b=4),
                              base[:, u % BASE_SLOTS].rearrange("p b (k h) -> p k b h", k=KC)).then_inc(base_turned, 1)

            def add_weight(u):
                dve.wait_ge(base_turned, u + 1)
                for half in range(2):
                    part_t = base_t[:, u, 512 * half:512 * half + 512]
                    dve.wait_ge(w_psum, 2 * u + half + 1)
                    dve.tensor_tensor(part_t, ps[:, weight_bank(u, half), :], part_t, ALU.add).then_inc(w_added, 1)

            def effective_weight():
                for u in range(4):
                    turn_base(u)
                dve.wait_ge(enc_in, 32)
                dve.tensor_copy(enc_tiles.rearrange("r k (q d) -> r k q d", q=4),
                                enc.rearrange("r (q k d) -> r k q d", q=4, k=KC)).then_inc(g_read, 1)
                dve.wait_ge(g_psum, 1)
                dve.tensor_copy(low_rank, ps[0:RL, 6:8, :].rearrange("p a n -> p (a n)")).then_inc(g_read, 1)
                for u in range(4):
                    if u == 3:
                        first_weight_unit(0, 0)
                    add_weight(u)
                    turn_base(u + 4)
                for u in (1, 2):
                    first_weight_unit(0, u)

            def first_layer_all(g, making):
                for u in range(KC):
                    x1_total(g, u)
                    if making and u < 4:
                        add_weight(u + 4)
                    if u < 5:
                        first_weight_unit(g, 3 + u)
                        if u == 4:
                            dve.wait_ge(x1_sum, 8 * g + 2)
                            lora_b_tiles(g, 0, "B", 0)
                    elif u == 5:
                        adapter_unit(g, "AG", 0, SPLIT_AG)
                    elif u == 6:
                        adapter_unit(g, "AU", 1, SPLIT_AU)
                    else:
                        weight_unit(g, 0, "REM", NAT_REM, SPLIT_REM)
                    x1_low(g, u)
                lora_b_rest(g)

            def group(g, last):
                rank(g, 0)
                down_rest(g)
                a_down_rest(g)
                rank(g, 1)
                weight_unit(g, 0, "G0", NAT_FIRST[0], SPLIT_GU)
                weight_unit(g, 0, "U0", NAT_FIRST[1], SPLIT_GU + 1)
                act_rest(g)
                for i in range(9):
                    down_add(g, 0, i)
                sign_unit(g, 0)
                sign_unit(g, 1)
                weight_unit(g, 0, "G1", NAT_FIRST[2], SPLIT_GU + 2)
                with dve.Fori(0, NQ - 1) as q:
                    part(g, q, False)
                part(g, NQ - 1, True)
                for m in range(1, KC):
                    down_low(g, m)
                if not last:
                    mixing_ahead(g + 1)
                for half in range(2):
                    dve.wait_ge(out_stored[half], 64 * (START + g))
                    if half:
                        dve.wait_ge(piece_turned, piece_number(g, NQ - 1, first_of("D2") + 2))
                    for o in range(4 * half, 4 * half + 4):
                        out_tile(g, o, out_halves[half][:, :, 32 * (o % 4):32 * (o % 4) + 32])
                if not last:
                    mixing_all(g + 1, True)
                    first_layer_all(g + 1, False)

            dve.memset(nat_c[:], 0.0).then_inc(const_set, 1)
            dve.memset(lora_b_rem[:].bitcast(F32), 0.0).then_inc(const_set, 1)
            dve.wait_ge(ident_in, 16)
            for s in range(2):
                dve.tensor_copy(mix[:, s, 1, :], act_f[:, 0:P]).then_inc(const_set, 1)
            dve.wait_ge(const_set, CONSTS)
            for semaphore in (piece_lo, mix_lo, up_read, out_read, out_sum, out_turned, rank_lo, act_lo):
                dve.sem_inc(semaphore, START)
            mixing_ahead(0, adapter_sum)
            mixing_all(0, False)
            effective_weight()
            dve.wait_ge(const_in, 16 * 9)
            first_layer_all(0, True)
            with dve.Fori(0, NG - 1) as g:
                group(g, False)
            group(NG - 1, True)

        @block.tensor
        def _(pe):
            def product(dst, a, b, first, last):
                pe.matmul(dst, a[0], b[0], start=first, stop=False)
                pe.matmul(dst, a[0], b[1], start=False, stop=False)
                return pe.matmul(dst, a[1], b[0], start=False, stop=last)

            def stationary(m, k):
                return [split[:, m % SPLIT_SLOTS, s, P * k:P * k + P] for s in range(2)]

            def mixing(g, e, before):
                p, kh = e // 2, e % 2
                if kh == 0:
                    pe.wait_ge(plain_lo, 12 * g + p + 1)
                    pe.wait_ge(mix_lo, START + 4 * g + p + 1)
                if e < 3:
                    if before is not None:
                        pe.wait_ge(out_read, START + 8 * before + (2, 6, 8)[e])
                else:
                    pe.wait_ge(mixed_lo, 8 * g + e - 2)
                    pe.wait_ge(xt_copied, 8 * g + e - 2)
                for k in range(4):
                    bank = S1_BANKS[e % 3][0] + k // 2
                    dst = ps[:, bank, 256 * (k % 2):256 * (k % 2) + 256]
                    xs = stationary(SPLIT_X + p, 4 * kh + k)
                    both = mix[:, p % 2, 0:2, :].rearrange("p n t -> p (n t)")
                    pe.matmul(dst, xs[0], both, start=True, stop=False)
                    pe.matmul(dst[:, 0:P], xs[0], mix[:, p % 2, 2, :], start=False, stop=False)
                    mm = pe.matmul(dst, xs[1], both, start=False, stop=True)
                mm.then_inc(mixed_psum, 1)

            def first_layer(g, u, half=None):
                m = SPLIT_W + u
                pe.wait_ge(plain_lo, 12 * g + 4 + u + 1)
                if half == 0:
                    pe.wait_ge(mixed_lo, 8 * g + 4)
                if u >= 5:
                    pe.wait_ge(x1_sum, 8 * g + u - 2)
                t = slice(0, G) if half is None else slice(256 * half, 256 * half + 256)
                for k in range(KC):
                    if half == 1 and k % 4 == 0:
                        pe.wait_ge(mixed_lo, 8 * g + 7 + k // 4)
                        pe.wait_ge(xt_copied, 8 * g + 7 + k // 4)
                    mm = product(ps[:, X1_BANKS[u], t], stationary(m, k), [mixed[:, s, k, t] for s in range(2)],
                                 k == 0, k == KC - 1)
                if half != 0:
                    mm.then_inc(x1_psum, 1)

            def adapter_product(dst, kinds, n, last):
                for kind, (_, tokens) in enumerate(HALVES):
                    pe.matmul(dst[:, tokens], kinds[kind], lora_t[:, n, 1, tokens], start=False, stop=False)
                return pe.matmul(dst, kinds[2], lora_t[:, n, 0, :], start=False, stop=last)

            def wait_unit(g, q, name):
                pe.wait_ge(piece_lo, START + low_number(g, q, first_of(name) + 2))

            def of_x1(dst, m, last, wait=lambda k: None):
                for k in range(KC):
                    wait(k)
                    mm = product(dst, stationary(m, k), [x1[:, s, k, :] for s in range(2)], k == 0, last and k == KC - 1)
                return mm

            def rank(g, n):
                wait_unit(g, 0, ("AG", "AU")[n])
                pe.wait_ge(x1_sum, 8 * g + (6, 7)[n])
                of_x1(ps[:, (2, 0)[n], :], SPLIT_AG + n, True, lambda k: pe.wait_ge(x1_lo, 8 * g + k + 1))\
                    .then_inc(rank_psum, 1)

            def gate_up_rest(g):
                wait_unit(g, 0, "REM")
                pe.wait_ge(x1_sum, 8 * g + 8)
                of_x1(ps[:, 1, :], SPLIT_REM, False)
                pe.wait_ge(piece_lo, START + low_number(g, 0, first_of("BREM") + 1))
                pe.wait_ge(rank_lo, START + 3 * g + 2)
                for t in range(2):
                    mm = adapter_product(ps[:, 1, :], [lora_b_rem[:, kind, t, :] for kind in range(3)], t, t == 1)
                mm.then_inc(rest_psum, 1)

            def down_rest(g):
                pe.wait_ge(piece_lo, START + low_number(g, 0, first_of("ADREM") + 1))
                pe.wait_ge(act_lo, START + ACTS * g + 1)
                for i in range(9):
                    m = DOWN_ORDER[i]
                    if i >= 3:
                        pe.wait_ge(down_added, DOWNS * g + i - 2)
                    w = [(down_w[0:64, s, 0, m, :] if m < KC else lora_ad[0:64, s, 0, :]) for s in range(2)]
                    product(ps[:, D_BANK + i % 3, :], w, [acts[0:64, s, 0, :] for s in range(2)], True, True)\
                        .then_inc(down_psum, 1)

            def gate_up_weight(g, q, k, name, in_part):
                t, j = k % 2, k // 2
                pe.wait_ge(piece_lo, START + low_number(g, in_part, first_of(name) + 2))
                if t == 0:
                    pe.wait_ge(up_read, START + ACTS * g + PT * q + j)
                else:
                    pe.wait_ge(gate_read, ACTS * g + PT * q + j + 1)
                of_x1(ps[:, k % 3, :], SPLIT_GU + k, False)

            def gate_up_adapter(g, q, k):
                t, j = k % 2, k // 2
                if k == 0:
                    pe.wait_ge(piece_lo, START + low_number(g, q - 1, first_of("nextB") + 3))
                adapter_product(ps[:, k % 3, :], [lora_b[:, kind, j, t, :] for kind in range(3)], t, True)\
                    .then_inc(up_psum if t else gate_psum, 1)

            def part_gate_up(g, q):
                gate_up_adapter(g, q, 0)
                for k, name in enumerate(("nextU0", "nextG1", "U1", "G2", "U2"), 1):
                    gate_up_weight(g, q, k, name, q if k > 2 else q - 1)
                    gate_up_adapter(g, q, k)

            def down_part(g, q, last):
                pe.wait_ge(piece_lo, START + low_number(g, q, first_of("AD") + 1))

                def tiles(i, js, stop=True):
                    m = DOWN_ORDER[i]
                    for j in js:
                        w = [(down_w[:, s, j, m, :] if m < KC else lora_ad[:, s, j, :]) for s in range(2)]
                        mm = product(ps[:, D_BANK + i % 3, :], w, [acts[:, s, j, :] for s in range(2)],
                                     j == 0, stop and j == PT - 1)
                    return mm

                def adapter(i):
                    product(ps[:, D_BANK + i % 3, :], stationary(SPLIT_BD, DOWN_ORDER[i]),
                            [lora_t[:, 0, s, :] for s in range(2)], False, True).then_inc(down_psum, 1)

                def bank_read(i):
                    pe.wait_ge(down_added, DOWNS * g + 9 * (q + 1) + i - 2)

                pe.wait_ge(act_lo, START + ACTS * g + PT * q + 3)
                for i in range(3):
                    bank_read(i)
                    tiles(i, (0, 1))
                pe.wait_ge(act_lo, START + ACTS * g + PT * q + 4)
                if not last:
                    for i in range(3):
                        tiles(i, (2,)).then_inc(down_psum, 1)
                    for i in range(3, 9):
                        bank_read(i)
                        tiles(i, range(PT)).then_inc(down_psum, 1)
                    return
                tiles(0, (2,)).then_inc(down_psum, 1)
                for i in (1, 2):
                    tiles(i, (2,), False)
                bank_read(3)
                tiles(3, range(PT), False)
                pe.wait_ge(piece_lo, START + LOW_PIECES * (g + 1))
                pe.wait_ge(rank_lo, START + 3 * g + 3)
                for i in (1, 2, 3):
                    adapter(i)
                for i in range(4, 9):
                    bank_read(i)
                    tiles(i, range(PT), False)
                    adapter(i)

            def sign_product(g, o, m):
                for s in range(2):
                    mm = pe.matmul(ps[:, OUT_BANKS[o], :], signs[:, m, P * o:P * o + P], down(s, m),
                                   start=(m == 0 and s == 0), stop=(m == KC - 1 and s == 1))
                if m == KC - 1:
                    mm.then_inc(out_psum, 1)

            def mixing_all(g, before=None):
                for e in range(8):
                    mixing(g, e, before)
                    if e == 6 and before is not None:
                        first_layer(g, 0, 0)
                if before is not None:
                    first_layer(g, 1, 0)

            low_v = low_rank.rearrange("r (q u o) -> r u q o", q=4, u=KC)

            def weight_tile(u):
                for half in range(2):
                    if 2 * u + half >= 3:
                        pe.wait_ge(w_added, 2 * u + half - 2)
                    for k in range(4):
                        mm = pe.matmul(ps[:, weight_bank(u, half), P * k:P * k + P], enc_tiles[:, 4 * half + k],
                                       low_v[:, u], start=True, stop=True)
                    mm.then_inc(w_psum, 1)

            def effective_weight():
                pe.wait_ge(table_in, 16 * KC)
                pe.wait_ge(wsum_done, 2)
                for half in range(2):
                    for c in range(KC):
                        mm = pe.matmul(ps[0:RL, 6 + half, :], wsum[:, c], table[:, c, 512 * half:512 * half + 512],
                                       start=(c == 0), stop=(c == KC - 1))
                mm.then_inc(g_psum, 1)
                pe.wait_ge(g_read, 2)
                for u in range(4):
                    weight_tile(u)

            def first_layer_all(g, making):
                if making:
                    first_layer(g, 0, 0)
                first_layer(g, 0, 1)
                for u in range(1, KC):
                    if making and u < 5:
                        weight_tile(u + 3)
                    if u == 1:
                        if making:
                            first_layer(g, 1, 0)
                        first_layer(g, 1, 1)
                    else:
                        first_layer(g, u)

            def group(g, last):
                for n in range(2):
                    rank(g, n)
                gate_up_rest(g)
                gate_up_weight(g, 0, 0, "G0", 0)
                down_rest(g)
                with pe.Fori(0, NQ - 1) as q:
                    part_gate_up(g, q)
                    gate_up_weight(g, q + 1, 0, "nextG0", q)
                    down_part(g, q, False)
                part_gate_up(g, NQ - 1)
                down_part(g, NQ - 1, True)
                pe.wait_ge(up_read, START + ACTS * (g + 1))
                pe.wait_ge(piece_hi, PIECES * (g + 1))
                for m in range(KC):
                    pe.wait_ge(down_lo, 8 * g + m + 1)
                    for o in range(4):
                        sign_product(g, o, m)
                for o in range(4, 8):
                    for m in range(KC):
                        sign_product(g, o, m)
                if not last:
                    mixing_all(g + 1, g)
                    first_layer_all(g + 1, False)

            pe.wait_ge(const_set, CONSTS)
            for semaphore in (down_psum, mixed_psum, up_psum, out_psum):
                pe.sem_inc(semaphore, START)
            mixing_all(0)
            effective_weight()
            first_layer_all(0, True)
            with pe.Fori(0, NG - 1) as g:
                group(g, False)
            group(NG - 1, True)


_INS = ["x", "itok_B_0_15", "itok_B_2_6", "L0_cond_weights", "L0_ffn_W_base", "L0_ffn_b_base", "L0_ffn_enc0",
        "L0_ffn_enc1", "L0_ffn_coefs0", "L0_ffn_coefs1", "L0_ffn_mask0", "L0_ffn_mask1", "L1_cond_W_gate",
        "L1_cond_W_up", "L1_cond_W_down", "L1_cond_A_gate", "L1_cond_B_gate", "L1_cond_A_up", "L1_cond_B_up",
        "L1_cond_A_down", "L1_cond_B_down", "L1_ffn_weight", "L1_ffn_bias"]


def shape_constants():
    import numpy as np

    n = np.arange(H)
    table = np.empty((H, H))
    table[0] = 1 / np.sqrt(H)
    for f in range(1, H // 2):
        angle = 2 * np.pi * (f * n % H) / H
        table[2 * f - 1] = np.sqrt(2 / H) * np.cos(angle)
        table[2 * f] = np.sqrt(2 / H) * np.sin(angle)
    table[H - 1] = (1 - 2 * (n % 2)) / np.sqrt(H)
    row = np.arange(P)
    batch = 2 * (row // 32) + row % 2
    own = 0.5 * (batch[:, None] == np.arange(GB)[None, :])
    return {"fourier": table.astype(np.float32), "identity": np.eye(P, dtype=np.float32),
            "own_batch": own.astype(np.float32)}


def kernel(**inputs):
    import numpy as np
    import concourse.bacc as bacc
    from concourse.bass_utils import run_bass_kernel_spmd

    nc = bacc.Bacc("TRN2", target_bir_lowering=False, num_devices=1, dynamic_dma_scratch_size=4096)
    arrays, ap = {}, {}
    for name, a in {**{n: inputs[n] for n in _INS}, **shape_constants()}.items():
        a = np.ascontiguousarray(a)
        if name == "x":
            a = a.reshape(NB * S, H)
        if name.startswith("itok"):
            a = a.reshape(1, NB)
        arrays[name] = a
        ap[name] = nc.dram_tensor(name, a.shape, mybir.dt.from_np(a.dtype), kind="ExternalInput").ap()
    out = nc.dram_tensor("out", (NB * S, H), F32, kind="ExternalOutput").ap()
    scratch = nc.dram_tensor("effective_weight", (KC, P, H), F32, kind="Internal").ap()
    c = {n.removeprefix("L1_cond_"): v for n, v in ap.items() if n.startswith("L1_cond_")}
    build_layers(nc, ap["x"], ap["itok_B_0_15"], ap["itok_B_2_6"], ap["L0_cond_weights"], ap["L0_ffn_W_base"],
                 ap["L0_ffn_b_base"], ap["L0_ffn_enc0"], ap["L0_ffn_enc1"], (ap["L0_ffn_coefs0"], ap["L0_ffn_coefs1"]),
                 (ap["L0_ffn_mask0"], ap["L0_ffn_mask1"]), ap["fourier"], scratch, c["W_gate"], c["W_up"], c["W_down"],
                 c["A_gate"], c["B_gate"], c["A_up"], c["B_up"], c["A_down"], c["B_down"], ap["L1_ffn_weight"],
                 ap["L1_ffn_bias"], ap["identity"], ap["own_batch"], out)
    r = run_bass_kernel_spmd(nc, [arrays], core_ids=[0])
    return np.asarray(r.results[0]["out"]).reshape(NB, S, H)
```
